# Optimizing a Trainium2 kernel written in Bass

```python
import numpy as np
import jax
import jax.numpy as jnp

def _softmax(x, axis=-1):
    return jax.nn.softmax(x, axis=axis)

def _gelu(x):
    return jax.nn.gelu(x, approximate=True)

def _silu(x):
    return jax.nn.silu(x)

def _sigmoid(x):
    return jax.nn.sigmoid(x)

def _layernorm(x, axis=-1, eps=1e-05):
    m = jnp.mean(x, axis=axis, keepdims=True)
    v = jnp.var(x, axis=axis, keepdims=True)
    return (x - m) / jnp.sqrt(v + eps)

def _scatter_add(tgt, idx, src, axis=0):
    return tgt.at[idx].add(src)

def _segment_sum(src, seg, n):
    return jax.ops.segment_sum(src, seg, n)
kernel_name = 'mk_decoder_preln_d1_seqx_r2_2d5325'

def setup_inputs(seed: int=0):
    np.random.seed(seed)
    _w = jnp.asarray

    def _rec_inputs():
        import jax
        import jax.numpy as jnp
        _rk = jax.random.key(seed)
        x = -0.0002928 + 1 * jax.random.normal(jax.random.fold_in(_rk, 1), (4, 2048, 512), jnp.float32)
        _lenS = 2048 - jax.random.randint(jax.random.fold_in(_rk, 7), (4,), 0, max(1, 2048 // 4) + 1, jnp.int32)
        _lenS2 = 128 - jax.random.randint(jax.random.fold_in(_rk, 8), (4,), 0, max(1, 128 // 4) + 1, jnp.int32)
        _ctx_1024P = jax.random.normal(jax.random.fold_in(_rk, 11), (4, 16, 512), jnp.float32)
        _ctx_1024c = jax.random.dirichlet(jax.random.fold_in(_rk, 511), 0.3 * jnp.ones((16,), jnp.float32), (4, 128))
        _ctx_1024t = jnp.einsum('bsk,bkd->bsd', _ctx_1024c, _ctx_1024P)
        _ctx_1024t = _ctx_1024t * jax.lax.rsqrt(jnp.mean(jnp.square(_ctx_1024t)) + 1e-12) * 0.953939
        ctx_1024 = -1.39393e-06 + 0.999914 * (_ctx_1024t + 0.3 * jax.random.normal(jax.random.fold_in(_rk, 611), (4, 128, 512), jnp.float32))
        _validS = jnp.arange(2048)[None, :] < _lenS[:, None]
        _validS2 = jnp.arange(128)[None, :] < _lenS2[:, None]
        _causal = jnp.tril(jnp.ones((2048, 2048), dtype=bool))
        mask_BxS2_bf1 = jnp.ones((4, 128), dtype=bool)
        return (x, ctx_1024, mask_BxS2_bf1)
    x, ctx_1024, mask_BxS2_bf1 = _rec_inputs()

    def _L0_attn_setup():
        import jax, jax.numpy as jnp
        import numpy as np
        T, B, E, H = (512, 8, 512, 16)
        DH = E // H
        MASKED_BIAS = -10000.0
        key = jax.random.key(seed)
        k1, k2, k3 = jax.random.split(key, 3)
        query = jax.random.normal(k1, (T, B, E), dtype=jnp.float32)
        qkv_w = jax.random.normal(k2, (3 * E, E), dtype=jnp.float32) * (1.0 / np.sqrt(2.0 * E))
        out_w = jax.random.normal(k3, (E, E), dtype=jnp.float32) * (1.0 / np.sqrt(E))
        return {'query': query, 'qkv_w': qkv_w, 'qkv_b': jnp.zeros((3 * E,), jnp.float32), 'out_w': out_w, 'out_b': jnp.zeros((E,), jnp.float32)}
    _L0_attn_all = _L0_attn_setup()
    _L0_attn_in = {k: v for k, v in _L0_attn_all.items() if k in ('qkv_w', 'qkv_b', 'out_w', 'out_b')}
    del _L0_attn_all

    def _L0_xattn_setup():
        import jax, jax.numpy as jnp
        import numpy as np
        N_HEADS = 16
        D_MODEL = 512
        HEAD_DIM = D_MODEL // N_HEADS
        MASK_FILL = -100000000.0

        def _split_heads(x):
            B, S, _ = x.shape
            return x.reshape(B, S, N_HEADS, HEAD_DIM).transpose(0, 2, 1, 3)
        key = jax.random.key(seed)
        ks = jax.random.split(key, 12)
        B, L, P = (2, 1024, 1024)
        s = 1.0 / np.sqrt(D_MODEL).astype(np.float32)
        inp = {'q': jax.random.normal(ks[0], (B, L, D_MODEL), dtype=jnp.float32), 'k': jax.random.normal(ks[1], (B, P, D_MODEL), dtype=jnp.float32), 'v': jax.random.normal(ks[2], (B, P, D_MODEL), dtype=jnp.float32), 'attention_mask': jnp.ones((B, P), dtype=bool), 'Wq': jax.random.normal(ks[3], (D_MODEL, D_MODEL), dtype=jnp.float32) * s, 'bq': jnp.zeros((D_MODEL,), dtype=jnp.float32), 'Wk': jax.random.normal(ks[4], (D_MODEL, D_MODEL), dtype=jnp.float32) * s, 'bk': jnp.zeros((D_MODEL,), dtype=jnp.float32), 'Wv': jax.random.normal(ks[5], (D_MODEL, D_MODEL), dtype=jnp.float32) * s, 'bv': jnp.zeros((D_MODEL,), dtype=jnp.float32), 'Wo': jax.random.normal(ks[6], (D_MODEL, D_MODEL), dtype=jnp.float32) * s, 'bo': jnp.zeros((D_MODEL,), dtype=jnp.float32)}
        return inp
    _L0_xattn_all = _L0_xattn_setup()
    _L0_xattn_in = {k: v for k, v in _L0_xattn_all.items() if k in ('Wq', 'bq', 'Wk', 'bk', 'Wv', 'bv', 'Wo', 'bo')}
    del _L0_xattn_all

    def _L0_ffn_setup():
        import jax, jax.numpy as jnp
        import numpy as np
        D_MODEL = 512
        M = 64
        INNER = 16
        key = jax.random.key(seed)
        ks = jax.random.split(key, 9)

        def init(k, shape, fan_in):
            bound = 1.0 / np.sqrt(fan_in)
            return jax.random.uniform(k, shape, jnp.float32, -bound, bound)
        x = jax.random.normal(ks[0], (16, 2048, D_MODEL), dtype=jnp.float32)
        Win = init(ks[1], (D_MODEL, M), D_MODEL)
        bin_ = init(ks[2], (M,), D_MODEL)
        W1 = init(ks[3], (M, INNER), 1)
        b1 = init(ks[4], (M, INNER), 1)
        W2 = init(ks[5], (M, INNER), INNER)
        b2 = init(ks[6], (M,), INNER)
        Wout = init(ks[7], (M, D_MODEL), M)
        bout = init(ks[8], (D_MODEL,), M)
        return {'x': x, 'Win': Win, 'bin_': bin_, 'W1': W1, 'b1': b1, 'W2': W2, 'b2': b2, 'Wout': Wout, 'bout': bout}
    _L0_ffn_all = _L0_ffn_setup()
    _L0_ffn_in = {k: v for k, v in _L0_ffn_all.items() if k in ('Win', 'bin_', 'W1', 'b1', 'W2', 'b2', 'Wout', 'bout')}
    del _L0_ffn_all
    return {'x': x, 'ctx_1024': ctx_1024, 'mask_BxS2_bf1': mask_BxS2_bf1, 'L0_attn_qkv_w': _L0_attn_in['qkv_w'], 'L0_attn_qkv_b': _L0_attn_in['qkv_b'], 'L0_attn_out_w': _L0_attn_in['out_w'], 'L0_attn_out_b': _L0_attn_in['out_b'], 'L0_xattn_Wq': _L0_xattn_in['Wq'], 'L0_xattn_bq': _L0_xattn_in['bq'], 'L0_xattn_Wk': _L0_xattn_in['Wk'], 'L0_xattn_bk': _L0_xattn_in['bk'], 'L0_xattn_Wv': _L0_xattn_in['Wv'], 'L0_xattn_bv': _L0_xattn_in['bv'], 'L0_xattn_Wo': _L0_xattn_in['Wo'], 'L0_xattn_bo': _L0_xattn_in['bo'], 'L0_ffn_Win': _L0_ffn_in['Win'], 'L0_ffn_bin_': _L0_ffn_in['bin_'], 'L0_ffn_W1': _L0_ffn_in['W1'], 'L0_ffn_b1': _L0_ffn_in['b1'], 'L0_ffn_W2': _L0_ffn_in['W2'], 'L0_ffn_b2': _L0_ffn_in['b2'], 'L0_ffn_Wout': _L0_ffn_in['Wout'], 'L0_ffn_bout': _L0_ffn_in['bout']}

def reference(x, ctx_1024, mask_BxS2_bf1, L0_attn_qkv_w, L0_attn_qkv_b, L0_attn_out_w, L0_attn_out_b, L0_xattn_Wq, L0_xattn_bq, L0_xattn_Wk, L0_xattn_bk, L0_xattn_Wv, L0_xattn_bv, L0_xattn_Wo, L0_xattn_bo, L0_ffn_Win, L0_ffn_bin_, L0_ffn_W1, L0_ffn_b1, L0_ffn_W2, L0_ffn_b2, L0_ffn_Wout, L0_ffn_bout):
    import jax
    import jax.numpy as jnp

    def _L0_attn_ref(query, qkv_w, qkv_b, out_w, out_b):
        import jax, jax.numpy as jnp
        import numpy as np
        T, B, E, H = (512, 8, 512, 16)
        DH = E // H
        MASKED_BIAS = -10000.0
        tgt_len, bsz, embed_dim = query.shape
        scaling = DH ** (-0.5)
        qkv = jnp.einsum('tbe,fe->tbf', query, qkv_w) + qkv_b
        q, k, v = jnp.split(qkv, 3, axis=-1)
        q = q * scaling

        def to_heads(x):
            return x.reshape(tgt_len, bsz * H, DH).transpose(1, 0, 2)
        q, k, v = (to_heads(q), to_heads(k), to_heads(v))
        attn_weights = jnp.einsum('ntd,nsd->nts', q, k)
        causal = jnp.tril(jnp.ones((tgt_len, tgt_len), dtype=bool))
        attn_weights = jnp.where(causal[None, :, :], attn_weights, jnp.asarray(MASKED_BIAS, attn_weights.dtype))
        attn_probs = jax.nn.softmax(attn_weights, axis=-1)
        attn = jnp.einsum('nts,nsd->ntd', attn_probs, v)
        attn = attn.transpose(1, 0, 2).reshape(tgt_len, bsz, embed_dim)
        out = jnp.einsum('tbe,fe->tbf', attn, out_w) + out_b
        return out

    def _L0_xattn_ref(q, k, v, attention_mask, Wq, bq, Wk, bk, Wv, bv, Wo, bo):
        import jax, jax.numpy as jnp
        import numpy as np
        N_HEADS = 16
        D_MODEL = 512
        HEAD_DIM = D_MODEL // N_HEADS
        MASK_FILL = -100000000.0

        def _split_heads(x):
            B, S, _ = x.shape
            return x.reshape(B, S, N_HEADS, HEAD_DIM).transpose(0, 2, 1, 3)
        qm = _split_heads(q @ Wq.T + bq)
        km = _split_heads(k @ Wk.T + bk)
        vm = _split_heads(v @ Wv.T + bv)
        scores = jnp.einsum('bnlh,bnph->bnlp', qm, km) / np.sqrt(HEAD_DIM).astype(np.float32)
        mask = attention_mask[:, None, None, :]
        scores = jnp.where(mask, scores, MASK_FILL)
        attn = jax.nn.softmax(scores, axis=-1)
        out = jnp.einsum('bnlp,bnph->bnlh', attn, vm)
        B, _, L, _ = out.shape
        out = out.transpose(0, 2, 1, 3).reshape(B, L, D_MODEL)
        return out @ Wo.T + bo

    def _L0_ffn_ref(x, Win, bin_, W1, b1, W2, b2, Wout, bout):
        import jax, jax.numpy as jnp
        import numpy as np
        D_MODEL = 512
        M = 64
        INNER = 16
        s = jnp.einsum('btd,dm->btm', x, Win) + bin_
        h = jax.nn.relu(s[..., None] * W1 + b1)
        g = jnp.einsum('btmh,mh->btm', h, W2) + b2
        out = jnp.einsum('btm,md->btd', g, Wout) + bout
        return out
    x = x + _L0_attn_ref(_layernorm(x, axis=-1), L0_attn_qkv_w, L0_attn_qkv_b, L0_attn_out_w, L0_attn_out_b)
    x = x + _L0_xattn_ref(_layernorm(x, axis=-1), ctx_1024, ctx_1024, mask_BxS2_bf1, L0_xattn_Wq, L0_xattn_bq, L0_xattn_Wk, L0_xattn_bk, L0_xattn_Wv, L0_xattn_bv, L0_xattn_Wo, L0_xattn_bo)
    x = x + _L0_ffn_ref(_layernorm(x, axis=-1), L0_ffn_Win, L0_ffn_bin_, L0_ffn_W1, L0_ffn_b1, L0_ffn_W2, L0_ffn_b2, L0_ffn_Wout, L0_ffn_bout)
    return x

_drawn_inputs = setup_inputs


def setup_inputs(seed=0):
    import zlib

    import numpy as np

    out = dict(_drawn_inputs(seed))
    spreads = {'L0_attn_qkv_b': (0.0, 0.1),
     'L0_attn_out_b': (0.0, 0.1),
     'L0_xattn_bq': (0.0, 0.461),
     'L0_xattn_bk': (0.0, 2.0),
     'L0_xattn_bv': (0.0, 0.1),
     'L0_xattn_bo': (0.0, 0.1)}
    factors = {'L0_ffn_bin_': 25.64}
    for name, (base, spread) in spreads.items():
        noise = np.random.default_rng([zlib.crc32(name.encode()), seed]).standard_normal(out[name].shape)
        drawn = base * np.exp(spread * noise) if base else spread * noise
        out[name] = jnp.asarray(drawn.astype(out[name].dtype))
    for name, factor in factors.items():
        out[name] = (out[name] * factor).astype(out[name].dtype)
    return out
```

```python
from contextlib import ExitStack

import numpy as np

import concourse.bass as bass
from concourse import mybir

F32 = mybir.dt.float32
F32R = mybir.dt.float32r
F16 = mybir.dt.float16
U8 = mybir.dt.uint8
ALU = mybir.AluOpType
ACT = mybir.ActivationFunctionType
AX = mybir.AxisListType

P = 128
D = 512
DK = D // P
R = 4
S = 2048
H = 16
DH = D // H
C = 128
TILES = S // P
SCALE = DH ** -0.5
EPS = 1e-5
CAUSAL_FILL = -10000.0
MASK_FILL = -100000000.0
MASK_FILL_HI = -99975168.0
MASK_FILL_LO = MASK_FILL - MASK_FILL_HI
M = 64
INNER = 16
PAIRS = INNER // 2
PASSES = ((0, 0), (0, 1), (1, 0))


def wait(eng, sem, count):
    if isinstance(count, int) and count <= 0:
        return
    eng.wait_ge(sem, count)


def wait_each(eng, *pairs):
    pairs = [(sem, count if isinstance(count, int) else eng.snap(count)) for sem, count in pairs]
    for sem, count in pairs:
        wait(eng, sem, count)


def bcast(ap, n):
    return ap.rearrange("p (a b) -> p a b", b=1).to_broadcast([ap.shape[0], ap.shape[1], n])


def run_steps(eng, step, last):
    for j in (-1, 0, 1, 2):
        step(j, j % 2)
    with eng.Fori(0, (TILES - 4) // 2) as i:
        step(2 * i + 3, 1)
        step(2 * i + 4, 0)
    for j in range(TILES - 1, last + 1):
        step(j, j % 2)


def has(j, shift=0):
    return not isinstance(j, int) or 0 <= j + shift < TILES


def prepare_block(nc, ctx_in, mask_in, w_in, b_in, scratch, keep):
    with ExitStack() as stack:
        def sb(name, shape, dt=F32):
            return stack.enter_context(nc.sbuf_tensor(name, shape, dt))

        def sem(name):
            return stack.enter_context(nc.semaphore(name))

        ctx = sb("ctx", [P, R, D])
        raw = [sb(f"raw{i}", [P, DK, D]) for i in range(2)]
        wkv = [[sb(f"wkv{i}_{h}", [P, DK, D], F32R) for h in range(2)] for i in range(2)]
        ctxT = [sb(f"ctxT{h}", [P, DK, R * C], F32R) for h in range(2)]
        kvT = sb("kvT", [P, DK, R * C])
        khi = sb("khi", [P, DK, R * C], F32R)
        klo = sb("klo", [P, DK, R * C], F32R)
        vhi = sb("vhi", [P, R, D], F16)
        vlo = sb("vlo", [P, R, D], F16)
        mask8 = sb("mask8", [P, R * C], U8)
        mask = sb("mask", [P, R * C])
        bkv = sb("bkv", [P, 2, DK])
        rvs = sb("rvs", [P, DK])
        fill = sb("fill", [P, 1])
        maskfill = sb("maskfill", [P, R * C], F32R)
        ps = [stack.enter_context(nc.psum_tensor(f"pp{i}", [P, 512], F32)) for i in range(4)]

        in_ctx, in_mask, in_bkv, in_bias = sem("in_ctx"), sem("in_mask"), sem("in_bkv"), sem("in_bias")
        in_raw = [sem("in_raw0"), sem("in_raw1")]
        zeroed, ident_ready = sem("zeroed"), sem("ident_ready")
        w_hi, w_lo = sem("w_hi"), sem("w_lo")
        trans, t_hi, t_lo = sem("trans"), sem("t_hi"), sem("t_lo")
        kvt_done, kvt_sb = sem("kvt_done"), sem("kvt_sb")
        k_masked, k_hi, k_lo = sem("k_masked"), sem("k_hi"), sem("k_lo")
        bk_scaled, mask_f, mask_inv, fill_ready, mask_rows = (
            sem("bk_scaled"), sem("mask_f"), sem("mask_inv"), sem("fill_ready"), sem("mask_rows"))
        v_max, v_rcp, v_unit = sem("v_max"), sem("v_rcp"), sem("v_unit")
        v_trans, v_h, v_l = sem("v_trans"), sem("v_h"), sem("v_l")
        kv_out, bias_ready = sem("kv_out"), sem("bias_ready")

        ident, wqkv, wout = keep["ident"], keep["wqkv"], keep["wout"]
        bqkv, bout, vscale = keep["bqkv"], keep["bout"], keep["vscale"]
        k_dram, v_dram = scratch["k"], scratch["v"]

        pieces = ([(w_in["wk"], wkv[0][0][:, :, :], wkv[0][1][:, :, :]),
                   (w_in["wv"], wkv[1][0][:, :, :], wkv[1][1][:, :, :])]
                  + [(w_in["wqkv"][:, c * D:(c + 1) * D], wqkv[0][:, :, c * D:(c + 1) * D],
                      wqkv[1][:, :, c * D:(c + 1) * D]) for c in range(3)]
                  + [(w_in["wout"], wout[0][:, :, :], wout[1][:, :, :])])

        block = stack.enter_context(nc.Block())

        @block.sync
        def _(sp):
            sp.dma_start(ctx[:, :, :], ctx_in.rearrange("b c d -> c b d")).then_inc(in_ctx, 16)
            for n, (src, _, _) in enumerate(pieces):
                wait(sp, w_lo, n - 1)
                sp.dma_start(raw[n % 2][:, :, :], src.rearrange("(k p) n -> p k n", p=P)).then_inc(in_raw[n % 2], 16)
            sp.wait_ge(k_lo, DK)
            for r in range(R):
                cols = slice(r * C, (r + 1) * C)
                sp.dma_start(k_dram[r, :, 0, :, :], khi[:, :, cols].bitcast(F32)).then_inc(kv_out, 16)
                sp.dma_start(k_dram[r, :, 1, :, :], klo[:, :, cols].bitcast(F32)).then_inc(kv_out, 16)
            sp.wait_ge(v_h, R)
            sp.wait_ge(v_l, R)
            sp.wait_ge(mask_rows, 1)
            for r in range(R):
                sp.dma_start(scratch["mask"][r, :, :], maskfill[:, r * C:(r + 1) * C].bitcast(F32)).then_inc(kv_out, 16)
                sp.dma_start(v_dram[r, :, 0, :], vhi[:, r, :]).then_inc(kv_out, 16)
                sp.dma_start(v_dram[r, :, 1, :], vlo[:, r, :]).then_inc(kv_out, 16)
            sp.wait_ge(kv_out, 16 * 5 * R)

        @block.gpsimd
        def _(pool):
            nc.gpsimd.memset(ident[:, :], 0.0).then_inc(zeroed, 1)
            pool.wait_ge(zeroed, 1)
            nc.gpsimd.affine_select(out=ident[:, :], in_=ident[:, :], compare_op=ALU.not_equal, fill=1.0,
                                    base=0, pattern=[[-1, P]], channel_multiplier=1).then_inc(ident_ready, 1)

        @block.tensor
        def _(pe):
            pe.wait_ge(ident_ready, 1)
            pe.wait_ge(in_ctx, 16)
            for k in range(DK):
                for r in range(R):
                    last = nc.tensor.transpose(ps[k][:, r * C:(r + 1) * C], ctx[:, r, k * P:(k + 1) * P], ident[:, :])
                last.then_inc(trans, 1)
            pe.wait_ge(t_lo, DK)
            for i in range(2):
                pe.wait_ge(w_lo, i + 1)
                for m in range(DK):
                    wait(pe, kvt_sb, DK * (i - 1) + m + 1)
                    n = 0
                    for k in range(DK):
                        for a, b in PASSES:
                            last = nc.tensor.matmul(ps[m][:, :], wkv[i][a][:, k, m * P:(m + 1) * P],
                                                    ctxT[b][:, k, :], start=(n == 0), stop=(n == 11))
                            n += 1
                    last.then_inc(kvt_done, 1)
            pe.wait_ge(v_unit, 1)
            for r in range(R):
                for m in range(DK):
                    last = nc.tensor.transpose(ps[r][:, m * P:(m + 1) * P], kvT[:, m, r * C:(r + 1) * C], ident[:, :])
                last.then_inc(v_trans, 1)

        @block.scalar
        def _(act):
            act.dma_start(mask8[:, :], mask_in.rearrange("b c -> (b c)").rearrange("(o n) -> o n", o=1).to_broadcast([P, R * C])
                          ).then_inc(in_mask, 16)
            for i, name in enumerate(("bk", "bv")):
                act.dma_start(bkv[:, i, :], b_in[name]).then_inc(in_bkv, 16)
            act.dma_start(bqkv[:, :], b_in["bqkv"].rearrange("(o n) -> o n", o=1).to_broadcast([P, 3 * D])
                          ).then_inc(in_bias, 16)
            act.dma_start(bout[:, :], b_in["bout"].rearrange("(o n) -> o n", o=1).to_broadcast([P, D])
                          ).then_inc(in_bias, 16)
            for n in range(2):
                act.wait_ge(in_raw[n % 2], 16 * (n // 2 + 1))
                nc.scalar.activation(pieces[n][1], raw[n % 2][:, :, :], ACT.Copy).then_inc(w_hi, 1)
            for k in range(DK):
                act.wait_ge(trans, k + 1)
                nc.scalar.activation(ctxT[0][:, k, :], ps[k][:, :], ACT.Copy).then_inc(t_hi, 1)
            act.wait_ge(bk_scaled, 1)
            for m in range(DK):
                act.wait_ge(kvt_done, m + 1)
                nc.scalar.activation(kvT[:, m, :], ps[m][:, :], ACT.Identity, bias=bkv[:, 0, m:m + 1],
                                     scale=SCALE).then_inc(kvt_sb, 1)
            for m in range(DK):
                act.wait_ge(kvt_done, DK + m + 1)
                act.wait_ge(k_lo, m + 1)
                nc.scalar.activation(kvT[:, m, :], ps[m][:, :], ACT.Identity, bias=bkv[:, 1, m:m + 1]
                                     ).then_inc(kvt_sb, 1)
            for n in range(2, len(pieces)):
                act.wait_ge(in_raw[n % 2], 16 * (n // 2 + 1))
                nc.scalar.activation(pieces[n][1], raw[n % 2][:, :, :], ACT.Copy).then_inc(w_hi, 1)
            for r in range(R):
                act.wait_ge(v_trans, r + 1)
                nc.scalar.activation(vhi[:, r, :], ps[r][:, :], ACT.Copy).then_inc(v_h, 1)

        @block.vector
        def _(dve):
            def split_lo(n):
                dve.wait_ge(w_hi, n + 1)
                nc.vector.tensor_tensor(pieces[n][2], raw[n % 2][:, :, :], pieces[n][1].bitcast(F32),
                                        ALU.subtract).then_inc(w_lo, 1)

            nc.vector.memset(fill[:, :], 0.0).then_inc(fill_ready, 1)
            dve.wait_ge(fill_ready, 1)
            nc.vector.memset(fill[0:2, :], MASK_FILL_LO).then_inc(fill_ready, 1)
            dve.wait_ge(fill_ready, 2)
            nc.vector.memset(fill[0:1, :], MASK_FILL_HI).then_inc(fill_ready, 1)
            dve.wait_ge(in_mask, 16)
            nc.vector.tensor_copy(mask[:, :], mask8[:, :]).then_inc(mask_f, 1)
            dve.wait_ge(in_bkv, 32)
            nc.vector.tensor_scalar(bkv[:, 0, :], bkv[:, 0, :], SCALE, None, ALU.mult).then_inc(bk_scaled, 1)
            split_lo(0)
            split_lo(1)
            for k in range(DK):
                dve.wait_ge(t_hi, k + 1)
                nc.vector.tensor_tensor(ctxT[1][:, k, :], ps[k][:, :], ctxT[0][:, k, :].bitcast(F32),
                                        ALU.subtract).then_inc(t_lo, 1)
            dve.wait_ge(mask_f, 1)
            for m in range(DK):
                dve.wait_ge(kvt_sb, m + 1)
                nc.vector.tensor_tensor(kvT[:, m, :], kvT[:, m, :], mask[:, :], ALU.mult).then_inc(k_masked, 1)
                dve.wait_ge(k_masked, m + 1)
                nc.vector.tensor_copy(khi[:, m, :], kvT[:, m, :]).then_inc(k_hi, 1)
                dve.wait_ge(k_hi, m + 1)
                nc.vector.tensor_tensor(klo[:, m, :], kvT[:, m, :], khi[:, m, :].bitcast(F32),
                                        ALU.subtract).then_inc(k_lo, 1)
            nc.vector.tensor_scalar(mask[:, :], mask[:, :], -1.0, 1.0, ALU.mult, ALU.add).then_inc(mask_inv, 1)
            dve.wait_ge(mask_inv, 1)
            dve.wait_ge(fill_ready, 3)
            nc.vector.tensor_scalar(maskfill[:, :], mask[:, :], fill[:, 0:1], None, ALU.mult).then_inc(mask_rows, 1)
            for m in range(DK):
                dve.wait_ge(kvt_sb, DK + m + 1)
                nc.vector.tensor_reduce(vscale[:, m:m + 1], kvT[:, m, :], AX.X, ALU.max,
                                        apply_absolute_value=True).then_inc(v_max, 1)
            dve.wait_ge(v_max, DK)
            nc.vector.tensor_scalar(vscale[:, :], vscale[:, :], 1e-30, None, ALU.max).then_inc(v_max, 1)
            dve.wait_ge(v_max, DK + 1)
            nc.vector.reciprocal(rvs[:, :], vscale[:, :]).then_inc(v_rcp, 1)
            dve.wait_ge(v_rcp, 1)
            for m in range(DK):
                last = nc.vector.tensor_scalar(kvT[:, m, :], kvT[:, m, :], rvs[:, m:m + 1], None, ALU.mult)
            last.then_inc(v_unit, 1)
            for n in range(2, len(pieces)):
                split_lo(n)
            for r in range(R):
                dve.wait_ge(v_h, r + 1)
                nc.vector.tensor_tensor(vlo[:, r, :], ps[r][:, :], vhi[:, r, :], ALU.subtract).then_inc(v_l, 1)
            dve.wait_ge(in_bias, 32)
            nc.vector.tensor_scalar(bqkv[:, 0:D], bqkv[:, 0:D], SCALE, None, ALU.mult).then_inc(bias_ready, 1)


def self_block(nc, x_in, x1_dram, keep):
    with ExitStack() as stack:
        def sb(name, shape, dt=F32):
            return stack.enter_context(nc.sbuf_tensor(name, shape, dt))

        def sem(name):
            return stack.enter_context(nc.semaphore(name))

        ident, wqkv, wout, bqkv, bout = keep["ident"], keep["wqkv"], keep["wout"], keep["bqkv"], keep["bout"]
        x = sb("x", [P, R, D])
        xres = [sb(f"xres{p}", [P, R, D]) for p in range(2)]
        xn = sb("xn", [P, R, D])
        xT = [sb(f"xT{h}", [P, DK, R * P], F32R) for h in range(2)]
        qkv = [sb(f"qkv{p}", [P, 3, R, D]) for p in range(2)]
        prod = sb("prod", [P, R, D])
        prod_pool = sb("prod_pool", [P, 2, D])
        attn = sb("attn", [P, R, D])
        aT = [[sb(f"aT{b}_{h}", [P, DK, P], F32R) for h in range(2)] for b in range(2)]
        logit = sb("logit", [P, R, R, H])
        prob = sb("prob", [P, R, R, H])
        top = sb("top", [P, R, H])
        total = sb("total", [P, R, H])
        stats = sb("stats", [P, R, 6])
        mv = sb("mv", [P, R, 2])
        vare = sb("vare", [P, R])
        rstd = sb("rstd", [P, R])
        nmr = sb("nmr", [P, R])
        half = sb("half", [P, R])

        tb = [stack.enter_context(nc.psum_tensor(f"tb{i}", [P, 512], F32)) for i in range(2)]
        qb = [stack.enter_context(nc.psum_tensor(f"qb{i}", [P, 512], F32)) for i in range(4)]
        ob = [stack.enter_context(nc.psum_tensor(f"ob{i}", [P, 512], F32)) for i in range(2)]

        x_in_sem = sem("x_in")
        x1_out = [sem(f"x1_out{p}") for p in range(2)]
        consts, half_set = sem("consts"), sem("half_set")
        bn_done, mv_done, var_done, rstd_done, nmr_done, xn_done = (
            sem("bn_done"), sem("mv_done"), sem("var_done"), sem("rstd_done"), sem("nmr_done"), sem("xn_done"))
        res_done = sem("res_done")
        xt_psum, xt_hi, xt_lo = sem("xt_psum"), sem("xt_hi"), sem("xt_lo")
        qkv_psum, qkv_sb = sem("qkv_psum"), sem("qkv_sb")
        qk_mul, qk_sum, top_done, sub_done, exp_done, tot_done, rcp_done, prob_done = (
            sem("qk_mul"), sem("qk_sum"), sem("top_done"), sem("sub_done"), sem("exp_done"), sem("tot_done"),
            sem("rcp_done"), sem("prob_done"))
        pv_mul, pv_half, attn_dve = sem("pv_mul"), sem("pv_half"), sem("attn_dve")
        pool_step, attn_pool = sem("pool_step"), sem("attn_pool")
        at_psum, at_hi, at_lo = sem("at_psum"), sem("at_hi"), sem("at_lo")
        out_psum, x1_done = sem("out_psum"), sem("x1_done")

        N_QKV = 3 * R
        block = stack.enter_context(nc.Block())

        @block.sync
        def _(sp):
            def rows(j):
                return bass.ds(j * P, P) if isinstance(j, int) else bass.ds(sp.snap(j * P), P)

            def step(j, p):
                if has(j, 1):
                    at = rows(j + 1)
                    wait_each(sp, (xn_done, R * (j + 1)), (res_done, j + 1))
                    sp.dma_start(x[:, :, :], x_in[:, at, :].rearrange("t p d -> p t d")).then_inc(x_in_sem, 16)
                if has(j, -1):
                    at = rows(j - 1)
                    wait(sp, x1_done, R * j)
                    sp.dma_start(x1_dram[:, at, :].rearrange("t p d -> p t d"),
                                 xres[1 - p][:, :, :]).then_inc(x1_out[1 - p], 16)

            run_steps(sp, step, TILES)
            for p in range(2):
                sp.wait_ge(x1_out[p], 16 * (TILES // 2))

        @block.gpsimd
        def _(pool):

            def step(j, p):
                if has(j, -1):
                    a = j - 1
                    wait(pool, prob_done, a + 1)
                    wait(pool, qkv_sb, N_QKV * (a + 1))
                    v = qkv[1 - p][:, 2, :, :]
                    for t in (2, 3):
                        base = 8 * a + 4 * (t - 2)
                        wait(pool, at_psum, R * (a - 1) + t + 1)
                        for s in (0, 2):
                            wait(pool, pool_step, base + s)
                            nc.gpsimd.tensor_tensor(
                                prod_pool[:, :, :].rearrange("p s (h d) -> p (s h) d", d=DH),
                                v[:, s:s + 2, :].rearrange("p s (h d) -> p (s h) d", d=DH),
                                bcast(prob[:, t, s:s + 2, :].rearrange("p s h -> p (s h)"), DH),
                                ALU.mult).then_inc(pool_step, 1)
                            pool.wait_ge(pool_step, base + s + 1)
                            if s == 0:
                                nc.gpsimd.tensor_tensor(attn[:, t, :], prod_pool[:, 0, :], prod_pool[:, 1, :],
                                                        ALU.add).then_inc(pool_step, 1)
                            else:
                                nc.gpsimd.tensor_tensor(prod_pool[:, 0, :], prod_pool[:, 0, :],
                                                        prod_pool[:, 1, :], ALU.add).then_inc(pool_step, 1)
                        pool.wait_ge(pool_step, base + 4)
                        nc.gpsimd.tensor_tensor(attn[:, t, :], attn[:, t, :], prod_pool[:, 0, :],
                                                ALU.add).then_inc(attn_pool, 1)
                        pool.wait_ge(attn_pool, 2 * a + t - 1)
                if has(j, 1):
                    wait(pool, var_done, j + 2)
                    wait(pool, xn_done, R * (j + 1))
                    nc.gpsimd.tensor_tensor(rstd[:, :], vare[:, :], half[:, :], ALU.pow).then_inc(rstd_done, 1)
                    if isinstance(j, int):
                        wait(pool, x1_out[1 - p], 16 * ((j + 1) // 2))
                    else:
                        wait(pool, x1_out[1 - p], 8 * (j + 1 - (1 - p)))
                    wait(pool, x_in_sem, 16 * (j + 2))
                    for t in range(R):
                        last = nc.gpsimd.tensor_tensor(xres[1 - p][:, t, :], x[:, t, :], bout[:, :], ALU.add)
                    last.then_inc(res_done, 1)

            nc.gpsimd.memset(half[:, :], -0.5).then_inc(half_set, 1)
            pool.wait_ge(half_set, 1)
            run_steps(pool, step, TILES)

        @block.tensor
        def _(pe):
            def step(j, p):
                if has(j):
                    wait(pe, xn_done, R * (j + 1))
                    for k in range(DK):
                        if k >= 2:
                            wait(pe, xt_lo, DK * j + k - 1)
                        else:
                            wait(pe, at_lo, R * (j - 2) + k + 3)
                        for t in range(R):
                            last = nc.tensor.transpose(tb[k % 2][:, t * P:(t + 1) * P],
                                                       xn[:, t, k * P:(k + 1) * P], ident[:, :])
                        last.then_inc(xt_psum, 1)
                    wait(pe, xt_lo, DK * (j + 1))
                    for g in range(N_QKV):
                        t, c = g // 3, g % 3
                        wait(pe, qkv_sb, N_QKV * j + g - 3)
                        n = 0
                        for k in range(DK):
                            for a, b in PASSES:
                                last = nc.tensor.matmul(qb[g % 4][:, :], xT[a][:, k, t * P:(t + 1) * P],
                                                        wqkv[b][:, k, c * D:(c + 1) * D],
                                                        start=(n == 0), stop=(n == 11))
                                n += 1
                        last.then_inc(qkv_psum, 1)
                if has(j, -1):
                    a_ = j - 1
                    for t in range(R):
                        if t < 2:
                            wait(pe, attn_dve, 2 * a_ + t + 1)
                            if has(j):
                                wait(pe, xt_lo, DK * j + t + 3)
                            else:
                                wait(pe, at_lo, R * (a_ - 1) + t + 3)
                        else:
                            wait(pe, attn_pool, 2 * a_ + t - 1)
                            wait(pe, at_lo, R * a_ + t - 1)
                        for k in range(DK):
                            last = nc.tensor.transpose(tb[t % 2][:, k * P:(k + 1) * P],
                                                       attn[:, t, k * P:(k + 1) * P], ident[:, :])
                        last.then_inc(at_psum, 1)
                    for t in range(R):
                        wait(pe, at_lo, R * a_ + t + 1)
                        wait(pe, x1_done, R * a_ + t - 1)
                        n = 0
                        for k in range(DK):
                            for a, b in PASSES:
                                last = nc.tensor.matmul(ob[t % 2][:, :], aT[t % 2][a][:, k, :],
                                                        wout[b][:, k, :], start=(n == 0), stop=(n == 11))
                                n += 1
                        last.then_inc(out_psum, 1)

            run_steps(pe, step, TILES)

        @block.scalar
        def _(act):
            def step(j, p):
                if has(j):
                    for k in range(DK):
                        if k == 0:
                            wait(act, qkv_psum, N_QKV * j)
                        wait(act, xt_psum, DK * j + k + 1)
                        nc.scalar.activation(xT[0][:, k, :], tb[k % 2][:, :], ACT.Copy).then_inc(xt_hi, 1)
                if has(j, -1):
                    a = j - 1
                    wait(act, sub_done, a + 1)
                    nc.scalar.activation(prob[:, :, :, :], prob[:, :, :, :], ACT.Exp).then_inc(exp_done, 1)
                    for t in range(R):
                        wait(act, at_psum, R * a + t + 1)
                        wait(act, out_psum, R * a + t - 1)
                        nc.scalar.activation(aT[t % 2][0][:, :, :].rearrange("p k n -> p (k n)"),
                                             tb[t % 2][:, :], ACT.Copy).then_inc(at_hi, 1)
                if has(j, 1):
                    wait(act, nmr_done, j + 2)
                    wait(act, rstd_done, j + 2)
                    wait(act, x_in_sem, 16 * (j + 2))
                    wait(act, xt_psum, DK * (j + 1))
                    for t in range(R):
                        nc.scalar.activation(xn[:, t, :], x[:, t, :], ACT.Identity, bias=nmr[:, t:t + 1],
                                             scale=rstd[:, t:t + 1]).then_inc(xn_done, 1)

            run_steps(act, step, TILES)

        @block.vector
        def _(dve):
            nc.vector.memset(logit[:, :, :, :], CAUSAL_FILL).then_inc(consts, 1)
            dve.wait_ge(consts, 1)

            def step(j, p):
                q_, k_, v_ = (qkv[1 - p][:, c, :, :] for c in range(3))
                a = j - 1

                def take_qkv(g):
                    if not has(j):
                        return
                    t, c = g // 3, g % 3
                    wait(dve, qkv_psum, N_QKV * j + g + 1)
                    if g == 0:
                        wait(dve, attn_pool, 2 * (j - 1))
                        wait(dve, attn_dve, 2 * (j - 1))
                    if c == 0:
                        nc.vector.scalar_tensor_tensor(out=qkv[p][:, 0, t, :], in0=qb[g % 4][:, :], scalar=SCALE,
                                                       in1=bqkv[:, 0:D], op0=ALU.mult,
                                                       op1=ALU.add).then_inc(qkv_sb, 1)
                    else:
                        nc.vector.tensor_tensor(qkv[p][:, c, t, :], qb[g % 4][:, :], bqkv[:, c * D:(c + 1) * D],
                                                ALU.add).then_inc(qkv_sb, 1)

                def scores(t):
                    if not has(j, -1):
                        return
                    n = t + 1
                    wait(dve, qkv_sb, N_QKV * (a + 1))
                    wait(dve, qk_sum, R * a + t)
                    wait(dve, attn_dve, 2 * a)
                    nc.vector.tensor_tensor(prod[:, 0:n, :], k_[:, 0:n, :],
                                            q_[:, t:t + 1, :].to_broadcast([P, n, D]), ALU.mult).then_inc(qk_mul, 1)
                    wait(dve, qk_mul, R * a + t + 1)
                    nc.vector.tensor_reduce(logit[:, t, 0:n, :].rearrange("p s h -> p (s h)"),
                                            prod[:, 0:n, :].rearrange("p s (h d) -> p (s h) d", d=DH),
                                            AX.X, ALU.add).then_inc(qk_sum, 1)

                def softmax_top():
                    if not has(j, -1):
                        return
                    wait(dve, qk_sum, R * (a + 1))
                    nc.vector.tensor_reduce(top[:, :, :], logit[:, :, :, :].rearrange("p t s h -> p t h s"),
                                            AX.X, ALU.max).then_inc(top_done, 1)
                    wait(dve, top_done, a + 1)
                    wait(dve, attn_pool, 2 * a)
                    for t in range(R):
                        last = nc.vector.tensor_tensor(prob[:, t, :, :], logit[:, t, :, :],
                                                       top[:, t:t + 1, :].to_broadcast([P, R, H]), ALU.subtract)
                    last.then_inc(sub_done, 1)

                def softmax_norm():
                    if not has(j, -1):
                        return
                    wait(dve, exp_done, a + 1)
                    nc.vector.tensor_reduce(total[:, :, :], prob[:, :, :, :].rearrange("p t s h -> p t h s"),
                                            AX.X, ALU.add).then_inc(tot_done, 1)
                    wait(dve, tot_done, a + 1)
                    nc.vector.reciprocal(total[:, :, :], total[:, :, :]).then_inc(rcp_done, 1)
                    wait(dve, rcp_done, a + 1)
                    for t in range(R):
                        last = nc.vector.tensor_tensor(prob[:, t, :, :], prob[:, t, :, :],
                                                       total[:, t:t + 1, :].to_broadcast([P, R, H]), ALU.mult)
                    last.then_inc(prob_done, 1)

                def weigh_mul(t):
                    if not has(j, -1):
                        return
                    wait(dve, prob_done, a + 1)
                    wait(dve, qk_sum, R * (a + 1))
                    wait(dve, attn_dve, 2 * a + t)
                    nc.vector.tensor_tensor(prod[:, :, :].rearrange("p s (h d) -> p (s h) d", d=DH),
                                            v_.rearrange("p s (h d) -> p (s h) d", d=DH),
                                            bcast(prob[:, t, :, :].rearrange("p s h -> p (s h)"), DH),
                                            ALU.mult).then_inc(pv_mul, 1)

                def weigh_sum(t):
                    if not has(j, -1):
                        return
                    wait(dve, pv_mul, 2 * a + t + 1)
                    nc.vector.tensor_tensor(prod[:, 0:2, :], prod[:, 0:2, :], prod[:, 2:4, :],
                                            ALU.add).then_inc(pv_half, 1)
                    wait(dve, pv_half, 2 * a + t + 1)
                    wait(dve, at_psum, R * (a - 1) + t + 1)
                    nc.vector.tensor_tensor(attn[:, t, :], prod[:, 0, :], prod[:, 1, :],
                                            ALU.add).then_inc(attn_dve, 1)

                if has(j):
                    for k in range(DK):
                        wait(dve, xt_hi, DK * j + k + 1)
                        nc.vector.tensor_tensor(xT[1][:, k, :], tb[k % 2][:, :], xT[0][:, k, :].bitcast(F32),
                                                ALU.subtract).then_inc(xt_lo, 1)
                scores(0)
                take_qkv(0)
                scores(1)
                take_qkv(1)
                scores(2)
                take_qkv(2)
                scores(3)
                take_qkv(3)
                take_qkv(4)
                softmax_top()
                take_qkv(5)
                softmax_norm()
                take_qkv(6)
                weigh_mul(0)
                take_qkv(7)
                weigh_sum(0)
                take_qkv(8)
                weigh_mul(1)
                take_qkv(9)
                weigh_sum(1)
                if has(j, 1):
                    wait(dve, x_in_sem, 16 * (j + 2))
                    for t in range(R):
                        last = nc.vector.bn_stats(stats[:, t, :], x[:, t, :])
                    last.then_inc(bn_done, 1)
                    wait(dve, bn_done, j + 2)
                take_qkv(10)
                if has(j, 1):
                    for t in range(R):
                        last = nc.vector.bn_aggr(mv[:, t, :], stats[:, t, :])
                    last.then_inc(mv_done, 1)
                    wait(dve, mv_done, j + 2)
                    wait(dve, rstd_done, j + 1)
                    nc.vector.tensor_scalar(vare[:, :], mv[:, :, 1], EPS, None, ALU.add).then_inc(var_done, 1)
                take_qkv(11)
                if has(j, 1):
                    wait(dve, rstd_done, j + 2)
                    wait(dve, xn_done, R * (j + 1))
                    nc.vector.scalar_tensor_tensor(out=nmr[:, :], in0=mv[:, :, 0], scalar=-1.0, in1=rstd[:, :],
                                                   op0=ALU.mult, op1=ALU.mult).then_inc(nmr_done, 1)
                if has(j, -1):
                    def take_x1(t):
                        wait(dve, out_psum, R * a + t + 1)
                        wait(dve, res_done, a + 1)
                        nc.vector.tensor_tensor(xres[1 - p][:, t, :], ob[t % 2][:, :], xres[1 - p][:, t, :],
                                                ALU.add).then_inc(x1_done, 1)

                    for t in range(R):
                        if t >= 2:
                            take_x1(t - 2)
                        wait(dve, at_hi, R * a + t + 1)
                        nc.vector.tensor_tensor(aT[t % 2][1][:, :, :].rearrange("p k n -> p (k n)"), tb[t % 2][:, :],
                                                aT[t % 2][0][:, :, :].rearrange("p k n -> p (k n)").bitcast(F32),
                                                ALU.subtract).then_inc(at_lo, 1)
                    take_x1(2)
                    take_x1(3)

            run_steps(dve, step, TILES)


def slot_turns(t):
    turns = [("pv", t), ("out", t)]
    if t == 2:
        turns += [("s", 0), ("s", 1)]
    turns += [("x2T", t)]
    if t in (1, 2):
        turns += [("xT", 2 * t - 2), ("xT", 2 * t - 1)]
    turns += [("aT", t)]
    if t == 3:
        turns += [("q", m) for m in range(DK)]
    return turns + [("pT", 4 * t + g) for g in range(4)] + [("wo", t)]


TURNS = [turn for t in range(R) for turn in slot_turns(t)]
TURNS_OVER = {
    "pv": lambda j, i: 4 * j + i,
    "aT": lambda j, i: 4 * j + i,
    "wo": lambda j, i: 4 * j + i,
    "x2T": lambda j, i: 4 * j + i - 1,
    "pT": lambda j, i: 16 * j + i + 1,
    "xT": lambda j, i: 4 * (j + 1) + i + 1,
    "q": lambda j, i: 4 * (j + 1) + i + 1,
    "s": lambda j, i: 2 * (j - 1) + i + 1,
    "out": lambda j, i: 4 * (j - 2) + i + 1,
}


def active(j, kind, i):
    shift = {"pv": -(i == 0), "aT": -(i == 0), "wo": -(i == 0), "x2T": -(i < 2), "pT": 0,
             "xT": 1, "q": 1, "s": -1, "out": -2}[kind]
    return has(j, shift)


def bank_of(parity, turn):
    return (TURNS.index(turn) + 2 * parity) % 4


def bank_before(j, turn):
    at = TURNS.index(turn) - 4
    while True:
        step, place = (j, at) if at >= 0 else (j - 1, at + len(TURNS))
        if isinstance(step, int) and step < -1:
            return None
        kind, i = TURNS[place]
        if active(step, kind, i):
            return kind, TURNS_OVER[kind](step, i)
        at -= 4
        if at < -len(TURNS):
            return None


def cross_block(nc, x1_dram, scratch, w_in, b_in, out, keep):
    with ExitStack() as stack:
        def sb(name, shape, dt=F32):
            return stack.enter_context(nc.sbuf_tensor(name, shape, dt))

        def sem(name):
            return stack.enter_context(nc.semaphore(name))

        ident, vscale = keep["ident"], keep["vscale"]
        wq = [sb(f"wq{h}", [P, DK, D], F32R) for h in range(2)]
        wo = [sb(f"wo{h}", [P, DK, D], F32R) for h in range(2)]
        win = [sb(f"win{h}", [P, DK, 2 * M], F32R) for h in range(2)]
        wf = [sb(f"wf{h}", [2 * M, D], F32R) for h in range(2)]
        bo = sb("bo", [P, D])
        bf = sb("bf", [P, D])
        bq = sb("bq", [P, DK])
        bin_ = sb("bin", [P, 1])
        hinge = sb("hinge", [P, 3, PAIRS])
        b2 = sb("b2", [P, 1])
        ones = sb("ones", [P, P], F32R)
        kbd = sb("kbd", [P, 2, DK, 4, C], F32R)
        fill = sb("fillrows", [P, C], F32R)
        v = sb("v", [C, 2, 2, D], F16)
        x1 = sb("x1", [P, R, D])
        xr = [sb(f"xr{p}", [P, R, D]) for p in range(2)]
        x2 = [sb(f"x2_{p}", [P, R, D]) for p in range(2)]
        xn = sb("xn_c", [P, 2, D])
        xT = [sb(f"xT_c{h}", [P, DK, 4 * P], F32R) for h in range(2)]
        q = [sb(f"q{h}", [P, DK, 4 * P], F32R) for h in range(2)]
        prob = sb("prob_c", [P, H, C])
        pT = [sb(f"pT{h}", [C, H, P], F16) for h in range(2)]
        attn = sb("attn_c", [P, D])
        aT = [sb(f"aT_c{h}", [P, DK, P], F32R) for h in range(2)]
        xn2 = sb("xn2", [P, D])
        x2T = [sb(f"x2T{h}", [P, DK, 4 * P], F32R) for h in range(2)]
        s_sb = sb("s_sb", [P, 4 * P])
        relu = sb("relu", [P, 2, 4 * P])
        g_sb = sb("g_sb", [P, 4 * P])
        gT = [sb(f"gT{h}", [P, 4 * P], F32R) for h in range(2)]
        ntop = sb("ntop", [P, H])
        total = sb("total_c", [P, 2, H])
        rtotal = sb("rtotal", [P, H])
        half = sb("half_c", [P, R])
        stats, mv, vare, rstd, nmr = (sb(f"{n}_c", sh) for n, sh in
                                      (("stats", [P, R, 6]), ("mv", [P, R, 2]), ("vare", [P, R]),
                                       ("rstd", [P, R]), ("nmr", [P, R])))
        stats2, mv2, vare2, rstd2, nmr2 = (sb(f"{n}_2", sh) for n, sh in
                                           (("stats", [P, 6]), ("mv", [P, 2]), ("vare", [P, 1]),
                                            ("rstd", [P, 1]), ("nmr", [P, 1])))

        sc = [stack.enter_context(nc.psum_tensor(f"sc{m}", [P, 512], F32)) for m in range(4)]
        ring = [stack.enter_context(nc.psum_tensor(f"ring{i}", [P, 512], F32)) for i in range(4)]

        psum = {k: sem(f"psum_{k}") for k in TURNS_OVER}
        taken = {k: sem(f"taken_{k}") for k in TURNS_OVER}
        hi = {k: sem(f"hi_{k}") for k in ("xT", "x2T", "aT", "pT", "q")}
        in_w = [sem(f"in_w{i}") for i in range(4)]
        in_small = sem("in_small")
        w_hi, w_lo = sem("cw_hi"), sem("cw_lo")
        consts, k_zero = sem("c_consts"), sem("k_zero")
        x1_in, ctx_in = sem("c_x1_in"), sem("c_ctx_in")
        k_in, v_in = sem("k_in"), [sem("v_in0"), sem("v_in1")]
        bn_done, mv_done, var_done, rstd_done, nmr_done, xn_done, res_done = (
            sem(f"c_{n}") for n in ("bn", "mv", "var", "rstd", "nmr", "xn", "res"))
        bn2_done, mv2_done, var2_done, rstd2_done, nmr2_done, xn2_done, bf_added = (
            sem(f"c_{n}") for n in ("bn2", "mv2", "var2", "rstd2", "nmr2", "xn2", "bf_added"))
        scored, topped, exped, summed = sem("scored"), sem("topped"), sem("exped"), sem("summed")
        relu_done, hinged, g_hi, g_lo = sem("relu_done"), sem("hinged"), sem("g_hi"), sem("g_lo")
        stored = [[sem(f"stored{p}_{t}") for t in range(R)] for p in range(2)]

        blocks = "(k p) n -> p k n"
        pieces = [([(xr[0][:, :, :], w_in["wq"].rearrange(blocks, p=P))], wq, xr[0][:, :, :]),
                  ([(xr[1][:, :, :], w_in["wo"].rearrange(blocks, p=P))], wo, xr[1][:, :, :]),
                  ([(x2[0][:, :, M * z:M * z + M], w_in["win"].rearrange(blocks, p=P)) for z in range(2)],
                   win, x2[0][:, :, 0:2 * M]),
                  ([(x2[1][M * z:M * z + M, 0, :], w_in["wf"]) for z in range(2)], wf, x2[1][:, 0, :])]
        small = [(bo[:, :], b_in["bo"].rearrange("(o n) -> o n", o=1).to_broadcast([P, D])),
                 (bf[:, :], b_in["bf"].rearrange("(o n) -> o n", o=1).to_broadcast([P, D])),
                 (bq[:, :], b_in["bq"]), (bin_[0:M, :], b_in["bin"]), (bin_[M:2 * M, :], b_in["bin"]),
                 (b2[0:M, :], b_in["b2"])]
        small += [(hinge[M * z:M * z + M, n, :], b_in[name][z]) for n, name in enumerate(("w1", "b1", "w2"))
                  for z in range(2)]

        block = stack.enter_context(nc.Block())

        @block.sync
        def _(sp):
            def load_ctx(j, p):
                row = j // 4
                rows = [row * P + DH * h for h in range(4)]
                rows = rows if isinstance(j, int) else [sp.snap(first) for first in rows]
                sp.wait_ge(k_zero, 1)
                wait_each(sp, (scored, 16 * j), (psum["pv"], 4 * (j - 1)))
                for h in range(4):
                    sp.dma_start(kbd[DH * h:DH * h + DH, :, :, h, :].bitcast(F32),
                                 k_flat[bass.ds(rows[h], DH), :, :, :]).then_inc(k_in, 16)
                sp.dma_start(fill[:, :].bitcast(F32), mask_flat[bass.ds(rows[0], P), :]).then_inc(k_in, 16)
                sp.dma_start(v[:, p, :, :], v_flat[bass.ds(rows[0], P), :, :]).then_inc(v_in[p], 16)

            k_flat = scratch["k"].rearrange("r p a m c -> (r p) a m c")
            mask_flat = scratch["mask"].rearrange("r p c -> (r p) c")
            v_flat = scratch["v"].rearrange("r c a n -> (r c) a n")
            x1_flat = x1_dram.rearrange("r s d -> (r s) d")
            out_flat = out.rearrange("r s d -> (r s) d")

            def tokens(first, count):
                first = first if isinstance(first, int) else sp.snap(first)
                return bass.ds(first, count)

            def step(j, p):
                if has(j, 1):
                    at = tokens((j + 1) * (R * P), R * P)
                    wait_each(sp, (xn_done, R * (j + 1)), (res_done, R * (j + 1)))
                    sp.dma_start(x1[:, :, :], x1_flat[at, :].rearrange("(t p) d -> p t d", p=P)).then_inc(x1_in, 16)
                for t in range(R):
                    if active(j, "out", t):
                        at = tokens((j - 2) * (R * P) + t * P, P)
                        wait(sp, taken["out"], TURNS_OVER["out"](j, t))
                        sp.dma_start(out_flat[at, :], x2[p][:, t, :]).then_inc(stored[p][t], 16)
                if has(j, 1):
                    load_ctx(j + 1, 1 - p)

            for n, (src, _, _) in enumerate(pieces):
                for dst, part in src:
                    sp.dma_start(dst, part).then_inc(in_w[n], 16)
            sp.wait_ge(w_lo, len(pieces))
            run_steps(sp, step, TILES + 1)
            for p in range(2):
                for t in range(R):
                    sp.wait_ge(stored[p][t], 16 * (TILES // 2))

        @block.gpsimd
        def _(pool):
            def step(j, p):
                for t in range(R):
                    if active(j, "x2T", t):
                        over = TURNS_OVER["x2T"](j, t)
                        wait(pool, var2_done, over)
                        wait(pool, xn2_done, over - 1)
                        nc.gpsimd.tensor_tensor(rstd2[:, :], vare2[:, :], half[:, 0:1], ALU.pow).then_inc(rstd2_done, 1)
                    if has(j, 1) and t == 0:
                        wait(pool, var_done, j + 2)
                        wait(pool, xn_done, R * (j + 1))
                        nc.gpsimd.tensor_tensor(rstd[:, :], vare[:, :], half[:, :], ALU.pow).then_inc(rstd_done, 1)
                    if has(j, 1):
                        wait(pool, x1_in, 16 * (j + 2))
                        if t == 0:
                            wait(pool, taken["wo"], 4 * (j - 1) + 3)
                        if t == 3:
                            wait(pool, taken["wo"], 4 * j)
                        nc.gpsimd.tensor_tensor(xr[1 - p][:, t, :], x1[:, t, :], bo[:, :], ALU.add).then_inc(res_done, 1)
                    if active(j, "x2T", t):
                        pp, tt = (1 - p, t + 2) if t < 2 else (p, t - 2)
                        wait(pool, xn2_done, over)
                        wait(pool, bn2_done, over)
                        nc.gpsimd.tensor_tensor(x2[pp][:, tt, :], x2[pp][:, tt, :], bf[:, :],
                                                ALU.add).then_inc(bf_added, 1)

            nc.gpsimd.memset(half[:, :], -0.5)
            nc.gpsimd.memset(ones[:, :].bitcast(F32), 1.0)
            nc.gpsimd.memset(kbd[:, :, :, :, :].bitcast(F32), 0.0).then_inc(k_zero, 1)
            pool.wait_ge(k_zero, 1)
            pool.wait_ge(in_small, 16 * len(small))
            pool.wait_ge(w_lo, len(pieces))
            run_steps(pool, step, TILES + 1)

        @block.tensor
        def _(pe):
            def bank(j, p, turn):
                before = bank_before(j, turn)
                if before:
                    wait(pe, taken[before[0]], before[1])
                return ring[bank_of(p, turn)]

            def product(dst, terms):
                terms = [(s[a], m[b]) for s, m in terms for a, b in PASSES]
                for n, (s, m) in enumerate(terms):
                    last = nc.tensor.matmul(dst, s, m, start=(n == 0), stop=(n == len(terms) - 1))
                return last

            def transpose_tile(dst, src):
                for k in range(DK):
                    last = nc.tensor.transpose(dst[:, k * P:(k + 1) * P], src[:, k * P:(k + 1) * P], ident[:, :])
                return last

            def step(j, p):
                for t in range(R):
                    cols = slice(t * P, (t + 1) * P)
                    if has(j):
                        if t == 0:
                            wait(pe, taken["q"], 4 * (j + 1))
                            wait(pe, k_in, 80 * (j + 1))
                        for m in range(4):
                            wait(pe, exped, 16 * j + 4 * t + m - 3)
                            for n, (a, b) in enumerate(PASSES):
                                nc.tensor.matmul(sc[m][:, :], q[a][:, m, cols],
                                                 kbd[:, b, m, :, :].rearrange("p h c -> p (h c)"),
                                                 start=(n == 0), stop=False)
                            nc.tensor.matmul(sc[m][:, :], ones[:, :],
                                             fill[:, :].rearrange("p (o c) -> p o c", o=1).to_broadcast([P, 4, C]),
                                             start=False, stop=True).then_inc(scored, 1)
                    if active(j, "pv", t):
                        over = TURNS_OVER["pv"](j, t)
                        pp = p if t > 0 else 1 - p
                        wait(pe, taken["pT"], 4 * over)
                        if t == 1:
                            if isinstance(j, int):
                                pe.wait_ge(v_in[pp], 16 * (j // 2 + 1))
                            else:
                                pe.wait_ge(v_in[pp], 8 * (j - p) + 16)
                        dst = bank(j, p, ("pv", t))
                        for h in range(H):
                            head = slice(h * DH, (h + 1) * DH)
                            for n, (a, b) in enumerate(PASSES):
                                last = nc.tensor.matmul(dst[:, head], pT[a][:, h, :], v[:, pp, b, head],
                                                        start=(n == 0), stop=(n == 2))
                        last.then_inc(psum["pv"], 1)
                    if active(j, "out", t):
                        if t == 0:
                            wait(pe, g_lo, j - 1)
                        dst = bank(j, p, ("out", t))
                        product(dst[:, :], [([gT[0][:, cols], gT[1][:, cols]],
                                             [wf[0][:, :], wf[1][:, :]])]).then_inc(psum["out"], 1)
                    if t == 2 and active(j, "s", 0):
                        wait(pe, taken["x2T"], 4 * j)
                        for i in range(2):
                            dst = bank(j, p, ("s", i))
                            part = slice(2 * P * i, 2 * P * (i + 1))
                            product(dst[:, 0:2 * P], [([win[0][:, k, :], win[1][:, k, :]],
                                                       [x2T[0][:, k, part], x2T[1][:, k, part]])
                                                      for k in range(DK)]).then_inc(psum["s"], 1)
                    if active(j, "x2T", t):
                        wait(pe, xn2_done, TURNS_OVER["x2T"](j, t))
                        transpose_tile(bank(j, p, ("x2T", t)), xn2).then_inc(psum["x2T"], 1)
                    if t in (1, 2) and has(j, 1):
                        for i in (2 * t - 2, 2 * t - 1):
                            wait(pe, xn_done, 4 * (j + 1) + i + 1)
                            transpose_tile(bank(j, p, ("xT", i)), xn[:, i % 2, :]).then_inc(psum["xT"], 1)
                    if active(j, "aT", t):
                        wait(pe, taken["pv"], TURNS_OVER["pv"](j, t))
                        transpose_tile(bank(j, p, ("aT", t)), attn).then_inc(psum["aT"], 1)
                    if t == 3 and has(j, 1):
                        wait(pe, taken["xT"], 4 * (j + 2))
                        for m in range(DK):
                            dst = bank(j, p, ("q", m))
                            ms = slice(m * P, (m + 1) * P)
                            product(dst[:, :], [([wq[0][:, k, ms], wq[1][:, k, ms]],
                                                 [xT[0][:, k, :], xT[1][:, k, :]])
                                                for k in range(DK)]).then_inc(psum["q"], 1)
                    if has(j):
                        for g in range(4):
                            wait(pe, exped, 16 * j + 4 * t + g + 1)
                            dst = bank(j, p, ("pT", 4 * t + g))
                            for h in range(4):
                                last = nc.tensor.transpose(dst[:, h * P:(h + 1) * P], prob[:, 4 * g + h, :], ident[:, :])
                            last.then_inc(psum["pT"], 1)
                    if active(j, "wo", t):
                        wait(pe, taken["aT"], TURNS_OVER["aT"](j, t))
                        dst = bank(j, p, ("wo", t))
                        product(dst[:, :], [([aT[0][:, k, :], aT[1][:, k, :]], [wo[0][:, k, :], wo[1][:, k, :]])
                                            for k in range(DK)]).then_inc(psum["wo"], 1)

            pe.wait_ge(w_lo, len(pieces))
            pe.wait_ge(k_zero, 1)
            run_steps(pe, step, TILES + 1)

        @block.scalar
        def _(act):
            def take_hi(j, p, kind, i, dst, func=ACT.Copy, **kw):
                wait(act, psum[kind], TURNS_OVER[kind](j, i))
                nc.scalar.activation(dst, ring[bank_of(p, (kind, i))][:, :], func, **kw).then_inc(hi[kind], 1)

            def step(j, p):
                for t in range(R):
                    if active(j, "x2T", t):
                        over = TURNS_OVER["x2T"](j, t)
                        pp, tt = (1 - p, t + 2) if t < 2 else (p, t - 2)
                        wait(act, nmr2_done, over)
                        wait(act, psum["x2T"], over - 1)
                        nc.scalar.activation(xn2[:, :], x2[pp][:, tt, :], ACT.Identity, bias=nmr2[:, 0:1],
                                             scale=rstd2[:, 0:1]).then_inc(xn2_done, 1)

                    def exps(g):
                        wait(act, topped, 16 * j + 4 * t + g + 1)
                        wait(act, psum["pT"], 16 * j + 4 * t - 3 + g)
                        if g == 0:
                            wait(act, taken["pv"], 4 * j + t - 1)
                        for h in range(4 * g, 4 * g + 4):
                            last = nc.scalar.activation(prob[:, h, :], sc[g][:, (h % 4) * C:(h % 4 + 1) * C], ACT.Exp,
                                                        bias=ntop[:, h:h + 1], accum_out=total[:, t % 2, h:h + 1])
                        last.then_inc(exped, 1)

                    def norm(i):
                        wait(act, nmr_done, j + 2)
                        wait(act, psum["xT"], 4 * (j + 1) + i - 1)
                        nc.scalar.activation(xn[:, i % 2, :], x1[:, i, :], ACT.Identity, bias=nmr[:, i:i + 1],
                                             scale=rstd[:, i:i + 1]).then_inc(xn_done, 1)

                    if has(j):
                        exps(0)
                        exps(1)
                    if t in (1, 2) and has(j, 1) and t == 1:
                        norm(0)
                        norm(1)
                    if has(j):
                        exps(2)
                    if active(j, "x2T", t):
                        if t == 2:
                            wait(act, psum["s"], 2 * j)
                        tok = slice((t + 2) % 4 * P, ((t + 2) % 4 + 1) * P)
                        take_hi(j, p, "x2T", t, x2T[0][:, :, tok])
                    if has(j):
                        exps(3)
                    if t in (1, 2) and has(j, 1):
                        for i in (2 * t - 2, 2 * t - 1):
                            if i == 0:
                                wait(act, psum["q"], 4 * (j + 1))
                            take_hi(j, p, "xT", i, xT[0][:, :, i * P:(i + 1) * P])
                            if t == 1:
                                norm(i + 2)
                    if active(j, "aT", t):
                        wait(act, psum["wo"], 4 * j + t - 1)
                        take_hi(j, p, "aT", t, aT[0][:, :, :])
                    if t == 3 and has(j, 1):
                        wait(act, scored, 16 * (j + 1))
                        for m in range(DK):
                            take_hi(j, p, "q", m, q[0][:, m, :], ACT.Identity, bias=bq[:, m:m + 1])
                    if has(j):
                        wait(act, psum["pv"], 4 * j + t)
                        for g in range(4):
                            take_hi(j, p, "pT", 4 * t + g, pT[0][:, 4 * g:4 * g + 4, :])
                    if t == 3 and active(j, "s", 0):
                        wait(act, taken["s"], 2 * j)
                        for i in range(PAIRS):
                            wait(act, hinged, PAIRS * (j - 1) + i - 1)
                            nc.scalar.activation(relu[:, i % 2, :], s_sb[:, :], ACT.Relu, bias=hinge[:, 1, i:i + 1],
                                                 scale=hinge[:, 0, i:i + 1]).then_inc(relu_done, 1)

            for dst, src in small:
                act.dma_start(dst, src).then_inc(in_small, 16)
            for n, (loads, (whi, _), staging) in enumerate(pieces):
                act.wait_ge(in_w[n], 16 * len(loads))
                whi = whi[:, :, :] if n < 3 else whi[:, :]
                if n == 1:
                    for k in range(DK):
                        last = nc.scalar.activation(whi[:, k, :], staging[:, k, :], ACT.Copy, scale=vscale[:, k:k + 1])
                else:
                    last = nc.scalar.activation(whi, staging, ACT.Copy)
                last.then_inc(w_hi, 1)
            act.wait_ge(in_small, 16 * len(small))
            run_steps(act, step, TILES + 1)

        @block.vector
        def _(dve):
            def take_lo(j, p, kind, i, dst, hi_part):
                wait(dve, hi[kind], TURNS_OVER[kind](j, i))
                src = ring[bank_of(p, (kind, i))][:, :]
                nc.vector.tensor_tensor(dst, src, hi_part, ALU.subtract).then_inc(taken[kind], 1)

            def step(j, p):
                for t in range(R):
                    tile = 4 * j + t
                    two, one = active(j, "x2T", t), has(j, 1) and t == 0
                    over2 = TURNS_OVER["x2T"](j, t)
                    pp, tt = (1 - p, t + 2) if t < 2 else (p, t - 2)

                    def tops(g):
                        if not has(j):
                            return
                        wait(dve, scored, 16 * j + 4 * t + g + 1)
                        if g == 0:
                            wait(dve, exped, 16 * j + 4 * t)
                        nc.vector.tensor_reduce(ntop[:, 4 * g:4 * g + 4], sc[g][:, :].rearrange("p (h c) -> p h c", c=C),
                                                AX.X, ALU.max, negate=True).then_inc(topped, 1)

                    if two:
                        wait(dve, taken["wo"], over2)
                        nc.vector.bn_stats(stats2[:, :], x2[pp][:, tt, :]).then_inc(bn2_done, 1)
                        wait(dve, bn2_done, over2)
                        wait(dve, rstd2_done, over2 - 1)
                    tops(0)
                    if two:
                        nc.vector.bn_aggr(mv2[:, :], stats2[:, :]).then_inc(mv2_done, 1)
                        wait(dve, mv2_done, over2)
                        nc.vector.tensor_scalar(vare2[:, :], mv2[:, 1:2], EPS, None, ALU.add).then_inc(var2_done, 1)
                    tops(1)
                    if two:
                        wait(dve, rstd2_done, over2)
                        wait(dve, xn2_done, over2 - 1)
                        nc.vector.scalar_tensor_tensor(out=nmr2[:, :], in0=mv2[:, 0:1], scalar=-1.0, in1=rstd2[:, :],
                                                       op0=ALU.mult, op1=ALU.mult).then_inc(nmr2_done, 1)
                    tops(2)
                    if one:
                        wait(dve, x1_in, 16 * (j + 2))
                        for i in range(R):
                            last = nc.vector.bn_stats(stats[:, i, :], x1[:, i, :])
                        last.then_inc(bn_done, 1)
                        wait(dve, bn_done, j + 2)
                    tops(3)
                    if one:
                        for i in range(R):
                            last = nc.vector.bn_aggr(mv[:, i, :], stats[:, i, :])
                        last.then_inc(mv_done, 1)
                        wait(dve, mv_done, j + 2)
                        wait(dve, rstd_done, j + 1)
                        nc.vector.tensor_scalar(vare[:, :], mv[:, :, 1], EPS, None, ALU.add).then_inc(var_done, 1)
                    if active(j, "pv", t):
                        over = TURNS_OVER["pv"](j, t)
                        wait(dve, exped, 4 * over)
                        wait(dve, taken["pv"], over - 1)
                        nc.vector.reciprocal(rtotal[:, :], total[:, (t - 1) % 2, :]).then_inc(summed, 1)
                        wait(dve, summed, over)
                        wait(dve, psum["pv"], over)
                        wait(dve, psum["aT"], over - 1)
                        nc.vector.tensor_tensor(attn[:, :].rearrange("p (h d) -> p h d", d=DH),
                                                ring[bank_of(p, ("pv", t))][:, :].rearrange("p (h d) -> p h d", d=DH),
                                                bcast(rtotal[:, :], DH), ALU.mult).then_inc(taken["pv"], 1)
                    if active(j, "out", t):
                        wait(dve, psum["out"], TURNS_OVER["out"](j, t))
                        if t == 0:
                            wait(dve, bf_added, 4 * (j - 1))
                        nc.vector.tensor_tensor(x2[p][:, t, :], ring[bank_of(p, ("out", t))][:, :], x2[p][:, t, :],
                                                ALU.add).then_inc(taken["out"], 1)
                    if one:
                        wait(dve, rstd_done, j + 2)
                        wait(dve, xn_done, R * (j + 1))
                        nc.vector.scalar_tensor_tensor(out=nmr[:, :], in0=mv[:, :, 0], scalar=-1.0, in1=rstd[:, :],
                                                       op0=ALU.mult, op1=ALU.mult).then_inc(nmr_done, 1)
                    if t == 2 and active(j, "s", 0):
                        wait(dve, relu_done, PAIRS * (j - 1))
                        for i in range(2):
                            wait(dve, psum["s"], TURNS_OVER["s"](j, i))
                            nc.vector.tensor_scalar(s_sb[:, 2 * P * i:2 * P * (i + 1)],
                                                    ring[bank_of(p, ("s", i))][:, 0:2 * P], bin_[:, 0:1], None,
                                                    ALU.add).then_inc(taken["s"], 1)
                    if two:
                        tok = slice((t + 2) % 4 * P, ((t + 2) % 4 + 1) * P)
                        take_lo(j, p, "x2T", t, x2T[1][:, :, tok], x2T[0][:, :, tok].bitcast(F32))
                    if t in (1, 2) and has(j, 1):
                        for i in (2 * t - 2, 2 * t - 1):
                            tok = slice(i * P, (i + 1) * P)
                            take_lo(j, p, "xT", i, xT[1][:, :, tok], xT[0][:, :, tok].bitcast(F32))
                    if active(j, "aT", t):
                        take_lo(j, p, "aT", t, aT[1][:, :, :], aT[0][:, :, :].bitcast(F32))
                    if t == 3 and has(j, 1):
                        for m in range(DK):
                            wait(dve, hi["q"], TURNS_OVER["q"](j, m))
                            nc.vector.scalar_tensor_tensor(out=q[1][:, m, :], in0=ring[bank_of(p, ("q", m))][:, :],
                                                           scalar=bq[:, m:m + 1], in1=q[0][:, m, :].bitcast(F32),
                                                           op0=ALU.add, op1=ALU.subtract).then_inc(taken["q"], 1)
                    if has(j):
                        for g in range(4):
                            heads = slice(4 * g, 4 * g + 4)
                            take_lo(j, p, "pT", 4 * t + g, pT[1][:, heads, :], pT[0][:, heads, :])
                    if active(j, "wo", t):
                        over = TURNS_OVER["wo"](j, t)
                        pw, tw = (1 - p, 3) if t == 0 else (p, t - 1)
                        wait(dve, psum["wo"], over)
                        wait(dve, res_done, over)
                        if isinstance(j, int):
                            wait(dve, stored[pw][tw], 16 * ((j - (t == 0)) // 2))
                        else:
                            wait(dve, stored[pw][tw], 8 * (j - (t == 0) - pw))
                        nc.vector.tensor_tensor(x2[pw][:, tw, :], ring[bank_of(p, ("wo", t))][:, :], xr[pw][:, tw, :],
                                                ALU.add).then_inc(taken["wo"], 1)
                    if t == 3 and active(j, "s", 0):
                        base = PAIRS * (j - 1)
                        wait(dve, g_lo, j - 1)
                        for i in range(PAIRS):
                            wait(dve, relu_done, base + i + 1)
                            wait(dve, hinged, base + i)
                            if i == 0:
                                nc.vector.tensor_scalar(g_sb[:, :], relu[:, 0, :], hinge[:, 2, 0:1], b2[:, 0:1],
                                                        ALU.mult, ALU.add).then_inc(hinged, 1)
                            else:
                                nc.vector.scalar_tensor_tensor(out=g_sb[:, :], in0=relu[:, i % 2, :],
                                                               scalar=hinge[:, 2, i:i + 1], in1=g_sb[:, :],
                                                               op0=ALU.mult, op1=ALU.add).then_inc(hinged, 1)
                        wait(dve, hinged, base + PAIRS)
                        wait(dve, psum["out"], 4 * (j - 1))
                        nc.vector.tensor_copy(gT[0][:, :], g_sb[:, :]).then_inc(g_hi, 1)
                        wait(dve, g_hi, j)
                        nc.vector.tensor_tensor(gT[1][:, :], g_sb[:, :], gT[0][:, :].bitcast(F32),
                                                ALU.subtract).then_inc(g_lo, 1)

            nc.vector.memset(b2[M:2 * M, :], 0.0).then_inc(consts, 1)
            for n, (_, (whi, wlo), staging) in enumerate(pieces):
                dve.wait_ge(w_hi, n + 1)
                whi, wlo = (x[:, :, :] if n < 3 else x[:, :] for x in (whi, wlo))
                if n == 1:
                    for k in range(DK):
                        last = nc.vector.scalar_tensor_tensor(out=wlo[:, k, :], in0=staging[:, k, :],
                                                              scalar=vscale[:, k:k + 1], in1=whi[:, k, :].bitcast(F32),
                                                              op0=ALU.mult, op1=ALU.subtract)
                else:
                    last = nc.vector.tensor_tensor(wlo, staging, whi.bitcast(F32), ALU.subtract)
                last.then_inc(w_lo, 1)
            dve.wait_ge(in_small, 16 * len(small))
            dve.wait_ge(consts, 1)
            run_steps(dve, step, TILES + 1)


def build_program(nc, x, ctx, mask, w, b, out, debug_x1=None):
    x1_dram = debug_x1 if debug_x1 is not None else nc.dram_tensor("x1_scratch", [R, S, D], F32).ap()
    scratch = {"k": nc.dram_tensor("k_scratch", [R, P, 2, DK, C], F32).ap(),
               "v": nc.dram_tensor("v_scratch", [R, C, 2, D], F16).ap(),
               "mask": nc.dram_tensor("mask_scratch", [R, P, C], F32).ap()}
    with ExitStack() as stack:
        def sb(name, shape, dt=F32):
            return stack.enter_context(nc.sbuf_tensor(name, shape, dt))

        keep = {"ident": sb("ident", [P, P]), "vscale": sb("vscale", [P, DK])}
        with ExitStack() as stack1:
            def sb1(name, shape, dt=F32):
                return stack1.enter_context(nc.sbuf_tensor(name, shape, dt))

            keep["wqkv"] = [sb1(f"wqkv{h}", [P, DK, 3 * D], F32R) for h in range(2)]
            keep["wout"] = [sb1(f"wout{h}", [P, DK, D], F32R) for h in range(2)]
            keep["bqkv"] = sb1("bqkv", [P, 3 * D])
            keep["bout"] = sb1("bout", [P, D])
            prepare_block(nc, ctx, mask, w, b, scratch, keep)
            self_block(nc, x, x1_dram, keep)
        if debug_x1 is None:
            cross_block(nc, x1_dram, scratch, w, b, out, keep)


def kernel(**inputs):
    import concourse.bacc as bacc
    from concourse.bass_utils import run_bass_kernel_spmd

    nc = bacc.Bacc("TRN2", target_bir_lowering=False, num_devices=1)
    arrays = {}

    def dram(name, array):
        arrays[name] = np.ascontiguousarray(array)
        return nc.dram_tensor(name, arrays[name].shape, mybir.dt.from_np(arrays[name].dtype),
                              kind="ExternalInput").ap()

    given = {name: np.asarray(a) for name, a in inputs.items()}
    w = {name: dram(f"in_{name}", given[key].T) for name, key in (
        ("wqkv", "L0_attn_qkv_w"), ("wout", "L0_attn_out_w"), ("wq", "L0_xattn_Wq"), ("wk", "L0_xattn_Wk"),
        ("wv", "L0_xattn_Wv"), ("wo", "L0_xattn_Wo"))}
    w["win"] = dram("in_win", given["L0_ffn_Win"])
    w["wf"] = dram("in_wf", given["L0_ffn_Wout"])
    b = {name: dram(f"in_{name}", given[key]) for name, key in (
        ("bqkv", "L0_attn_qkv_b"), ("bout", "L0_attn_out_b"), ("bo", "L0_xattn_bo"), ("bf", "L0_ffn_bout"))}
    for name, key in (("bk", "L0_xattn_bk"), ("bv", "L0_xattn_bv"), ("bq", "L0_xattn_bq")):
        b[name] = dram(f"in_{name}", given[key].reshape(DK, P).T)
    for name, key in (("bin", "L0_ffn_bin_"), ("b2", "L0_ffn_b2")):
        b[name] = dram(f"in_{name}", given[key].reshape(M, 1))
    for name, key in (("w1", "L0_ffn_W1"), ("b1", "L0_ffn_b1"), ("w2", "L0_ffn_W2")):
        b[name] = dram(f"in_{name}", given[key].reshape(M, PAIRS, 2).transpose(2, 0, 1))
    x = dram("in_x", given["x"])
    ctx = dram("in_ctx", given["ctx_1024"])
    mask = dram("in_mask", given["mask_BxS2_bf1"].view(np.uint8))
    out = nc.dram_tensor("out", (R, S, D), F32, kind="ExternalOutput").ap()
    build_program(nc, x, ctx, mask, w, b, out)
    return run_bass_kernel_spmd(nc, [arrays], core_ids=[0]).results[0]["out"]
```

```python
from contextlib import ExitStack

import numpy as np

import concourse.bass as bass
from concourse import mybir

F32 = mybir.dt.float32
F32R = mybir.dt.float32r
F16 = mybir.dt.float16
U8 = mybir.dt.uint8
ALU = mybir.AluOpType
ACT = mybir.ActivationFunctionType
AX = mybir.AxisListType

P = 128
D = 512
DK = D // P
R = 4
S = 2048
H = 16
DH = D // H
C = 128
TILES = S // P
SCALE = DH ** -0.5
EPS = 1e-5
CAUSAL_FILL = -10000.0
MASK_FILL = -100000000.0
MASK_FILL_HI = -99975168.0
MASK_FILL_LO = MASK_FILL - MASK_FILL_HI
M = 64
INNER = 16
PAIRS = INNER // 2
PASSES = ((0, 0), (0, 1), (1, 0))


def wait(eng, sem, count):
    if isinstance(count, int) and count <= 0:
        return
    eng.wait_ge(sem, count)


def wait_each(eng, *pairs):
    pairs = [(sem, count if isinstance(count, int) else eng.snap(count)) for sem, count in pairs]
    for sem, count in pairs:
        wait(eng, sem, count)


def bcast(ap, n):
    return ap.rearrange("p (a b) -> p a b", b=1).to_broadcast([ap.shape[0], ap.shape[1], n])


def run_steps(eng, step, last):
    for j in (-1, 0, 1, 2):
        step(j, j % 2)
    with eng.Fori(0, (TILES - 4) // 2) as i:
        step(2 * i + 3, 1)
        step(2 * i + 4, 0)
    for j in range(TILES - 1, last + 1):
        step(j, j % 2)


def has(j, shift=0):
    return not isinstance(j, int) or 0 <= j + shift < TILES


def prepare_block(nc, ctx_in, mask_in, w_in, b_in, scratch, keep):
    with ExitStack() as stack:
        def sb(name, shape, dt=F32):
            return stack.enter_context(nc.sbuf_tensor(name, shape, dt))

        def sem(name):
            return stack.enter_context(nc.semaphore(name))

        ctx = sb("ctx", [P, R, D])
        raw = [sb(f"raw{i}", [P, DK, D]) for i in range(2)]
        wkv = [[sb(f"wkv{i}_{h}", [P, DK, D], F32R) for h in range(2)] for i in range(2)]
        ctxT = [sb(f"ctxT{h}", [P, DK, R * C], F32R) for h in range(2)]
        kvT = sb("kvT", [P, DK, R * C])
        khi = sb("khi", [P, DK, R * C], F32R)
        klo = sb("klo", [P, DK, R * C], F32R)
        vhi = sb("vhi", [P, R, D], F16)
        vlo = sb("vlo", [P, R, D], F16)
        mask8 = sb("mask8", [P, R * C], U8)
        mask = sb("mask", [P, R * C])
        bkv = sb("bkv", [P, 2, DK])
        rvs = sb("rvs", [P, DK])
        fill = sb("fill", [P, 1])
        maskfill = sb("maskfill", [P, R * C], F32R)
        ps = [stack.enter_context(nc.psum_tensor(f"pp{i}", [P, 512], F32)) for i in range(4)]

        in_ctx, in_mask, in_bkv, in_bias = sem("in_ctx"), sem("in_mask"), sem("in_bkv"), sem("in_bias")
        in_raw = [sem("in_raw0"), sem("in_raw1")]
        zeroed, ident_ready = sem("zeroed"), sem("ident_ready")
        w_hi, w_lo = sem("w_hi"), sem("w_lo")
        trans, t_hi, t_lo = sem("trans"), sem("t_hi"), sem("t_lo")
        kvt_done, kvt_sb = sem("kvt_done"), sem("kvt_sb")
        k_masked, k_hi, k_lo = sem("k_masked"), sem("k_hi"), sem("k_lo")
        bk_scaled, mask_f, mask_inv, fill_ready, mask_rows = (
            sem("bk_scaled"), sem("mask_f"), sem("mask_inv"), sem("fill_ready"), sem("mask_rows"))
        v_max, v_rcp, v_unit = sem("v_max"), sem("v_rcp"), sem("v_unit")
        v_trans, v_h, v_l = sem("v_trans"), sem("v_h"), sem("v_l")
        kv_out, bias_ready = sem("kv_out"), sem("bias_ready")

        ident, wqkv, wout = keep["ident"], keep["wqkv"], keep["wout"]
        bqkv, bout, vscale = keep["bqkv"], keep["bout"], keep["vscale"]
        k_dram, v_dram = scratch["k"], scratch["v"]

        pieces = ([(w_in["wk"], wkv[0][0][:, :, :], wkv[0][1][:, :, :]),
                   (w_in["wv"], wkv[1][0][:, :, :], wkv[1][1][:, :, :])]
                  + [(w_in["wqkv"][:, c * D:(c + 1) * D], wqkv[0][:, :, c * D:(c + 1) * D],
                      wqkv[1][:, :, c * D:(c + 1) * D]) for c in range(3)]
                  + [(w_in["wout"], wout[0][:, :, :], wout[1][:, :, :])])

        block = stack.enter_context(nc.Block())

        @block.sync
        def _(sp):
            sp.dma_start(ctx[:, :, :], ctx_in.rearrange("b c d -> c b d")).then_inc(in_ctx, 16)
            for n, (src, _, _) in enumerate(pieces):
                wait(sp, w_lo, n - 1)
                sp.dma_start(raw[n % 2][:, :, :], src.rearrange("(k p) n -> p k n", p=P)).then_inc(in_raw[n % 2], 16)
            sp.wait_ge(k_lo, DK)
            for r in range(R):
                cols = slice(r * C, (r + 1) * C)
                sp.dma_start(k_dram[r, :, 0, :, :], khi[:, :, cols].bitcast(F32)).then_inc(kv_out, 16)
                sp.dma_start(k_dram[r, :, 1, :, :], klo[:, :, cols].bitcast(F32)).then_inc(kv_out, 16)
            sp.wait_ge(v_h, R)
            sp.wait_ge(v_l, R)
            sp.wait_ge(mask_rows, 1)
            for r in range(R):
                sp.dma_start(scratch["mask"][r, :, :], maskfill[:, r * C:(r + 1) * C].bitcast(F32)).then_inc(kv_out, 16)
                sp.dma_start(v_dram[r, :, 0, :], vhi[:, r, :]).then_inc(kv_out, 16)
                sp.dma_start(v_dram[r, :, 1, :], vlo[:, r, :]).then_inc(kv_out, 16)
            sp.wait_ge(kv_out, 16 * 5 * R)

        @block.gpsimd
        def _(pool):
            nc.gpsimd.memset(ident[:, :], 0.0).then_inc(zeroed, 1)
            pool.wait_ge(zeroed, 1)
            nc.gpsimd.affine_select(out=ident[:, :], in_=ident[:, :], compare_op=ALU.not_equal, fill=1.0,
                                    base=0, pattern=[[-1, P]], channel_multiplier=1).then_inc(ident_ready, 1)

        @block.tensor
        def _(pe):
            pe.wait_ge(ident_ready, 1)
            pe.wait_ge(in_ctx, 16)
            for k in range(DK):
                for r in range(R):
                    last = nc.tensor.transpose(ps[k][:, r * C:(r + 1) * C], ctx[:, r, k * P:(k + 1) * P], ident[:, :])
                last.then_inc(trans, 1)
            pe.wait_ge(t_lo, DK)
            for i in range(2):
                pe.wait_ge(w_lo, i + 1)
                for m in range(DK):
                    wait(pe, kvt_sb, DK * (i - 1) + m + 1)
                    n = 0
                    for k in range(DK):
                        for a, b in PASSES:
                            last = nc.tensor.matmul(ps[m][:, :], wkv[i][a][:, k, m * P:(m + 1) * P],
                                                    ctxT[b][:, k, :], start=(n == 0), stop=(n == 11))
                            n += 1
                    last.then_inc(kvt_done, 1)
            pe.wait_ge(v_unit, 1)
            for r in range(R):
                for m in range(DK):
                    last = nc.tensor.transpose(ps[r][:, m * P:(m + 1) * P], kvT[:, m, r * C:(r + 1) * C], ident[:, :])
                last.then_inc(v_trans, 1)

        @block.scalar
        def _(act):
            act.dma_start(mask8[:, :], mask_in.rearrange("b c -> (b c)").rearrange("(o n) -> o n", o=1).to_broadcast([P, R * C])
                          ).then_inc(in_mask, 16)
            for i, name in enumerate(("bk", "bv")):
                act.dma_start(bkv[:, i, :], b_in[name]).then_inc(in_bkv, 16)
            act.dma_start(bqkv[:, :], b_in["bqkv"].rearrange("(o n) -> o n", o=1).to_broadcast([P, 3 * D])
                          ).then_inc(in_bias, 16)
            act.dma_start(bout[:, :], b_in["bout"].rearrange("(o n) -> o n", o=1).to_broadcast([P, D])
                          ).then_inc(in_bias, 16)
            for n in range(2):
                act.wait_ge(in_raw[n % 2], 16 * (n // 2 + 1))
                nc.scalar.activation(pieces[n][1], raw[n % 2][:, :, :], ACT.Copy).then_inc(w_hi, 1)
            for k in range(DK):
                act.wait_ge(trans, k + 1)
                nc.scalar.activation(ctxT[0][:, k, :], ps[k][:, :], ACT.Copy).then_inc(t_hi, 1)
            act.wait_ge(bk_scaled, 1)
            for m in range(DK):
                act.wait_ge(kvt_done, m + 1)
                nc.scalar.activation(kvT[:, m, :], ps[m][:, :], ACT.Identity, bias=bkv[:, 0, m:m + 1],
                                     scale=SCALE).then_inc(kvt_sb, 1)
            for m in range(DK):
                act.wait_ge(kvt_done, DK + m + 1)
                act.wait_ge(k_lo, m + 1)
                nc.scalar.activation(kvT[:, m, :], ps[m][:, :], ACT.Identity, bias=bkv[:, 1, m:m + 1]
                                     ).then_inc(kvt_sb, 1)
            for n in range(2, len(pieces)):
                act.wait_ge(in_raw[n % 2], 16 * (n // 2 + 1))
                nc.scalar.activation(pieces[n][1], raw[n % 2][:, :, :], ACT.Copy).then_inc(w_hi, 1)
            for r in range(R):
                act.wait_ge(v_trans, r + 1)
                nc.scalar.activation(vhi[:, r, :], ps[r][:, :], ACT.Copy).then_inc(v_h, 1)

        @block.vector
        def _(dve):
            def split_lo(n):
                dve.wait_ge(w_hi, n + 1)
                nc.vector.tensor_tensor(pieces[n][2], raw[n % 2][:, :, :], pieces[n][1].bitcast(F32),
                                        ALU.subtract).then_inc(w_lo, 1)

            nc.vector.memset(fill[:, :], 0.0).then_inc(fill_ready, 1)
            dve.wait_ge(fill_ready, 1)
            nc.vector.memset(fill[0:2, :], MASK_FILL_LO).then_inc(fill_ready, 1)
            dve.wait_ge(fill_ready, 2)
            nc.vector.memset(fill[0:1, :], MASK_FILL_HI).then_inc(fill_ready, 1)
            dve.wait_ge(in_mask, 16)
            nc.vector.tensor_copy(mask[:, :], mask8[:, :]).then_inc(mask_f, 1)
            dve.wait_ge(in_bkv, 32)
            nc.vector.tensor_scalar(bkv[:, 0, :], bkv[:, 0, :], SCALE, None, ALU.mult).then_inc(bk_scaled, 1)
            split_lo(0)
            split_lo(1)
            for k in range(DK):
                dve.wait_ge(t_hi, k + 1)
                nc.vector.tensor_tensor(ctxT[1][:, k, :], ps[k][:, :], ctxT[0][:, k, :].bitcast(F32),
                                        ALU.subtract).then_inc(t_lo, 1)
            dve.wait_ge(mask_f, 1)
            for m in range(DK):
                dve.wait_ge(kvt_sb, m + 1)
                nc.vector.tensor_tensor(kvT[:, m, :], kvT[:, m, :], mask[:, :], ALU.mult).then_inc(k_masked, 1)
                dve.wait_ge(k_masked, m + 1)
                nc.vector.tensor_copy(khi[:, m, :], kvT[:, m, :]).then_inc(k_hi, 1)
                dve.wait_ge(k_hi, m + 1)
                nc.vector.tensor_tensor(klo[:, m, :], kvT[:, m, :], khi[:, m, :].bitcast(F32),
                                        ALU.subtract).then_inc(k_lo, 1)
            nc.vector.tensor_scalar(mask[:, :], mask[:, :], -1.0, 1.0, ALU.mult, ALU.add).then_inc(mask_inv, 1)
            dve.wait_ge(mask_inv, 1)
            dve.wait_ge(fill_ready, 3)
            nc.vector.tensor_scalar(maskfill[:, :], mask[:, :], fill[:, 0:1], None, ALU.mult).then_inc(mask_rows, 1)
            for m in range(DK):
                dve.wait_ge(kvt_sb, DK + m + 1)
                nc.vector.tensor_reduce(vscale[:, m:m + 1], kvT[:, m, :], AX.X, ALU.max,
                                        apply_absolute_value=True).then_inc(v_max, 1)
            dve.wait_ge(v_max, DK)
            nc.vector.tensor_scalar(vscale[:, :], vscale[:, :], 1e-30, None, ALU.max).then_inc(v_max, 1)
            dve.wait_ge(v_max, DK + 1)
            nc.vector.reciprocal(rvs[:, :], vscale[:, :]).then_inc(v_rcp, 1)
            dve.wait_ge(v_rcp, 1)
            for m in range(DK):
                last = nc.vector.tensor_scalar(kvT[:, m, :], kvT[:, m, :], rvs[:, m:m + 1], None, ALU.mult)
            last.then_inc(v_unit, 1)
            for n in range(2, len(pieces)):
                split_lo(n)
            for r in range(R):
                dve.wait_ge(v_h, r + 1)
                nc.vector.tensor_tensor(vlo[:, r, :], ps[r][:, :], vhi[:, r, :], ALU.subtract).then_inc(v_l, 1)
            dve.wait_ge(in_bias, 32)
            nc.vector.tensor_scalar(bqkv[:, 0:D], bqkv[:, 0:D], SCALE, None, ALU.mult).then_inc(bias_ready, 1)


def self_block(nc, x_in, x1_dram, keep):
    with ExitStack() as stack:
        def sb(name, shape, dt=F32):
            return stack.enter_context(nc.sbuf_tensor(name, shape, dt))

        def sem(name):
            return stack.enter_context(nc.semaphore(name))

        ident, wqkv, wout, bqkv, bout = keep["ident"], keep["wqkv"], keep["wout"], keep["bqkv"], keep["bout"]
        x = sb("x", [P, R, D])
        xres = [sb(f"xres{p}", [P, R, D]) for p in range(2)]
        xn = sb("xn", [P, R, D])
        xT = [[sb(f"xT{p}_{h}", [P, DK, R * P], F32R) for h in range(2)] for p in range(2)]
        qk = [sb(f"qk{p}", [P, 2, R, D]) for p in range(2)]
        v = sb("v", [P, R, D])
        prod = sb("prod", [P, R, D])
        prod_pool = sb("prod_pool", [P, 2, D])
        attn = sb("attn", [P, R, D])
        aT = [[sb(f"aT{b}_{h}", [P, DK, P], F32R) for h in range(2)] for b in range(2)]
        logit = sb("logit", [P, R, R, H])
        prob = sb("prob", [P, R, R, H])
        top = sb("top", [P, R, H])
        total = sb("total", [P, R, H])
        stats = sb("stats", [P, R, 6])
        mv = sb("mv", [P, R, 2])
        vare = sb("vare", [P, R])
        rstd = sb("rstd", [P, R])
        nmr = sb("nmr", [P, R])
        half = sb("half", [P, R])

        tb = [stack.enter_context(nc.psum_tensor(f"tb{i}", [P, 512], F32)) for i in range(2)]
        qb = [stack.enter_context(nc.psum_tensor(f"qb{i}", [P, 512], F32)) for i in range(4)]
        ob = [stack.enter_context(nc.psum_tensor(f"ob{i}", [P, 512], F32)) for i in range(2)]

        x_in_sem = sem("x_in")
        x1_out = [sem(f"x1_out{p}") for p in range(2)]
        consts, half_set = sem("consts"), sem("half_set")
        bn_done, mv_done, var_done, rstd_done, nmr_done, xn_done = (
            sem("bn_done"), sem("mv_done"), sem("var_done"), sem("rstd_done"), sem("nmr_done"), sem("xn_done"))
        res_done = sem("res_done")
        xt_psum, xt_hi, xt_lo = sem("xt_psum"), sem("xt_hi"), sem("xt_lo")
        qkv_psum, qkv_sb = sem("qkv_psum"), sem("qkv_sb")
        qk_mul, qk_sum, top_done, sub_done, exp_done, tot_done, rcp_done, prob_done = (
            sem("qk_mul"), sem("qk_sum"), sem("top_done"), sem("sub_done"), sem("exp_done"), sem("tot_done"),
            sem("rcp_done"), sem("prob_done"))
        pv_mul, pv_half, attn_dve = sem("pv_mul"), sem("pv_half"), sem("attn_dve")
        pool_step, attn_pool = sem("pool_step"), sem("attn_pool")
        at_psum, at_hi, at_lo = sem("at_psum"), sem("at_hi"), sem("at_lo")
        out_psum, x1_done = sem("out_psum"), sem("x1_done")

        N_QKV = 3 * R
        block = stack.enter_context(nc.Block())

        @block.sync
        def _(sp):
            def rows(j):
                return bass.ds(j * P, P) if isinstance(j, int) else bass.ds(sp.snap(j * P), P)

            def step(j, p):
                if has(j, 1):
                    at = rows(j + 1)
                    wait_each(sp, (xn_done, R * (j + 1)), (res_done, j + 1))
                    sp.dma_start(x[:, :, :], x_in[:, at, :].rearrange("t p d -> p t d")).then_inc(x_in_sem, 16)
                if has(j, -1):
                    at = rows(j - 1)
                    wait(sp, x1_done, R * j)
                    sp.dma_start(x1_dram[:, at, :].rearrange("t p d -> p t d"),
                                 xres[1 - p][:, :, :]).then_inc(x1_out[1 - p], 16)

            run_steps(sp, step, TILES)
            for p in range(2):
                sp.wait_ge(x1_out[p], 16 * (TILES // 2))

        @block.gpsimd
        def _(pool):

            def step(j, p):
                if has(j, 1):
                    wait(pool, var_done, j + 2)
                    wait(pool, xn_done, R * (j + 1))
                    nc.gpsimd.tensor_tensor(rstd[:, :], vare[:, :], half[:, :], ALU.pow).then_inc(rstd_done, 1)
                if has(j, -1):
                    a = j - 1
                    wait(pool, prob_done, a + 1)
                    wait(pool, qkv_sb, N_QKV * (a + 1))
                    for t in (2, 3):
                        base = 8 * a + 4 * (t - 2)
                        wait(pool, at_psum, R * (a - 1) + t + 1)
                        for s in (0, 2):
                            wait(pool, pool_step, base + s)
                            nc.gpsimd.tensor_tensor(
                                prod_pool[:, :, :].rearrange("p s (h d) -> p (s h) d", d=DH),
                                v[:, s:s + 2, :].rearrange("p s (h d) -> p (s h) d", d=DH),
                                bcast(prob[:, t, s:s + 2, :].rearrange("p s h -> p (s h)"), DH),
                                ALU.mult).then_inc(pool_step, 1)
                            pool.wait_ge(pool_step, base + s + 1)
                            if s == 0:
                                nc.gpsimd.tensor_tensor(attn[:, t, :], prod_pool[:, 0, :], prod_pool[:, 1, :],
                                                        ALU.add).then_inc(pool_step, 1)
                            else:
                                nc.gpsimd.tensor_tensor(prod_pool[:, 0, :], prod_pool[:, 0, :],
                                                        prod_pool[:, 1, :], ALU.add).then_inc(pool_step, 1)
                        pool.wait_ge(pool_step, base + 4)
                        nc.gpsimd.tensor_tensor(attn[:, t, :], attn[:, t, :], prod_pool[:, 0, :],
                                                ALU.add).then_inc(attn_pool, 1)
                        pool.wait_ge(attn_pool, 2 * a + t - 1)
                if has(j, 1):
                    if isinstance(j, int):
                        wait(pool, x1_out[1 - p], 16 * ((j + 1) // 2))
                    else:
                        wait(pool, x1_out[1 - p], 8 * (j + 1 - (1 - p)))
                    wait(pool, x_in_sem, 16 * (j + 2))
                    for t in range(R):
                        last = nc.gpsimd.tensor_tensor(xres[1 - p][:, t, :], x[:, t, :], bout[:, :], ALU.add)
                    last.then_inc(res_done, 1)

            nc.gpsimd.memset(half[:, :], -0.5).then_inc(half_set, 1)
            pool.wait_ge(half_set, 1)
            run_steps(pool, step, TILES)

        @block.tensor
        def _(pe):
            def products(j, p, groups):
                for g in groups:
                    c, t = g // R, g % R
                    wait(pe, qkv_sb, N_QKV * j + g - 3)
                    n = 0
                    for k in range(DK):
                        for a, b in PASSES:
                            last = nc.tensor.matmul(qb[g % 4][:, :], xT[p][a][:, k, t * P:(t + 1) * P],
                                                    wqkv[b][:, k, c * D:(c + 1) * D],
                                                    start=(n == 0), stop=(n == 11))
                            n += 1
                    last.then_inc(qkv_psum, 1)

            def step(j, p):
                if has(j):
                    wait(pe, xt_lo, R * (j + 1))
                    products(j, p, range(2 * R))
                if has(j, -1):
                    a_ = j - 1
                    for t in range(R):
                        if t < 2:
                            wait(pe, attn_dve, 2 * a_ + t + 1)
                            if has(j):
                                wait(pe, xt_lo, R * j + t + 3)
                            else:
                                wait(pe, at_lo, R * (a_ - 1) + t + 3)
                        else:
                            wait(pe, attn_pool, 2 * a_ + t - 1)
                            wait(pe, at_lo, R * a_ + t - 1)
                        for k in range(DK):
                            last = nc.tensor.transpose(tb[t % 2][:, k * P:(k + 1) * P],
                                                       attn[:, t, k * P:(k + 1) * P], ident[:, :])
                        last.then_inc(at_psum, 1)
                        if t >= 1:
                            output_projection(a_, t - 1)
                    output_projection(a_, 3)
                if has(j, 1):
                    for t in range(R):
                        if t >= 2:
                            wait(pe, xt_lo, R * (j + 1) + t - 1)
                        elif has(j, -1):
                            wait(pe, at_lo, R * (j - 1) + t + 3)
                        else:
                            wait(pe, xt_lo, R * j + t + 3)
                        wait(pe, xn_done, R * (j + 1) + t + 1)
                        for k in range(DK):
                            last = nc.tensor.transpose(tb[t % 2][:, k * P:(k + 1) * P],
                                                       xn[:, t, k * P:(k + 1) * P], ident[:, :])
                        last.then_inc(xt_psum, 1)
                if has(j):
                    products(j, p, range(2 * R, 3 * R))

            def output_projection(a_, t):
                wait(pe, at_lo, R * a_ + t + 1)
                wait(pe, x1_done, R * a_ + t - 1)
                n = 0
                for k in range(DK):
                    for a, b in PASSES:
                        last = nc.tensor.matmul(ob[t % 2][:, :], aT[t % 2][a][:, k, :],
                                                wout[b][:, k, :], start=(n == 0), stop=(n == 11))
                        n += 1
                last.then_inc(out_psum, 1)

            run_steps(pe, step, TILES)

        @block.scalar
        def _(act):
            def step(j, p):
                if has(j, -1):
                    a = j - 1
                    wait(act, sub_done, a + 1)
                    nc.scalar.activation(prob[:, :, :, :], prob[:, :, :, :], ACT.Exp).then_inc(exp_done, 1)
                if has(j, 1):
                    wait(act, nmr_done, j + 2)
                    wait(act, rstd_done, j + 2)
                    wait(act, x_in_sem, 16 * (j + 2))
                    wait(act, xt_psum, R * (j + 1))
                    for t in range(R):
                        nc.scalar.activation(xn[:, t, :], x[:, t, :], ACT.Identity, bias=nmr[:, t:t + 1],
                                             scale=rstd[:, t:t + 1]).then_inc(xn_done, 1)
                if has(j, -1):
                    for t in range(R):
                        wait(act, at_psum, R * a + t + 1)
                        wait(act, out_psum, R * a + t - 1)
                        nc.scalar.activation(aT[t % 2][0][:, :, :].rearrange("p k n -> p (k n)"),
                                             tb[t % 2][:, :], ACT.Copy).then_inc(at_hi, 1)
                if has(j, 1):
                    for t in range(R):
                        if t == 0:
                            wait(act, qkv_psum, N_QKV * j)
                        wait(act, xt_psum, R * (j + 1) + t + 1)
                        nc.scalar.activation(xT[1 - p][0][:, :, t * P:(t + 1) * P], tb[t % 2][:, :],
                                             ACT.Copy).then_inc(xt_hi, 1)

            run_steps(act, step, TILES)

        @block.vector
        def _(dve):
            nc.vector.memset(logit[:, :, :, :], CAUSAL_FILL).then_inc(consts, 1)
            dve.wait_ge(consts, 1)

            def take_qkv(j, p, g):
                if not has(j):
                    return
                c, t = g // R, g % R
                wait(dve, qkv_psum, N_QKV * j + g + 1)
                if g == 0:
                    wait(dve, qk_sum, R * (j - 1))
                if g == 2 * R:
                    wait(dve, attn_pool, 2 * j)
                    wait(dve, attn_dve, 2 * j)
                dst = v[:, t, :] if c == 2 else qk[p][:, c, t, :]
                if c == 0:
                    nc.vector.scalar_tensor_tensor(out=dst, in0=qb[g % 4][:, :], scalar=SCALE, in1=bqkv[:, 0:D],
                                                   op0=ALU.mult, op1=ALU.add).then_inc(qkv_sb, 1)
                else:
                    nc.vector.tensor_tensor(dst, qb[g % 4][:, :], bqkv[:, c * D:(c + 1) * D],
                                            ALU.add).then_inc(qkv_sb, 1)

            def scores(a, p, t):
                if not has(a):
                    return
                n = t + 1
                wait(dve, qkv_sb, N_QKV * a + 2 * R)
                wait(dve, qk_sum, R * a + t)
                wait(dve, attn_dve, 2 * a)
                nc.vector.tensor_tensor(prod[:, 0:n, :], qk[p][:, 1, 0:n, :],
                                        qk[p][:, 0, t:t + 1, :].to_broadcast([P, n, D]), ALU.mult).then_inc(qk_mul, 1)
                wait(dve, qk_mul, R * a + t + 1)
                nc.vector.tensor_reduce(logit[:, t, 0:n, :].rearrange("p s h -> p (s h)"),
                                        prod[:, 0:n, :].rearrange("p s (h d) -> p (s h) d", d=DH),
                                        AX.X, ALU.add).then_inc(qk_sum, 1)

            def step(j, p):
                a = j - 1

                def softmax_top():
                    if not has(j, -1):
                        return
                    wait(dve, qk_sum, R * (a + 1))
                    nc.vector.tensor_reduce(top[:, :, :], logit[:, :, :, :].rearrange("p t s h -> p t h s"),
                                            AX.X, ALU.max).then_inc(top_done, 1)
                    wait(dve, top_done, a + 1)
                    wait(dve, attn_pool, 2 * a)
                    for t in range(R):
                        last = nc.vector.tensor_tensor(prob[:, t, :, :], logit[:, t, :, :],
                                                       top[:, t:t + 1, :].to_broadcast([P, R, H]), ALU.subtract)
                    last.then_inc(sub_done, 1)

                def softmax_norm():
                    if not has(j, -1):
                        return
                    wait(dve, exp_done, a + 1)
                    nc.vector.tensor_reduce(total[:, :, :], prob[:, :, :, :].rearrange("p t s h -> p t h s"),
                                            AX.X, ALU.add).then_inc(tot_done, 1)
                    wait(dve, tot_done, a + 1)
                    nc.vector.reciprocal(total[:, :, :], total[:, :, :]).then_inc(rcp_done, 1)
                    wait(dve, rcp_done, a + 1)
                    for t in range(R):
                        last = nc.vector.tensor_tensor(prob[:, t, :, :], prob[:, t, :, :],
                                                       total[:, t:t + 1, :].to_broadcast([P, R, H]), ALU.mult)
                    last.then_inc(prob_done, 1)

                def weigh_mul(t):
                    if not has(j, -1):
                        return
                    wait(dve, prob_done, a + 1)
                    wait(dve, qkv_sb, N_QKV * (a + 1))
                    wait(dve, attn_dve, 2 * a + t)
                    nc.vector.tensor_tensor(prod[:, :, :].rearrange("p s (h d) -> p (s h) d", d=DH),
                                            v[:, :, :].rearrange("p s (h d) -> p (s h) d", d=DH),
                                            bcast(prob[:, t, :, :].rearrange("p s h -> p (s h)"), DH),
                                            ALU.mult).then_inc(pv_mul, 1)

                def weigh_sum(t):
                    if not has(j, -1):
                        return
                    wait(dve, pv_mul, 2 * a + t + 1)
                    nc.vector.tensor_tensor(prod[:, 0:2, :], prod[:, 0:2, :], prod[:, 2:4, :],
                                            ALU.add).then_inc(pv_half, 1)
                    wait(dve, pv_half, 2 * a + t + 1)
                    wait(dve, at_psum, R * (a - 1) + t + 1)
                    nc.vector.tensor_tensor(attn[:, t, :], prod[:, 0, :], prod[:, 1, :],
                                            ALU.add).then_inc(attn_dve, 1)

                def take_x1(t):
                    wait(dve, out_psum, R * a + t + 1)
                    wait(dve, res_done, a + 1)
                    nc.vector.tensor_tensor(xres[1 - p][:, t, :], ob[t % 2][:, :], xres[1 - p][:, t, :],
                                            ALU.add).then_inc(x1_done, 1)

                take_qkv(j, p, 0)
                scores(a, 1 - p, 3)
                take_qkv(j, p, 1)
                softmax_top()
                take_qkv(j, p, 2)
                if has(j, 1):
                    wait(dve, x_in_sem, 16 * (j + 2))
                    for t in range(R):
                        last = nc.vector.bn_stats(stats[:, t, :], x[:, t, :])
                    last.then_inc(bn_done, 1)
                    wait(dve, bn_done, j + 2)
                take_qkv(j, p, 3)
                if has(j, 1):
                    for t in range(R):
                        last = nc.vector.bn_aggr(mv[:, t, :], stats[:, t, :])
                    last.then_inc(mv_done, 1)
                    wait(dve, mv_done, j + 2)
                    wait(dve, rstd_done, j + 1)
                    nc.vector.tensor_scalar(vare[:, :], mv[:, :, 1], EPS, None, ALU.add).then_inc(var_done, 1)
                softmax_norm()
                take_qkv(j, p, 4)
                weigh_mul(0)
                take_qkv(j, p, 5)
                weigh_sum(0)
                if has(j, 1):
                    wait(dve, rstd_done, j + 2)
                    wait(dve, xn_done, R * (j + 1))
                    nc.vector.scalar_tensor_tensor(out=nmr[:, :], in0=mv[:, :, 0], scalar=-1.0, in1=rstd[:, :],
                                                   op0=ALU.mult, op1=ALU.mult).then_inc(nmr_done, 1)
                weigh_mul(1)
                take_qkv(j, p, 6)
                weigh_sum(1)
                take_qkv(j, p, 7)
                if has(j, -1):
                    for t in range(R):
                        wait(dve, at_hi, R * a + t + 1)
                        nc.vector.tensor_tensor(aT[t % 2][1][:, :, :].rearrange("p k n -> p (k n)"), tb[t % 2][:, :],
                                                aT[t % 2][0][:, :, :].rearrange("p k n -> p (k n)").bitcast(F32),
                                                ALU.subtract).then_inc(at_lo, 1)
                        if t >= 1:
                            take_x1(t - 1)
                    take_x1(3)
                if has(j, 1):
                    for t in range(R):
                        wait(dve, xt_hi, R * (j + 1) + t + 1)
                        nc.vector.tensor_tensor(xT[1 - p][1][:, :, t * P:(t + 1) * P], tb[t % 2][:, :],
                                                xT[1 - p][0][:, :, t * P:(t + 1) * P].bitcast(F32),
                                                ALU.subtract).then_inc(xt_lo, 1)
                take_qkv(j, p, 8)
                scores(j, p, 0)
                take_qkv(j, p, 9)
                scores(j, p, 1)
                take_qkv(j, p, 10)
                scores(j, p, 2)
                take_qkv(j, p, 11)

            run_steps(dve, step, TILES)


def slot_turns(t):
    turns = [("pv", t), ("wo", t)]
    if t == 3:
        turns += [("s", 0), ("s", 1)]
    turns += [("x2T", t)]
    if t in (1, 2):
        turns += [("xT", 2 * t - 2), ("xT", 2 * t - 1)]
    turns += [("aT", t)]
    if t == 3:
        turns += [("q", m) for m in range(DK)]
    return turns + [("pT", 4 * t + g) for g in range(4)] + [("out", t)]


TURNS = [turn for t in range(R) for turn in slot_turns(t)]
TURNS_OVER = {
    "pv": lambda j, i: 4 * j + i,
    "aT": lambda j, i: 4 * j + i,
    "wo": lambda j, i: 4 * j + i - 1,
    "x2T": lambda j, i: 4 * j + i - 2,
    "pT": lambda j, i: 16 * j + i + 1,
    "xT": lambda j, i: 4 * (j + 1) + i + 1,
    "q": lambda j, i: 4 * (j + 1) + i + 1,
    "s": lambda j, i: 2 * (j - 1) + i + 1,
    "out": lambda j, i: 4 * (j - 2) + i + 1,
}


def active(j, kind, i):
    shift = {"pv": -(i == 0), "aT": -(i == 0), "wo": -(i < 2), "x2T": -(i < 3), "pT": 0,
             "xT": 1, "q": 1, "s": -1, "out": -2}[kind]
    return has(j, shift)


def tile_at(t, lag, parity):
    return (parity, t - lag) if t >= lag else (1 - parity, t - lag + 4)


def bank_of(parity, turn):
    return (TURNS.index(turn) + 2 * parity) % 4


def bank_before(j, turn):
    at = TURNS.index(turn) - 4
    while True:
        step, place = (j, at) if at >= 0 else (j - 1, at + len(TURNS))
        if isinstance(step, int) and step < -1:
            return None
        kind, i = TURNS[place]
        if active(step, kind, i):
            return kind, TURNS_OVER[kind](step, i)
        at -= 4
        if at < -len(TURNS):
            return None


def cross_block(nc, x1_dram, scratch, w_in, b_in, out, keep):
    with ExitStack() as stack:
        def sb(name, shape, dt=F32):
            return stack.enter_context(nc.sbuf_tensor(name, shape, dt))

        def sem(name):
            return stack.enter_context(nc.semaphore(name))

        ident, vscale = keep["ident"], keep["vscale"]
        wq = [sb(f"wq{h}", [P, DK, D], F32R) for h in range(2)]
        wo = [sb(f"wo{h}", [P, DK, D], F32R) for h in range(2)]
        win = [sb(f"win{h}", [P, DK, 2 * M], F32R) for h in range(2)]
        wf = [sb(f"wf{h}", [2 * M, D], F32R) for h in range(2)]
        bo = sb("bo", [P, D])
        bf = sb("bf", [P, D])
        bq = sb("bq", [P, DK])
        bin_ = sb("bin", [P, 1])
        hinge = sb("hinge", [P, 3, PAIRS])
        b2 = sb("b2", [P, 1])
        ones = sb("ones", [P, P], F32R)
        kbd = sb("kbd", [P, 2, DK, 4, C], F32R)
        fill = sb("fillrows", [P, C], F32R)
        v = sb("v_c", [C, 2, 2, D], F16)
        x1 = sb("x1", [P, R, D])
        xr = [sb(f"xr{p}", [P, R, D]) for p in range(2)]
        x2 = [sb(f"x2_{p}", [P, R, D]) for p in range(2)]
        xn = sb("xn_c", [P, 2, D])
        xT = [sb(f"xT_c{h}", [P, DK, 4 * P], F32R) for h in range(2)]
        q = [sb(f"q{h}", [P, DK, 4 * P], F32R) for h in range(2)]
        prob = sb("prob_c", [P, H, C])
        pT = [sb(f"pT{h}", [C, H, P], F16) for h in range(2)]
        attn = sb("attn_c", [P, D])
        aT = [sb(f"aT_c{h}", [P, DK, P], F32R) for h in range(2)]
        xn2 = sb("xn2", [P, D])
        x2T = [sb(f"x2T{h}", [P, DK, 4 * P], F32R) for h in range(2)]
        s_sb = sb("s_sb", [P, 4 * P])
        relu = sb("relu", [P, 2, 4 * P])
        g_sb = sb("g_sb", [P, 4 * P])
        gT = [sb(f"gT{h}", [P, 4 * P], F32R) for h in range(2)]
        ntop = sb("ntop", [P, H])
        total = sb("total_c", [P, 2, H])
        rtotal = sb("rtotal", [P, H])
        half = sb("half_c", [P, R])
        stats, mv, vare, rstd = (sb(f"{n}_c", sh) for n, sh in
                                 (("stats", [P, R, 6]), ("mv", [P, R, 2]), ("vare", [P, R]), ("rstd", [P, R])))
        stats2, mv2, vare2, rstd2 = (sb(f"{n}_2", sh) for n, sh in
                                     (("stats", [P, 6]), ("mv", [P, 2]), ("vare", [P, 1]), ("rstd", [P, 1])))

        sc = [stack.enter_context(nc.psum_tensor(f"sc{m}", [P, 512], F32)) for m in range(4)]
        ring = [stack.enter_context(nc.psum_tensor(f"ring{i}", [P, 512], F32)) for i in range(4)]

        psum = {k: sem(f"psum_{k}") for k in TURNS_OVER}
        taken = {k: sem(f"taken_{k}") for k in TURNS_OVER}
        hi = {k: sem(f"hi_{k}") for k in ("xT", "x2T", "aT", "pT", "q")}
        in_w = [sem(f"in_w{i}") for i in range(4)]
        in_small = sem("in_small")
        w_hi, w_lo = sem("cw_hi"), sem("cw_lo")
        consts, k_zero = sem("c_consts"), sem("k_zero")
        x1_in, ctx_in = sem("c_x1_in"), sem("c_ctx_in")
        k_in, v_in = sem("k_in"), [sem("v_in0"), sem("v_in1")]
        bn_done, mv_done, var_done, rstd_done, xm_done, xn_done, res_done = (
            sem(f"c_{n}") for n in ("bn", "mv", "var", "rstd", "xm", "xn", "res"))
        bn2_done, mv2_done, var2_done, rstd2_done, x2m_done, xn2_done, bf_added = (
            sem(f"c_{n}") for n in ("bn2", "mv2", "var2", "rstd2", "x2m", "xn2", "bf_added"))
        scored, topped, exped, summed = sem("scored"), sem("topped"), sem("exped"), sem("summed")
        relu_done, hinged, g_hi, g_lo = sem("relu_done"), sem("hinged"), sem("g_hi"), sem("g_lo")
        stored = [[sem(f"stored{p}_{t}") for t in range(R)] for p in range(2)]

        blocks = "(k p) n -> p k n"
        pieces = [([(xr[0][:, :, :], w_in["wq"].rearrange(blocks, p=P))], wq, xr[0][:, :, :]),
                  ([(xr[1][:, :, :], w_in["wo"].rearrange(blocks, p=P))], wo, xr[1][:, :, :]),
                  ([(x2[0][:, :, M * z:M * z + M], w_in["win"].rearrange(blocks, p=P)) for z in range(2)],
                   win, x2[0][:, :, 0:2 * M]),
                  ([(x2[1][M * z:M * z + M, 0, :], w_in["wf"]) for z in range(2)], wf, x2[1][:, 0, :])]
        small = [(bo[:, :], b_in["bo"].rearrange("(o n) -> o n", o=1).to_broadcast([P, D])),
                 (bf[:, :], b_in["bf"].rearrange("(o n) -> o n", o=1).to_broadcast([P, D])),
                 (bq[:, :], b_in["bq"]), (bin_[0:M, :], b_in["bin"]), (bin_[M:2 * M, :], b_in["bin"]),
                 (b2[0:M, :], b_in["b2"])]
        small += [(hinge[M * z:M * z + M, n, :], b_in[name][z]) for n, name in enumerate(("w1", "b1", "w2"))
                  for z in range(2)]

        block = stack.enter_context(nc.Block())

        @block.sync
        def _(sp):
            def load_ctx(j, p):
                row = j // 4
                rows = [row * P + DH * h for h in range(4)]
                rows = rows if isinstance(j, int) else [sp.snap(first) for first in rows]
                sp.wait_ge(k_zero, 1)
                wait_each(sp, (scored, 16 * j), (psum["pv"], 4 * (j - 1)))
                for h in range(4):
                    sp.dma_start(kbd[DH * h:DH * h + DH, :, :, h, :].bitcast(F32),
                                 k_flat[bass.ds(rows[h], DH), :, :, :]).then_inc(k_in, 16)
                sp.dma_start(fill[:, :].bitcast(F32), mask_flat[bass.ds(rows[0], P), :]).then_inc(k_in, 16)
                sp.dma_start(v[:, p, :, :], v_flat[bass.ds(rows[0], P), :, :]).then_inc(v_in[p], 16)

            k_flat = scratch["k"].rearrange("r p a m c -> (r p) a m c")
            mask_flat = scratch["mask"].rearrange("r p c -> (r p) c")
            v_flat = scratch["v"].rearrange("r c a n -> (r c) a n")
            x1_flat = x1_dram.rearrange("r s d -> (r s) d")
            out_flat = out.rearrange("r s d -> (r s) d")

            def tokens(first, count):
                first = first if isinstance(first, int) else sp.snap(first)
                return bass.ds(first, count)

            def step(j, p):
                if has(j, 1):
                    at = tokens((j + 1) * (R * P), R * P)
                    wait_each(sp, (xn_done, R * (j + 1)), (res_done, R * (j + 1)))
                    sp.dma_start(x1[:, :, :], x1_flat[at, :].rearrange("(t p) d -> p t d", p=P)).then_inc(x1_in, 16)
                for t in range(R):
                    if has(j, 1) and t == 3:
                        load_ctx(j + 1, 1 - p)
                    if active(j, "out", t):
                        at = tokens((j - 2) * (R * P) + t * P, P)
                        wait(sp, taken["out"], TURNS_OVER["out"](j, t))
                        sp.dma_start(out_flat[at, :], x2[p][:, t, :]).then_inc(stored[p][t], 16)

            for n, (src, _, _) in enumerate(pieces):
                for dst, part in src:
                    sp.dma_start(dst, part).then_inc(in_w[n], 16)
            sp.wait_ge(w_lo, len(pieces))
            run_steps(sp, step, TILES + 1)
            for p in range(2):
                for t in range(R):
                    sp.wait_ge(stored[p][t], 16 * (TILES // 2))

        @block.gpsimd
        def _(pool):
            def step(j, p):
                def norm(i):
                    over = 4 * (j + 1) + i + 1
                    wait(pool, psum["xT"], over - 2)
                    nc.gpsimd.tensor_tensor(xn[:, i % 2, :], x1[:, i, :], mv[:, i, 0:1].to_broadcast([P, D]),
                                            ALU.subtract).then_inc(xm_done, 1)
                    wait(pool, xm_done, over)
                    nc.gpsimd.tensor_tensor(xn[:, i % 2, :], xn[:, i % 2, :], rstd[:, i:i + 1].to_broadcast([P, D]),
                                            ALU.mult).then_inc(xn_done, 1)

                def residual(i):
                    wait(pool, taken["wo"], 4 * (j - 1) + i + 1)
                    nc.gpsimd.tensor_tensor(xr[1 - p][:, i, :], x1[:, i, :], bo[:, :], ALU.add).then_inc(res_done, 1)

                for t in range(R):
                    if active(j, "x2T", t):
                        over = TURNS_OVER["x2T"](j, t)
                        pp, tt = tile_at(t, 3, p)
                        wait(pool, var2_done, over)
                        nc.gpsimd.tensor_tensor(rstd2[:, :], vare2[:, :], half[:, 0:1], ALU.pow).then_inc(rstd2_done, 1)
                        wait(pool, psum["x2T"], over - 1)
                        nc.gpsimd.tensor_tensor(xn2[:, :], x2[pp][:, tt, :], mv2[:, 0:1].to_broadcast([P, D]),
                                                ALU.subtract).then_inc(x2m_done, 1)
                        wait(pool, x2m_done, over)
                        wait(pool, rstd2_done, over)
                        nc.gpsimd.tensor_tensor(xn2[:, :], xn2[:, :], rstd2[:, 0:1].to_broadcast([P, D]),
                                                ALU.mult).then_inc(xn2_done, 1)
                        nc.gpsimd.tensor_tensor(x2[pp][:, tt, :], x2[pp][:, tt, :], bf[:, :],
                                                ALU.add).then_inc(bf_added, 1)
                    if has(j, 1):
                        if t == 0:
                            wait(pool, var_done, j + 2)
                            nc.gpsimd.tensor_tensor(rstd[:, :], vare[:, :], half[:, :], ALU.pow).then_inc(rstd_done, 1)
                            wait(pool, rstd_done, j + 2)
                            wait(pool, x1_in, 16 * (j + 2))
                            norm(0)
                            norm(1)
                        if t == 1:
                            norm(2)
                            norm(3)
                            residual(0)
                        if t == 2:
                            residual(1)
                            residual(2)
                            residual(3)

            nc.gpsimd.memset(half[:, :], -0.5)
            nc.gpsimd.memset(ones[:, :].bitcast(F32), 1.0)
            nc.gpsimd.memset(kbd[:, :, :, :, :].bitcast(F32), 0.0).then_inc(k_zero, 1)
            pool.wait_ge(k_zero, 1)
            pool.wait_ge(in_small, 16 * len(small))
            pool.wait_ge(w_lo, len(pieces))
            run_steps(pool, step, TILES + 1)

        @block.tensor
        def _(pe):
            def bank(j, p, turn):
                before = bank_before(j, turn)
                if before:
                    wait(pe, taken[before[0]], before[1])
                return ring[bank_of(p, turn)]

            def product(dst, terms):
                terms = [(s[a], m[b]) for s, m in terms for a, b in PASSES]
                for n, (s, m) in enumerate(terms):
                    last = nc.tensor.matmul(dst, s, m, start=(n == 0), stop=(n == len(terms) - 1))
                return last

            def transpose_tile(dst, src):
                for k in range(DK):
                    last = nc.tensor.transpose(dst[:, k * P:(k + 1) * P], src[:, k * P:(k + 1) * P], ident[:, :])
                return last

            def step(j, p):
                for t in range(R):
                    cols = slice(t * P, (t + 1) * P)
                    if has(j):
                        if t == 0:
                            wait(pe, taken["q"], 4 * (j + 1))
                            wait(pe, k_in, 80 * (j + 1))
                        for m in range(4):
                            wait(pe, exped, 16 * j + 4 * t + m - 3)
                            for n, (a, b) in enumerate(PASSES):
                                nc.tensor.matmul(sc[m][:, :], q[a][:, m, cols],
                                                 kbd[:, b, m, :, :].rearrange("p h c -> p (h c)"),
                                                 start=(n == 0), stop=False)
                            nc.tensor.matmul(sc[m][:, :], ones[:, :],
                                             fill[:, :].rearrange("p (o c) -> p o c", o=1).to_broadcast([P, 4, C]),
                                             start=False, stop=True).then_inc(scored, 1)
                    if active(j, "pv", t):
                        over = TURNS_OVER["pv"](j, t)
                        pp = p if t > 0 else 1 - p
                        wait(pe, taken["pT"], 4 * over)
                        if t == 1:
                            if isinstance(j, int):
                                pe.wait_ge(v_in[pp], 16 * (j // 2 + 1))
                            else:
                                pe.wait_ge(v_in[pp], 8 * (j - p) + 16)
                        dst = bank(j, p, ("pv", t))
                        for h in range(H):
                            head = slice(h * DH, (h + 1) * DH)
                            for n, (a, b) in enumerate(PASSES):
                                last = nc.tensor.matmul(dst[:, head], pT[a][:, h, :], v[:, pp, b, head],
                                                        start=(n == 0), stop=(n == 2))
                        last.then_inc(psum["pv"], 1)
                    if active(j, "wo", t):
                        wait(pe, taken["aT"], TURNS_OVER["wo"](j, t))
                        dst = bank(j, p, ("wo", t))
                        product(dst[:, :], [([aT[0][:, k, :], aT[1][:, k, :]], [wo[0][:, k, :], wo[1][:, k, :]])
                                            for k in range(DK)]).then_inc(psum["wo"], 1)
                    if t == 3 and active(j, "s", 0):
                        wait(pe, taken["x2T"], 4 * j)
                        for i in range(2):
                            dst = bank(j, p, ("s", i))
                            part = slice(2 * P * i, 2 * P * (i + 1))
                            product(dst[:, 0:2 * P], [([win[0][:, k, :], win[1][:, k, :]],
                                                       [x2T[0][:, k, part], x2T[1][:, k, part]])
                                                      for k in range(DK)]).then_inc(psum["s"], 1)
                    if active(j, "x2T", t):
                        wait(pe, xn2_done, TURNS_OVER["x2T"](j, t))
                        transpose_tile(bank(j, p, ("x2T", t)), xn2).then_inc(psum["x2T"], 1)
                    if t in (1, 2) and has(j, 1):
                        for i in (2 * t - 2, 2 * t - 1):
                            wait(pe, xn_done, 4 * (j + 1) + i + 1)
                            transpose_tile(bank(j, p, ("xT", i)), xn[:, i % 2, :]).then_inc(psum["xT"], 1)
                    if active(j, "aT", t):
                        wait(pe, taken["pv"], TURNS_OVER["pv"](j, t))
                        transpose_tile(bank(j, p, ("aT", t)), attn).then_inc(psum["aT"], 1)
                    if t == 3 and has(j, 1):
                        wait(pe, taken["xT"], 4 * (j + 2))
                        for m in range(DK):
                            dst = bank(j, p, ("q", m))
                            ms = slice(m * P, (m + 1) * P)
                            product(dst[:, :], [([wq[0][:, k, ms], wq[1][:, k, ms]],
                                                 [xT[0][:, k, :], xT[1][:, k, :]])
                                                for k in range(DK)]).then_inc(psum["q"], 1)
                    if has(j):
                        for g in range(4):
                            wait(pe, exped, 16 * j + 4 * t + g + 1)
                            dst = bank(j, p, ("pT", 4 * t + g))
                            for h in range(4):
                                last = nc.tensor.transpose(dst[:, h * P:(h + 1) * P], prob[:, 4 * g + h, :], ident[:, :])
                            last.then_inc(psum["pT"], 1)
                    if active(j, "out", t):
                        if t == 0:
                            wait(pe, g_lo, j - 1)
                        dst = bank(j, p, ("out", t))
                        product(dst[:, :], [([gT[0][:, cols], gT[1][:, cols]],
                                             [wf[0][:, :], wf[1][:, :]])]).then_inc(psum["out"], 1)

            pe.wait_ge(w_lo, len(pieces))
            pe.wait_ge(k_zero, 1)
            run_steps(pe, step, TILES + 1)

        @block.scalar
        def _(act):
            def take_hi(j, p, kind, i, dst, func=ACT.Copy, **kw):
                wait(act, psum[kind], TURNS_OVER[kind](j, i))
                nc.scalar.activation(dst, ring[bank_of(p, (kind, i))][:, :], func, **kw).then_inc(hi[kind], 1)

            def step(j, p):
                def hinges(first, count):
                    if not active(j, "s", 0):
                        return
                    wait(act, taken["s"], 2 * j)
                    for i in range(first, first + count):
                        wait(act, hinged, PAIRS * (j - 1) + i - 1)
                        nc.scalar.activation(relu[:, i % 2, :], s_sb[:, :], ACT.Relu, bias=hinge[:, 1, i:i + 1],
                                             scale=hinge[:, 0, i:i + 1]).then_inc(relu_done, 1)

                for t in range(R):
                    if has(j):
                        for g in range(4):
                            wait(act, topped, 16 * j + 4 * t + g + 1)
                            wait(act, psum["pT"], 16 * j + 4 * t - 3 + g)
                            if g == 0:
                                wait(act, taken["pv"], 4 * j + t - 1)
                            for h in range(4 * g, 4 * g + 4):
                                last = nc.scalar.activation(prob[:, h, :], sc[g][:, (h % 4) * C:(h % 4 + 1) * C],
                                                            ACT.Exp, bias=ntop[:, h:h + 1],
                                                            accum_out=total[:, t % 2, h:h + 1])
                            last.then_inc(exped, 1)
                    if active(j, "x2T", t):
                        if t == 3:
                            wait(act, psum["s"], 2 * j)
                        tok = slice((t + 1) % 4 * P, ((t + 1) % 4 + 1) * P)
                        take_hi(j, p, "x2T", t, x2T[0][:, :, tok])
                    if t in (1, 2) and has(j, 1):
                        for i in (2 * t - 2, 2 * t - 1):
                            if i == 0:
                                wait(act, psum["q"], 4 * (j + 1))
                            take_hi(j, p, "xT", i, xT[0][:, :, i * P:(i + 1) * P])
                    if active(j, "aT", t):
                        wait(act, psum["wo"], TURNS_OVER["wo"](j, t))
                        take_hi(j, p, "aT", t, aT[0][:, :, :])
                    if t == 3:
                        if has(j, 1):
                            wait(act, scored, 16 * (j + 1))
                        for m in range(DK):
                            hinges(2 * m, 2)
                            if has(j, 1):
                                take_hi(j, p, "q", m, q[0][:, m, :], ACT.Identity, bias=bq[:, m:m + 1])
                    if has(j):
                        wait(act, psum["pv"], 4 * j + t)
                        for g in range(4):
                            take_hi(j, p, "pT", 4 * t + g, pT[0][:, 4 * g:4 * g + 4, :])
                    if t == 3 and active(j, "s", 0):
                        wait(act, hinged, PAIRS * j)
                        wait(act, psum["out"], 4 * (j - 1))
                        nc.scalar.activation(gT[0][:, :], g_sb[:, :], ACT.Copy).then_inc(g_hi, 1)

            for dst, src in small:
                act.dma_start(dst, src).then_inc(in_small, 16)
            for n, (loads, (whi, _), staging) in enumerate(pieces):
                act.wait_ge(in_w[n], 16 * len(loads))
                whi = whi[:, :, :] if n < 3 else whi[:, :]
                if n == 1:
                    for k in range(DK):
                        last = nc.scalar.activation(whi[:, k, :], staging[:, k, :], ACT.Copy, scale=vscale[:, k:k + 1])
                else:
                    last = nc.scalar.activation(whi, staging, ACT.Copy)
                last.then_inc(w_hi, 1)
            act.wait_ge(in_small, 16 * len(small))
            run_steps(act, step, TILES + 1)

        @block.vector
        def _(dve):
            def take_lo(j, p, kind, i, dst, hi_part):
                wait(dve, hi[kind], TURNS_OVER[kind](j, i))
                src = ring[bank_of(p, (kind, i))][:, :]
                nc.vector.tensor_tensor(dst, src, hi_part, ALU.subtract).then_inc(taken[kind], 1)

            def step(j, p):
                def hinges(first, count):
                    if not active(j, "s", 0):
                        return
                    base = PAIRS * (j - 1)
                    for i in range(first, first + count):
                        wait(dve, relu_done, base + i + 1)
                        wait(dve, hinged, base + i)
                        if i == 0:
                            wait(dve, g_lo, j - 1)
                            nc.vector.tensor_scalar(g_sb[:, :], relu[:, 0, :], hinge[:, 2, 0:1], b2[:, 0:1],
                                                    ALU.mult, ALU.add).then_inc(hinged, 1)
                        else:
                            nc.vector.scalar_tensor_tensor(out=g_sb[:, :], in0=relu[:, i % 2, :],
                                                           scalar=hinge[:, 2, i:i + 1], in1=g_sb[:, :],
                                                           op0=ALU.mult, op1=ALU.add).then_inc(hinged, 1)

                for t in range(R):
                    two, one = active(j, "x2T", t), has(j, 1) and t == 0
                    over2 = TURNS_OVER["x2T"](j, t)
                    pp, tt = tile_at(t, 3, p)

                    def tops(g):
                        if not has(j):
                            return
                        wait(dve, scored, 16 * j + 4 * t + g + 1)
                        if g == 0:
                            wait(dve, exped, 16 * j + 4 * t)
                        nc.vector.tensor_reduce(ntop[:, 4 * g:4 * g + 4], sc[g][:, :].rearrange("p (h c) -> p h c", c=C),
                                                AX.X, ALU.max, negate=True).then_inc(topped, 1)

                    if two:
                        wait(dve, taken["wo"], over2)
                        nc.vector.bn_stats(stats2[:, :], x2[pp][:, tt, :]).then_inc(bn2_done, 1)
                        wait(dve, bn2_done, over2)
                        wait(dve, xn2_done, over2 - 1)
                    tops(0)
                    if two:
                        nc.vector.bn_aggr(mv2[:, :], stats2[:, :]).then_inc(mv2_done, 1)
                        wait(dve, mv2_done, over2)
                        nc.vector.tensor_scalar(vare2[:, :], mv2[:, 1:2], EPS, None, ALU.add).then_inc(var2_done, 1)
                    tops(1)
                    tops(2)
                    if one:
                        wait(dve, x1_in, 16 * (j + 2))
                        for i in range(2):
                            nc.vector.bn_stats(stats[:, i, :], x1[:, i, :])
                    tops(3)
                    if one:
                        for i in range(2, R):
                            last = nc.vector.bn_stats(stats[:, i, :], x1[:, i, :])
                        last.then_inc(bn_done, 1)
                        wait(dve, bn_done, j + 2)
                        wait(dve, xn_done, R * (j + 1))
                    if active(j, "pv", t):
                        over = TURNS_OVER["pv"](j, t)
                        wait(dve, exped, 4 * over)
                        wait(dve, taken["pv"], over - 1)
                        nc.vector.reciprocal(rtotal[:, :], total[:, (t - 1) % 2, :]).then_inc(summed, 1)
                        wait(dve, summed, over)
                        wait(dve, psum["pv"], over)
                        wait(dve, psum["aT"], over - 1)
                        nc.vector.tensor_tensor(attn[:, :].rearrange("p (h d) -> p h d", d=DH),
                                                ring[bank_of(p, ("pv", t))][:, :].rearrange("p (h d) -> p h d", d=DH),
                                                bcast(rtotal[:, :], DH), ALU.mult).then_inc(taken["pv"], 1)
                    if one:
                        for i in range(R):
                            last = nc.vector.bn_aggr(mv[:, i, :], stats[:, i, :])
                        last.then_inc(mv_done, 1)
                        wait(dve, mv_done, j + 2)
                        nc.vector.tensor_scalar(vare[:, :], mv[:, :, 1], EPS, None, ALU.add).then_inc(var_done, 1)
                    if active(j, "wo", t):
                        over = TURNS_OVER["wo"](j, t)
                        pw, tw = tile_at(t, 2, p)
                        wait(dve, psum["wo"], over)
                        wait(dve, res_done, over)
                        if isinstance(j, int):
                            wait(dve, stored[pw][tw], 16 * ((j - (t < 2)) // 2))
                        else:
                            wait(dve, stored[pw][tw], 8 * (j - (t < 2) - pw))
                        nc.vector.tensor_tensor(x2[pw][:, tw, :], ring[bank_of(p, ("wo", t))][:, :], xr[pw][:, tw, :],
                                                ALU.add).then_inc(taken["wo"], 1)
                    if t == 3 and active(j, "s", 0):
                        wait(dve, relu_done, PAIRS * (j - 1))
                        for i in range(2):
                            wait(dve, psum["s"], TURNS_OVER["s"](j, i))
                            nc.vector.tensor_scalar(s_sb[:, 2 * P * i:2 * P * (i + 1)],
                                                    ring[bank_of(p, ("s", i))][:, 0:2 * P], bin_[:, 0:1], None,
                                                    ALU.add).then_inc(taken["s"], 1)
                    if two:
                        tok = slice((t + 1) % 4 * P, ((t + 1) % 4 + 1) * P)
                        take_lo(j, p, "x2T", t, x2T[1][:, :, tok], x2T[0][:, :, tok].bitcast(F32))
                    if t in (1, 2) and has(j, 1):
                        for i in (2 * t - 2, 2 * t - 1):
                            tok = slice(i * P, (i + 1) * P)
                            take_lo(j, p, "xT", i, xT[1][:, :, tok], xT[0][:, :, tok].bitcast(F32))
                    if active(j, "aT", t):
                        take_lo(j, p, "aT", t, aT[1][:, :, :], aT[0][:, :, :].bitcast(F32))
                    if t == 3:
                        for m in range(DK):
                            hinges(2 * m, 1)
                            if has(j, 1):
                                wait(dve, hi["q"], TURNS_OVER["q"](j, m))
                                nc.vector.scalar_tensor_tensor(out=q[1][:, m, :], in0=ring[bank_of(p, ("q", m))][:, :],
                                                               scalar=bq[:, m:m + 1], in1=q[0][:, m, :].bitcast(F32),
                                                               op0=ALU.add, op1=ALU.subtract).then_inc(taken["q"], 1)
                            hinges(2 * m + 1, 1)
                    if has(j):
                        for g in range(4):
                            heads = slice(4 * g, 4 * g + 4)
                            take_lo(j, p, "pT", 4 * t + g, pT[1][:, heads, :], pT[0][:, heads, :])
                    if active(j, "out", t):
                        wait(dve, psum["out"], TURNS_OVER["out"](j, t))
                        if t == 0:
                            wait(dve, bf_added, 4 * (j - 1))
                        nc.vector.tensor_tensor(x2[p][:, t, :], ring[bank_of(p, ("out", t))][:, :], x2[p][:, t, :],
                                                ALU.add).then_inc(taken["out"], 1)
                    if t == 3 and active(j, "s", 0):
                        wait(dve, g_hi, j)
                        nc.vector.tensor_tensor(gT[1][:, :], g_sb[:, :], gT[0][:, :].bitcast(F32),
                                                ALU.subtract).then_inc(g_lo, 1)

            nc.vector.memset(b2[M:2 * M, :], 0.0).then_inc(consts, 1)
            for n, (_, (whi, wlo), staging) in enumerate(pieces):
                dve.wait_ge(w_hi, n + 1)
                whi, wlo = (x[:, :, :] if n < 3 else x[:, :] for x in (whi, wlo))
                if n == 1:
                    for k in range(DK):
                        last = nc.vector.scalar_tensor_tensor(out=wlo[:, k, :], in0=staging[:, k, :],
                                                              scalar=vscale[:, k:k + 1], in1=whi[:, k, :].bitcast(F32),
                                                              op0=ALU.mult, op1=ALU.subtract)
                else:
                    last = nc.vector.tensor_tensor(wlo, staging, whi.bitcast(F32), ALU.subtract)
                last.then_inc(w_lo, 1)
            dve.wait_ge(in_small, 16 * len(small))
            dve.wait_ge(consts, 1)
            run_steps(dve, step, TILES + 1)


def build_program(nc, x, ctx, mask, w, b, out, debug_x1=None):
    x1_dram = debug_x1 if debug_x1 is not None else nc.dram_tensor("x1_scratch", [R, S, D], F32).ap()
    scratch = {"k": nc.dram_tensor("k_scratch", [R, P, 2, DK, C], F32).ap(),
               "v": nc.dram_tensor("v_scratch", [R, C, 2, D], F16).ap(),
               "mask": nc.dram_tensor("mask_scratch", [R, P, C], F32).ap()}
    with ExitStack() as stack:
        def sb(name, shape, dt=F32):
            return stack.enter_context(nc.sbuf_tensor(name, shape, dt))

        keep = {"ident": sb("ident", [P, P]), "vscale": sb("vscale", [P, DK])}
        with ExitStack() as stack1:
            def sb1(name, shape, dt=F32):
                return stack1.enter_context(nc.sbuf_tensor(name, shape, dt))

            keep["wqkv"] = [sb1(f"wqkv{h}", [P, DK, 3 * D], F32R) for h in range(2)]
            keep["wout"] = [sb1(f"wout{h}", [P, DK, D], F32R) for h in range(2)]
            keep["bqkv"] = sb1("bqkv", [P, 3 * D])
            keep["bout"] = sb1("bout", [P, D])
            prepare_block(nc, ctx, mask, w, b, scratch, keep)
            self_block(nc, x, x1_dram, keep)
        if debug_x1 is None:
            cross_block(nc, x1_dram, scratch, w, b, out, keep)


def kernel(**inputs):
    import concourse.bacc as bacc
    from concourse.bass_utils import run_bass_kernel_spmd

    nc = bacc.Bacc("TRN2", target_bir_lowering=False, num_devices=1)
    arrays = {}

    def dram(name, array):
        arrays[name] = np.ascontiguousarray(array)
        return nc.dram_tensor(name, arrays[name].shape, mybir.dt.from_np(arrays[name].dtype),
                              kind="ExternalInput").ap()

    given = {name: np.asarray(a) for name, a in inputs.items()}
    w = {name: dram(f"in_{name}", given[key].T) for name, key in (
        ("wqkv", "L0_attn_qkv_w"), ("wout", "L0_attn_out_w"), ("wq", "L0_xattn_Wq"), ("wk", "L0_xattn_Wk"),
        ("wv", "L0_xattn_Wv"), ("wo", "L0_xattn_Wo"))}
    w["win"] = dram("in_win", given["L0_ffn_Win"])
    w["wf"] = dram("in_wf", given["L0_ffn_Wout"])
    b = {name: dram(f"in_{name}", given[key]) for name, key in (
        ("bqkv", "L0_attn_qkv_b"), ("bout", "L0_attn_out_b"), ("bo", "L0_xattn_bo"), ("bf", "L0_ffn_bout"))}
    for name, key in (("bk", "L0_xattn_bk"), ("bv", "L0_xattn_bv"), ("bq", "L0_xattn_bq")):
        b[name] = dram(f"in_{name}", given[key].reshape(DK, P).T)
    for name, key in (("bin", "L0_ffn_bin_"), ("b2", "L0_ffn_b2")):
        b[name] = dram(f"in_{name}", given[key].reshape(M, 1))
    for name, key in (("w1", "L0_ffn_W1"), ("b1", "L0_ffn_b1"), ("w2", "L0_ffn_W2")):
        b[name] = dram(f"in_{name}", given[key].reshape(M, PAIRS, 2).transpose(2, 0, 1))
    x = dram("in_x", given["x"])
    ctx = dram("in_ctx", given["ctx_1024"])
    mask = dram("in_mask", given["mask_BxS2_bf1"].view(np.uint8))
    out = nc.dram_tensor("out", (R, S, D), F32, kind="ExternalOutput").ap()
    build_program(nc, x, ctx, mask, w, b, out)
    return run_bass_kernel_spmd(nc, [arrays], core_ids=[0]).results[0]["out"]
```

```python
from contextlib import ExitStack

import numpy as np

import concourse.bass as bass
from concourse import mybir

F32 = mybir.dt.float32
F32R = mybir.dt.float32r
F16 = mybir.dt.float16
U8 = mybir.dt.uint8
ALU = mybir.AluOpType
ACT = mybir.ActivationFunctionType
AX = mybir.AxisListType

P = 128
D = 512
DK = D // P
R = 4
S = 2048
H = 16
DH = D // H
C = 128
TILES = S // P
SCALE = DH ** -0.5
EPS = 1e-5
CAUSAL_FILL = -10000.0
MASK_FILL = -100000000.0
MASK_FILL_HI = -99975168.0
MASK_FILL_LO = MASK_FILL - MASK_FILL_HI
M = 64
INNER = 16
PAIRS = INNER // 2
PASSES = ((0, 0), (0, 1), (1, 0))


def wait(eng, sem, count):
    if isinstance(count, int) and count <= 0:
        return
    eng.wait_ge(sem, count)


def wait_each(eng, *pairs):
    pairs = [(sem, count if isinstance(count, int) else eng.snap(count)) for sem, count in pairs]
    for sem, count in pairs:
        wait(eng, sem, count)


def bcast(ap, n):
    return ap.rearrange("p (a b) -> p a b", b=1).to_broadcast([ap.shape[0], ap.shape[1], n])


def run_steps(eng, step, last):
    for j in (-1, 0, 1, 2):
        step(j, j % 2)
    with eng.Fori(0, (TILES - 4) // 2) as i:
        step(2 * i + 3, 1)
        step(2 * i + 4, 0)
    for j in range(TILES - 1, last + 1):
        step(j, j % 2)


def is_step(j, n):
    return isinstance(j, int) and j == n


def has(j, shift=0):
    return not isinstance(j, int) or 0 <= j + shift < TILES


STAGES = 4


def prepare_block(nc, x_in, ctx_in, mask_in, w_in, b_in, scratch, keep):
    with ExitStack() as stack:
        def sb(name, shape, dt=F32):
            return stack.enter_context(nc.sbuf_tensor(name, shape, dt))

        def sem(name):
            return stack.enter_context(nc.semaphore(name))

        ctx = sb("ctx", [P, R, D])
        raw = [sb(f"raw{i}", [P, DK, D]) for i in range(STAGES)]
        wkv = [[sb(f"wkv{i}_{h}", [P, DK, D], F32R) for h in range(2)] for i in range(2)]
        ctxT = [sb(f"ctxT{h}", [P, DK, R * C], F32R) for h in range(2)]
        kvT = sb("kvT", [P, DK, R * C])
        khi = sb("khi", [P, DK, R * C], F32R)
        klo = sb("klo", [P, DK, R * C], F32R)
        vparts = sb("vparts", [P, R, 2, D], F16)
        mask8 = sb("mask8", [P, R * C], U8)
        mask = sb("mask", [P, R * C])
        bkv = sb("bkv", [P, 2, DK])
        rvs = sb("rvs", [P, DK])
        fill = sb("fill", [P, 1])
        maskfill = sb("maskfill", [P, R * C], F32R)
        ps = [stack.enter_context(nc.psum_tensor(f"pp{i}", [P, 512], F32)) for i in range(4)]
        pv = [stack.enter_context(nc.psum_tensor(f"pvt{i}", [P, 512], F32)) for i in range(R)]

        in_ctx, in_mask, in_bkv, in_bias = sem("in_ctx"), sem("in_mask"), sem("in_bkv"), sem("in_bias")
        in_raw = [sem(f"in_raw{i}") for i in range(STAGES)]
        zeroed, ident_ready = sem("zeroed"), sem("ident_ready")
        w_hi, w_lo = sem("w_hi"), sem("w_lo")
        trans, t_hi, t_lo = sem("trans"), sem("t_hi"), sem("t_lo")
        kvt_done, kvt_sb = sem("kvt_done"), sem("kvt_sb")
        k_masked, k_hi, k_lo = sem("k_masked"), sem("k_hi"), sem("k_lo")
        bk_scaled, mask_f, mask_inv, fill_ready, mask_rows = (
            sem("bk_scaled"), sem("mask_f"), sem("mask_inv"), sem("fill_ready"), sem("mask_rows"))
        v_max, v_rcp, v_unit = sem("v_max"), sem("v_rcp"), sem("v_unit")
        v_trans, v_h, v_l = sem("v_trans"), sem("v_h"), sem("v_l")
        kv_out, bias_ready = sem("kv_out"), sem("bias_ready")

        ident, wqkv, wout = keep["ident"], keep["wqkv"], keep["wout"]
        bqkv, bout, vscale = keep["bqkv"], keep["bout"], keep["vscale"]
        k_dram, v_dram = scratch["k"], scratch["v"]

        pieces = ([(w_in["wk"], wkv[0][0][:, :, :], wkv[0][1][:, :, :]),
                   (w_in["wv"], wkv[1][0][:, :, :], wkv[1][1][:, :, :])]
                  + [(w_in["wqkv"][:, c * D:(c + 1) * D], wqkv[0][:, :, c * D:(c + 1) * D],
                      wqkv[1][:, :, c * D:(c + 1) * D]) for c in range(3)]
                  + [(w_in["wout"], wout[0][:, :, :], wout[1][:, :, :])])

        block = stack.enter_context(nc.Block())

        @block.sync
        def _(sp):
            sp.dma_start(ctx[:, :, :], ctx_in.rearrange("b c d -> c b d")).then_inc(in_ctx, 16)
            for n, (src, _, _) in enumerate(pieces):
                wait(sp, w_lo, n - STAGES + 1)
                sp.dma_start(raw[n % STAGES][:, :, :],
                             src.rearrange("(k p) n -> p k n", p=P)).then_inc(in_raw[n % STAGES], 16)
            sp.dma_start(keep["x_tile"][:, :, :],
                         x_in[:, 0:P, :].rearrange("t p d -> p t d")).then_inc(keep["x_in"], 16)
            sp.wait_ge(k_lo, DK)
            for r in range(R):
                cols = slice(r * C, (r + 1) * C)
                sp.dma_start(k_dram[r, :, 0, :, :], khi[:, :, cols].bitcast(F32)).then_inc(kv_out, 16)
                sp.dma_start(k_dram[r, :, 1, :, :], klo[:, :, cols].bitcast(F32)).then_inc(kv_out, 16)
            sp.wait_ge(mask_rows, 1)
            sp.dma_start(scratch["mask"].rearrange("r p c -> p r c"),
                         maskfill[:, :].rearrange("p (r c) -> p r c", c=C).bitcast(F32)).then_inc(kv_out, 16)
            sp.wait_ge(v_l, R)
            sp.dma_start(v_dram.rearrange("r c a n -> c r (a n)"),
                         vparts[:, :, :, :].rearrange("p r a n -> p r (a n)")).then_inc(kv_out, 16)
            sp.wait_ge(kv_out, 16 * (2 * R + 2))

        @block.gpsimd
        def _(pool):
            nc.gpsimd.memset(ident[:, :], 0.0).then_inc(zeroed, 1)
            pool.wait_ge(zeroed, 1)
            nc.gpsimd.affine_select(out=ident[:, :], in_=ident[:, :], compare_op=ALU.not_equal, fill=1.0,
                                    base=0, pattern=[[-1, P]], channel_multiplier=1).then_inc(ident_ready, 1)

        @block.tensor
        def _(pe):
            pe.wait_ge(ident_ready, 1)
            pe.wait_ge(in_ctx, 16)
            for k in range(DK):
                for r in range(R):
                    last = nc.tensor.transpose(ps[k][:, r * C:(r + 1) * C], ctx[:, r, k * P:(k + 1) * P], ident[:, :])
                last.then_inc(trans, 1)
            pe.wait_ge(t_lo, DK)
            for i in range(2):
                pe.wait_ge(w_lo, i + 1)
                for m in range(DK):
                    wait(pe, kvt_sb, DK * (i - 1) + m + 1)
                    n = 0
                    for k in range(DK):
                        for a, b in PASSES:
                            last = nc.tensor.matmul(ps[m][:, :], wkv[i][a][:, k, m * P:(m + 1) * P],
                                                    ctxT[b][:, k, :], start=(n == 0), stop=(n == 11))
                            n += 1
                    last.then_inc(kvt_done, 1)
            for m in range(DK):
                pe.wait_ge(v_unit, m + 1)
                for r in range(R):
                    last = nc.tensor.transpose(pv[r][:, m * P:(m + 1) * P], kvT[:, m, r * C:(r + 1) * C], ident[:, :])
                    if m == DK - 1:
                        last.then_inc(v_trans, 1)

        @block.scalar
        def _(act):
            act.dma_start(mask8[:, :], mask_in.rearrange("b c -> (b c)").rearrange("(o n) -> o n", o=1).to_broadcast([P, R * C])
                          ).then_inc(in_mask, 16)
            for i, name in enumerate(("bk", "bv")):
                act.dma_start(bkv[:, i, :], b_in[name]).then_inc(in_bkv, 16)
            act.dma_start(bqkv[:, :], b_in["bqkv"].rearrange("(o n) -> o n", o=1).to_broadcast([P, 3 * D])
                          ).then_inc(in_bias, 16)
            act.dma_start(bout[:, :], b_in["bout"].rearrange("(o n) -> o n", o=1).to_broadcast([P, D])
                          ).then_inc(in_bias, 16)

            def split_hi(n):
                act.wait_ge(in_raw[n % STAGES], 16 * (n // STAGES + 1))
                nc.scalar.activation(pieces[n][1], raw[n % STAGES][:, :, :], ACT.Copy).then_inc(w_hi, 1)

            for k in range(DK):
                act.wait_ge(trans, k + 1)
                nc.scalar.activation(ctxT[0][:, k, :], ps[k][:, :], ACT.Copy).then_inc(t_hi, 1)
            for n in range(4):
                split_hi(n)
            act.wait_ge(bk_scaled, 1)
            for m in range(DK):
                act.wait_ge(kvt_done, m + 1)
                nc.scalar.activation(kvT[:, m, :], ps[m][:, :], ACT.Identity, bias=bkv[:, 0, m:m + 1],
                                     scale=SCALE).then_inc(kvt_sb, 1)
                if m + 4 < len(pieces):
                    split_hi(m + 4)
            for m in range(DK):
                act.wait_ge(kvt_done, DK + m + 1)
                act.wait_ge(k_lo, m + 1)
                nc.scalar.activation(kvT[:, m, :], ps[m][:, :], ACT.Identity, bias=bkv[:, 1, m:m + 1]
                                     ).then_inc(kvt_sb, 1)
            for r in range(R):
                act.wait_ge(v_trans, r + 1)
                nc.scalar.activation(vparts[:, r, 0, :], pv[r][:, :], ACT.Copy).then_inc(v_h, 1)

        @block.vector
        def _(dve):
            def split_lo(n):
                dve.wait_ge(w_hi, n + 1)
                nc.vector.tensor_tensor(pieces[n][2], raw[n % STAGES][:, :, :], pieces[n][1].bitcast(F32),
                                        ALU.subtract).then_inc(w_lo, 1)

            nc.vector.memset(fill[:, :], 0.0).then_inc(fill_ready, 1)
            dve.wait_ge(fill_ready, 1)
            nc.vector.memset(fill[0:2, :], MASK_FILL_LO).then_inc(fill_ready, 1)
            dve.wait_ge(fill_ready, 2)
            nc.vector.memset(fill[0:1, :], MASK_FILL_HI).then_inc(fill_ready, 1)
            for k in range(DK):
                dve.wait_ge(t_hi, k + 1)
                nc.vector.tensor_tensor(ctxT[1][:, k, :], ps[k][:, :], ctxT[0][:, k, :].bitcast(F32),
                                        ALU.subtract).then_inc(t_lo, 1)
            dve.wait_ge(in_mask, 16)
            nc.vector.tensor_copy(mask[:, :], mask8[:, :]).then_inc(mask_f, 1)
            dve.wait_ge(in_bkv, 32)
            nc.vector.tensor_scalar(bkv[:, 0, :], bkv[:, 0, :], SCALE, None, ALU.mult).then_inc(bk_scaled, 1)
            for n in range(4):
                split_lo(n)
            dve.wait_ge(mask_f, 1)
            for m in range(DK):
                dve.wait_ge(kvt_sb, m + 1)
                nc.vector.tensor_tensor(kvT[:, m, :], kvT[:, m, :], mask[:, :], ALU.mult).then_inc(k_masked, 1)
                dve.wait_ge(k_masked, m + 1)
                nc.vector.tensor_copy(khi[:, m, :], kvT[:, m, :]).then_inc(k_hi, 1)
                dve.wait_ge(k_hi, m + 1)
                nc.vector.tensor_tensor(klo[:, m, :], kvT[:, m, :], khi[:, m, :].bitcast(F32),
                                        ALU.subtract).then_inc(k_lo, 1)
            nc.vector.tensor_scalar(mask[:, :], mask[:, :], -1.0, 1.0, ALU.mult, ALU.add).then_inc(mask_inv, 1)
            dve.wait_ge(mask_inv, 1)
            dve.wait_ge(fill_ready, 3)
            nc.vector.tensor_scalar(maskfill[:, :], mask[:, :], fill[:, 0:1], None, ALU.mult).then_inc(mask_rows, 1)
            dve.wait_ge(in_bias, 32)
            nc.vector.tensor_scalar(bqkv[:, 0:D], bqkv[:, 0:D], SCALE, None, ALU.mult).then_inc(bias_ready, 1)
            for m in range(DK):
                if m + 4 < len(pieces):
                    split_lo(m + 4)
                dve.wait_ge(kvt_sb, DK + m + 1)
                nc.vector.tensor_reduce(vscale[:, m:m + 1], kvT[:, m, :], AX.X, ALU.max,
                                        apply_absolute_value=True).then_inc(v_max, 1)
                dve.wait_ge(v_max, 2 * m + 1)
                nc.vector.tensor_scalar(vscale[:, m:m + 1], vscale[:, m:m + 1], 1e-30, None, ALU.max).then_inc(v_max, 1)
                dve.wait_ge(v_max, 2 * m + 2)
                nc.vector.reciprocal(rvs[:, m:m + 1], vscale[:, m:m + 1]).then_inc(v_rcp, 1)
                dve.wait_ge(v_rcp, m + 1)
                nc.vector.tensor_scalar(kvT[:, m, :], kvT[:, m, :], rvs[:, m:m + 1], None, ALU.mult).then_inc(v_unit, 1)
            for r in range(R):
                dve.wait_ge(v_h, r + 1)
                nc.vector.tensor_tensor(vparts[:, r, 1, :], pv[r][:, :], vparts[:, r, 0, :],
                                        ALU.subtract).then_inc(v_l, 1)


def self_block(nc, x_in, x1_dram, w_in, keep):
    with ExitStack() as stack:
        def sb(name, shape, dt=F32):
            return stack.enter_context(nc.sbuf_tensor(name, shape, dt))

        def sem(name):
            return stack.enter_context(nc.semaphore(name))

        ident, wqkv, wout, bqkv, bout = keep["ident"], keep["wqkv"], keep["wout"], keep["bqkv"], keep["bout"]
        x = [keep["x_tile"], sb("x_tile1", [P, R, D])]
        xres = [sb(f"xres{p}", [P, R, D]) for p in range(2)]
        xn = sb("xn", [P, R, D])
        xT = [[sb(f"xT{p}_{h}", [P, DK, R * P], F32R) for h in range(2)] for p in range(2)]
        xT_raw = sb("xT_raw", [P, 2, DK, P])
        qk = sb("qk", [P, 2, R, D])
        v = sb("v", [P, R, D])
        prod = sb("prod", [P, R, D])
        prod_pool = sb("prod_pool", [P, 2, D])
        attn = sb("attn", [P, R, D])
        aT = [[sb(f"aT{b}_{h}", [P, DK, P], F32R) for h in range(2)] for b in range(2)]
        logit = sb("logit", [P, R, R, H])
        prob = sb("prob", [P, R, R, H])
        top = sb("top", [P, R, H])
        total = sb("total", [P, R, H])
        stats = sb("stats", [P, R, 6])
        mv = sb("mv", [P, R, 2])
        vare = sb("vare", [P, R])
        rstd = sb("rstd", [P, R])
        nmr = sb("nmr", [P, R])
        half = sb("half", [P, R])

        tb = [stack.enter_context(nc.psum_tensor(f"tb{i}", [P, 512], F32)) for i in range(2)]
        qb = [stack.enter_context(nc.psum_tensor(f"qb{i}", [P, 512], F32)) for i in range(4)]
        ob = [stack.enter_context(nc.psum_tensor(f"ob{i}", [P, 512], F32)) for i in range(2)]

        x_in_sem = [keep["x_in"], sem("x_in1")]
        x1_out = [sem(f"x1_out{p}") for p in range(2)]
        consts, fill_set = sem("consts"), sem("fill_set")
        bn_done, mv_done, var_done, rstd_done, nmr_done, xn_done = (
            sem("bn_done"), sem("mv_done"), sem("var_done"), sem("rstd_done"), sem("nmr_done"), sem("xn_done"))
        res_done = sem("res_done")
        xt_psum, xt_hi, xt_raw, xt_lo = sem("xt_psum"), sem("xt_hi"), sem("xt_raw"), sem("xt_lo")
        qkv_psum, qk_sb, v_raw, v_sb = sem("qkv_psum"), sem("qk_sb"), sem("v_raw"), sem("v_sb")
        qk_mul, qk_sum, top_done, sub_done, exp_done, tot_done, rcp_done, prob_done = (
            sem("qk_mul"), sem("qk_sum"), sem("top_done"), sem("sub_done"), sem("exp_done"), sem("tot_done"),
            sem("rcp_done"), sem("prob_done"))
        pv_mul, pv_half, attn_dve = sem("pv_mul"), sem("pv_half"), sem("attn_dve")
        pool_step, attn_pool = sem("pool_step"), sem("attn_pool")
        at_psum, at_hi, at_lo = sem("at_psum"), sem("at_hi"), sem("at_lo")
        out_psum, x1_done = sem("out_psum"), sem("x1_done")

        N_QK, N_QKV = 2 * R, 3 * R

        in_w = [sem(f"in_w{i}") for i in range(4)]
        w_hi, w_lo = sem("cw_hi"), sem("cw_lo")
        blocks = "(k p) n -> p k n"
        stage_win, stage_wf = xn[:, :, 0:2 * M], xn[:, :, 2 * M:2 * M + P]
        pieces = [([(qk[:, 0, :, :], w_in["wq"].rearrange(blocks, p=P))], keep["wq"], qk[:, 0, :, :]),
                  ([(qk[:, 1, :, :], w_in["wo"].rearrange(blocks, p=P))], keep["wo"], qk[:, 1, :, :]),
                  ([(stage_win[:, :, M * z:M * z + M], w_in["win"].rearrange(blocks, p=P)) for z in range(2)],
                   keep["win"], stage_win),
                  ([(stage_wf[M * z:M * z + M, :, :], w_in["wf"].rearrange("m (k n) -> m k n", k=DK))
                    for z in range(2)], keep["wf"], stage_wf)]

        def wait_x(eng, j, p, shift):
            q = (p + shift) % 2
            count = 16 * ((j + shift) // 2 + 1) if isinstance(j, int) else 8 * (j + shift - q) + 16
            eng.wait_ge(x_in_sem[q], count)

        block = stack.enter_context(nc.Block())

        @block.sync
        def _(sp):
            def rows(j):
                return bass.ds(j * P, P) if isinstance(j, int) else bass.ds(sp.snap(j * P), P)

            def step(j, p):
                if has(j, 1) and not is_step(j, -1):
                    at = rows(j + 1)
                    wait_each(sp, (xn_done, R * j), (res_done, j))
                    sp.dma_start(x[1 - p][:, :, :],
                                 x_in[:, at, :].rearrange("t p d -> p t d")).then_inc(x_in_sem[1 - p], 16)
                if is_step(j, TILES):
                    sp.wait_ge(qk_sum, R * TILES)
                    sp.wait_ge(xt_psum, R * TILES)
                    for n, (loads, _, _) in enumerate(pieces):
                        for dst, part in loads:
                            sp.dma_start(dst, part).then_inc(in_w[n], 16)
                    sp.wait_ge(res_done, TILES - 1)
                    for q in range(2):
                        sp.wait_ge(x1_out[q], 16 * ((TILES - 2) // 2))
                    sp.dma_start(x[0][:, :, :],
                                 x1_dram[0, 0:R * P, :].rearrange("(t p) d -> p t d", p=P)).then_inc(keep["x1_in"], 16)
                if has(j, -1):
                    at = rows(j - 1)
                    wait(sp, x1_done, R * j)
                    sp.dma_start(x1_dram[:, at, :].rearrange("t p d -> p t d"),
                                 xres[1 - p][:, :, :]).then_inc(x1_out[1 - p], 16)

            run_steps(sp, step, TILES)
            for p in range(2):
                sp.wait_ge(x1_out[p], 16 * (TILES // 2))

        @block.gpsimd
        def _(pool):
            def weigh(a, t):
                base = 8 * a + 4 * (t - 2)
                wait(pool, prob_done, a + 1)
                wait(pool, v_sb, R * (a + 1))
                wait(pool, at_psum, R * (a - 1) + t + 1)
                for s in (0, 2):
                    wait(pool, pool_step, base + s)
                    nc.gpsimd.tensor_tensor(
                        prod_pool[:, :, :].rearrange("p s (h d) -> p (s h) d", d=DH),
                        v[:, s:s + 2, :].rearrange("p s (h d) -> p (s h) d", d=DH),
                        bcast(prob[:, t, s:s + 2, :].rearrange("p s h -> p (s h)"), DH),
                        ALU.mult).then_inc(pool_step, 1)
                    pool.wait_ge(pool_step, base + s + 1)
                    dst = attn[:, t, :] if s == 0 else prod_pool[:, 0, :]
                    nc.gpsimd.tensor_tensor(dst, prod_pool[:, 0, :], prod_pool[:, 1, :],
                                            ALU.add).then_inc(pool_step, 1)
                pool.wait_ge(pool_step, base + 4)
                nc.gpsimd.tensor_tensor(attn[:, t, :], attn[:, t, :], prod_pool[:, 0, :],
                                        ALU.add).then_inc(attn_pool, 1)
                pool.wait_ge(attn_pool, 2 * a + t - 1)

            def step(j, p):
                def x_lo(t):
                    if not has(j, 1):
                        return
                    tok = slice(t * P, (t + 1) * P)
                    wait(pool, xt_raw, R * (j + 1) + t + 1)
                    nc.gpsimd.tensor_tensor(xT[1 - p][1][:, :, tok], xT_raw[:, t % 2, :, :],
                                            xT[1 - p][0][:, :, tok].bitcast(F32),
                                            ALU.subtract).then_inc(xt_lo, 1)

                def v_bias(t):
                    if not has(j):
                        return
                    wait(pool, v_raw, R * j + t + 1)
                    nc.gpsimd.tensor_tensor(v[:, t, :], v[:, t, :], bqkv[:, 2 * D:3 * D],
                                            ALU.add).then_inc(v_sb, 1)

                if has(j, -1):
                    weigh(j - 1, 2)
                if has(j):
                    if isinstance(j, int):
                        wait(pool, x1_out[p], 16 * (j // 2))
                    else:
                        wait(pool, x1_out[p], 8 * (j - p))
                    wait_x(pool, j, p, 0)
                    for t in range(R):
                        last = nc.gpsimd.tensor_tensor(xres[p][:, t, :], x[p][:, t, :], bout[:, :], ALU.add)
                    last.then_inc(res_done, 1)
                if has(j, -1):
                    weigh(j - 1, 3)
                if has(j, 1):
                    wait(pool, var_done, j + 2)
                    wait(pool, xn_done, R * (j + 1))
                    nc.gpsimd.tensor_tensor(rstd[:, :], vare[:, :], half[:, :], ALU.pow).then_inc(rstd_done, 1)
                x_lo(0)
                v_bias(0)
                v_bias(1)
                x_lo(1)
                v_bias(2)
                x_lo(2)
                x_lo(3)
                v_bias(3)

            nc.gpsimd.memset(half[:, :], -0.5).then_inc(consts, 1)
            pool.wait_ge(consts, 1)
            run_steps(pool, step, TILES)

        @block.tensor
        def _(pe):
            def products(j, p, g):
                if not has(j):
                    return
                c, t = g // R, g % R
                if c == 0:
                    wait(pe, xt_lo, R * j + t + 1)
                    wait(pe, v_raw, R * j + t - 3)
                else:
                    wait(pe, qk_sb, N_QK * j + g - 3)
                n = 0
                for k in range(DK):
                    for a, b in PASSES:
                        last = nc.tensor.matmul(qb[g % 4][:, :], xT[p][a][:, k, t * P:(t + 1) * P],
                                                wqkv[b][:, k, c * D:(c + 1) * D],
                                                start=(n == 0), stop=(n == 11))
                        n += 1
                last.then_inc(qkv_psum, 1)

            def transpose_row(bank, src, t):
                for k in range(DK):
                    last = nc.tensor.transpose(tb[bank][:, k * P:(k + 1) * P], src[:, t, k * P:(k + 1) * P],
                                               ident[:, :])
                return last

            def step(j, p):
                def attn_T(t):
                    if not has(j, -1):
                        return
                    a = j - 1
                    if t < 2:
                        wait(pe, attn_dve, 2 * a + t + 1)
                    else:
                        wait(pe, attn_pool, 2 * a + t - 1)
                    if t < 2 and has(j):
                        wait(pe, xt_raw, R * j + t + 3)
                    elif t < 2:
                        wait(pe, at_lo, R * (a - 1) + t + 3)
                    elif t == 2:
                        wait(pe, at_lo, R * a + 1)
                    elif has(j, 1):
                        wait(pe, xt_raw, R * (j + 1) + 1)
                    else:
                        wait(pe, at_lo, R * a + 2)
                    transpose_row((0, 1, 0, 1)[t], attn, t).then_inc(at_psum, 1)

                def xn_T(t):
                    if not has(j, 1):
                        return
                    wait(pe, xn_done, R * (j + 1) + t + 1)
                    if t == 2:
                        wait(pe, xt_raw, R * (j + 1) + 2)
                    elif has(j, -1):
                        wait(pe, at_lo, R * (j - 1) + (2, 3, 0, 4)[t])
                    elif t == 3:
                        wait(pe, xt_raw, R * (j + 1) + 1)
                    else:
                        wait(pe, xt_raw, R * j + 4 - t)
                    transpose_row((1, 0, 0, 1)[t], xn, t).then_inc(xt_psum, 1)

                for g in range(9):
                    products(j, p, g)
                attn_T(0)
                products(j, p, 9)
                attn_T(1)
                output_projection(j, 0)
                attn_T(2)
                xn_T(0)
                products(j, p, 10)
                xn_T(1)
                output_projection(j, 1)
                attn_T(3)
                products(j, p, 11)
                xn_T(2)
                output_projection(j, 2)
                xn_T(3)
                output_projection(j, 3)

            def output_projection(j, t):
                if not has(j, -1):
                    return
                a_ = j - 1
                wait(pe, at_lo, R * a_ + t + 1)
                wait(pe, x1_done, R * a_ + t - 1)
                n = 0
                for k in range(DK):
                    for a, b in PASSES:
                        last = nc.tensor.matmul(ob[t % 2][:, :], aT[t % 2][a][:, k, :],
                                                wout[b][:, k, :], start=(n == 0), stop=(n == 11))
                        n += 1
                last.then_inc(out_psum, 1)

            run_steps(pe, step, TILES)

        @block.scalar
        def _(act):
            def step(j, p):
                def a_hi(t):
                    if not has(j, -1):
                        return
                    a = j - 1
                    wait(act, at_psum, R * a + t + 1)
                    wait(act, out_psum, R * a + t - 1)
                    nc.scalar.activation(aT[t % 2][0][:, :, :].rearrange("p k n -> p (k n)"),
                                         tb[(0, 1, 0, 1)[t]][:, :], ACT.Copy).then_inc(at_hi, 1)

                def x_hi(t):
                    if not has(j, 1):
                        return
                    tok = slice(t * P, (t + 1) * P)
                    if t == 0:
                        wait(act, qkv_psum, N_QKV * j)
                    wait(act, xt_psum, R * (j + 1) + t + 1)
                    bank = tb[(1, 0, 0, 1)[t]][:, :]
                    nc.scalar.activation(xT[1 - p][0][:, :, tok], bank, ACT.Copy).then_inc(xt_hi, 1)
                    wait(act, xt_lo, R * (j + 1) + t - 1)
                    nc.scalar.activation(xT_raw[:, t % 2, :, :].rearrange("p k n -> p (k n)"), bank,
                                         ACT.Copy).then_inc(xt_raw, 1)

                def take_v(t):
                    if not has(j):
                        return
                    if t == 0:
                        wait(act, attn_pool, 2 * j)
                        wait(act, attn_dve, 2 * j)
                    wait(act, qkv_psum, N_QKV * j + 2 * R + t + 1)
                    nc.scalar.activation(v[:, t, :], qb[t][:, :], ACT.Copy).then_inc(v_raw, 1)

                def split_hi(n):
                    if not is_step(j, TILES):
                        return
                    loads, (whi, _), staging = pieces[n]
                    act.wait_ge(in_w[n], 16 * len(loads))
                    act.wait_ge(qkv_psum, N_QKV * TILES)
                    for k in range(DK):
                        if n == 1:
                            last = nc.scalar.activation(whi[:, k, :], staging[:, k, :], ACT.Copy,
                                                        scale=keep["vscale"][:, k:k + 1])
                        elif k == 0:
                            last = nc.scalar.activation(whi, staging, ACT.Copy)
                    last.then_inc(w_hi, 1)

                a_hi(0)
                split_hi(0)
                split_hi(1)
                if has(j, 1):
                    wait(act, nmr_done, j + 2)
                    wait(act, rstd_done, j + 2)
                    wait_x(act, j, p, 1)
                    wait(act, xt_psum, R * (j + 1))
                    for t in range(R):
                        nc.scalar.activation(xn[:, t, :], x[1 - p][:, t, :], ACT.Identity, bias=nmr[:, t:t + 1],
                                             scale=rstd[:, t:t + 1]).then_inc(xn_done, 1)
                a_hi(1)
                split_hi(2)
                split_hi(3)
                a_hi(2)
                x_hi(0)
                take_v(0)
                take_v(1)
                x_hi(1)
                a_hi(3)
                take_v(2)
                x_hi(2)
                take_v(3)
                x_hi(3)
                if has(j):
                    wait(act, sub_done, j + 1)
                    nc.scalar.activation(prob[:, :, :, :], prob[:, :, :, :], ACT.Exp).then_inc(exp_done, 1)

            run_steps(act, step, TILES)

        @block.vector
        def _(dve):
            def step(j, p):
                a = j - 1

                def take_qk(g):
                    if not has(j):
                        return
                    c, t = g // R, g % R
                    wait(dve, qkv_psum, N_QKV * j + g + 1)
                    if g == 0:
                        wait(dve, qk_sum, R * j)
                    dst = qk[:, c, t, :]
                    if c == 0:
                        nc.vector.scalar_tensor_tensor(out=dst, in0=qb[g % 4][:, :], scalar=SCALE, in1=bqkv[:, 0:D],
                                                       op0=ALU.mult, op1=ALU.add).then_inc(qk_sb, 1)
                    else:
                        nc.vector.tensor_tensor(dst, qb[g % 4][:, :], bqkv[:, c * D:(c + 1) * D],
                                                ALU.add).then_inc(qk_sb, 1)

                def scores(t):
                    if not has(j):
                        return
                    n = t + 1
                    wait(dve, qk_sb, N_QK * j + R + t + 1)
                    wait(dve, qk_sum, R * j + t)
                    wait(dve, attn_dve, 2 * j)
                    nc.vector.tensor_tensor(prod[:, 0:n, :], qk[:, 1, 0:n, :],
                                            qk[:, 0, t:t + 1, :].to_broadcast([P, n, D]), ALU.mult).then_inc(qk_mul, 1)
                    wait(dve, qk_mul, R * j + t + 1)
                    nc.vector.tensor_reduce(logit[:, t, 0:n, :].rearrange("p s h -> p (s h)"),
                                            prod[:, 0:n, :].rearrange("p s (h d) -> p (s h) d", d=DH),
                                            AX.X, ALU.add).then_inc(qk_sum, 1)

                def softmax_top():
                    if not has(j):
                        return
                    wait(dve, qk_sum, R * (j + 1))
                    nc.vector.tensor_reduce(top[:, :, :], logit[:, :, :, :].rearrange("p t s h -> p t h s"),
                                            AX.X, ALU.max).then_inc(top_done, 1)
                    wait(dve, top_done, j + 1)
                    wait(dve, attn_pool, 2 * j)
                    for t in range(R):
                        last = nc.vector.tensor_tensor(prob[:, t, :, :], logit[:, t, :, :],
                                                       top[:, t:t + 1, :].to_broadcast([P, R, H]), ALU.subtract)
                    last.then_inc(sub_done, 1)

                def softmax_norm():
                    if not has(j, -1):
                        return
                    wait(dve, exp_done, a + 1)
                    nc.vector.tensor_reduce(total[:, :, :], prob[:, :, :, :].rearrange("p t s h -> p t h s"),
                                            AX.X, ALU.add).then_inc(tot_done, 1)
                    wait(dve, tot_done, a + 1)
                    nc.vector.reciprocal(total[:, :, :], total[:, :, :]).then_inc(rcp_done, 1)
                    wait(dve, rcp_done, a + 1)
                    for t in range(R):
                        last = nc.vector.tensor_tensor(prob[:, t, :, :], prob[:, t, :, :],
                                                       total[:, t:t + 1, :].to_broadcast([P, R, H]), ALU.mult)
                    last.then_inc(prob_done, 1)

                def weigh_mul(t):
                    if not has(j, -1):
                        return
                    wait(dve, prob_done, a + 1)
                    wait(dve, v_sb, R * (a + 1))
                    wait(dve, attn_dve, 2 * a + t)
                    nc.vector.tensor_tensor(prod[:, :, :].rearrange("p s (h d) -> p (s h) d", d=DH),
                                            v[:, :, :].rearrange("p s (h d) -> p (s h) d", d=DH),
                                            bcast(prob[:, t, :, :].rearrange("p s h -> p (s h)"), DH),
                                            ALU.mult).then_inc(pv_mul, 1)

                def weigh_sum(t):
                    if not has(j, -1):
                        return
                    wait(dve, pv_mul, 2 * a + t + 1)
                    nc.vector.tensor_tensor(prod[:, 0:2, :], prod[:, 0:2, :], prod[:, 2:4, :],
                                            ALU.add).then_inc(pv_half, 1)
                    wait(dve, pv_half, 2 * a + t + 1)
                    wait(dve, at_psum, R * (a - 1) + t + 1)
                    nc.vector.tensor_tensor(attn[:, t, :], prod[:, 0, :], prod[:, 1, :],
                                            ALU.add).then_inc(attn_dve, 1)

                def a_lo(t):
                    if not has(j, -1):
                        return
                    wait(dve, at_hi, R * a + t + 1)
                    nc.vector.tensor_tensor(aT[t % 2][1][:, :, :].rearrange("p k n -> p (k n)"),
                                            tb[(0, 1, 0, 1)[t]][:, :],
                                            aT[t % 2][0][:, :, :].rearrange("p k n -> p (k n)").bitcast(F32),
                                            ALU.subtract).then_inc(at_lo, 1)

                def take_x1(t):
                    if not has(j, -1):
                        return
                    wait(dve, out_psum, R * a + t + 1)
                    wait(dve, res_done, a + 1)
                    nc.vector.tensor_tensor(xres[1 - p][:, t, :], ob[t % 2][:, :], xres[1 - p][:, t, :],
                                            ALU.add).then_inc(x1_done, 1)

                def split_lo(n):
                    if not is_step(j, TILES):
                        return
                    _, (whi, wlo), staging = pieces[n]
                    dve.wait_ge(w_hi, n + 1)
                    for k in range(DK):
                        if n == 1:
                            last = nc.vector.scalar_tensor_tensor(out=wlo[:, k, :], in0=staging[:, k, :],
                                                                  scalar=keep["vscale"][:, k:k + 1],
                                                                  in1=whi[:, k, :].bitcast(F32),
                                                                  op0=ALU.mult, op1=ALU.subtract)
                        elif k == 0:
                            last = nc.vector.tensor_tensor(wlo, staging, whi.bitcast(F32), ALU.subtract)
                    last.then_inc(w_lo, 1)

                softmax_norm()
                take_qk(0)
                weigh_mul(0)
                take_qk(1)
                weigh_sum(0)
                weigh_mul(1)
                take_qk(2)
                weigh_sum(1)
                take_qk(3)
                if has(j, 1):
                    wait_x(dve, j, p, 1)
                    for t in range(R):
                        last = nc.vector.bn_stats(stats[:, t, :], x[1 - p][:, t, :])
                    last.then_inc(bn_done, 1)
                    wait(dve, bn_done, j + 2)
                take_qk(4)
                if has(j, 1):
                    for t in range(R):
                        last = nc.vector.bn_aggr(mv[:, t, :], stats[:, t, :])
                    last.then_inc(mv_done, 1)
                    wait(dve, mv_done, j + 2)
                    wait(dve, rstd_done, j + 1)
                    nc.vector.tensor_scalar(vare[:, :], mv[:, :, 1], EPS, None, ALU.add).then_inc(var_done, 1)
                take_qk(5)
                scores(0)
                take_qk(6)
                scores(1)
                take_qk(7)
                a_lo(0)
                if has(j, 1):
                    wait(dve, rstd_done, j + 2)
                    wait(dve, xn_done, R * (j + 1))
                    nc.vector.scalar_tensor_tensor(out=nmr[:, :], in0=mv[:, :, 0], scalar=-1.0, in1=rstd[:, :],
                                                   op0=ALU.mult, op1=ALU.mult).then_inc(nmr_done, 1)
                scores(2)
                a_lo(1)
                split_lo(0)
                split_lo(1)
                a_lo(2)
                take_x1(0)
                scores(3)
                softmax_top()
                take_x1(1)
                a_lo(3)
                split_lo(2)
                split_lo(3)
                take_x1(2)
                take_x1(3)

            nc.vector.memset(logit[:, :, :, :], CAUSAL_FILL).then_inc(fill_set, 1)
            dve.wait_ge(fill_set, 1)
            run_steps(dve, step, TILES)


def slot_turns(t):
    turns = [("out", t), ("pv", t)]
    if t in (1, 2):
        turns += [("xT", 2 * t - 2), ("xT", 2 * t - 1)]
    turns += [("wo", t)]
    if t == 3:
        turns += [("s", 0), ("s", 1)]
    turns += [("x2T", t), ("aT", t)]
    if t == 3:
        turns += [("q", m) for m in range(DK)]
    return turns + [("pT", 4 * t + g) for g in range(4)]


TURNS = [turn for t in range(R) for turn in slot_turns(t)]
TURNS_OVER = {
    "pv": lambda j, i: 4 * j + i,
    "aT": lambda j, i: 4 * j + i,
    "wo": lambda j, i: 4 * j + i - 1,
    "x2T": lambda j, i: 4 * j + i - 2,
    "pT": lambda j, i: 16 * j + i + 1,
    "xT": lambda j, i: 4 * (j + 1) + i + 1,
    "q": lambda j, i: 4 * (j + 1) + i + 1,
    "s": lambda j, i: 2 * (j - 1) + i + 1,
    "out": lambda j, i: 4 * (j - 2) + i + 1,
}


HINGE_RUNS = ((0, 3), (3, 2), (5, 2), (7, 1))


def active(j, kind, i):
    shift = {"pv": -(i == 0), "aT": -(i == 0), "wo": -(i < 2), "x2T": -(i < 3), "pT": 0,
             "xT": 1, "q": 1, "s": -1, "out": -2}[kind]
    return has(j, shift)


def tile_at(t, lag, parity):
    return (parity, t - lag) if t >= lag else (1 - parity, t - lag + 4)


def bank_of(parity, turn):
    return (TURNS.index(turn) + 2 * parity) % 4


def bank_before(j, turn):
    at = TURNS.index(turn) - 4
    while True:
        step, place = (j, at) if at >= 0 else (j - 1, at + len(TURNS))
        if isinstance(step, int) and step < -1:
            return None
        kind, i = TURNS[place]
        if active(step, kind, i):
            return kind, TURNS_OVER[kind](step, i)
        at -= 4
        if at < -len(TURNS):
            return None


def cross_block(nc, x1_dram, scratch, w_in, b_in, out, keep):
    with ExitStack() as stack:
        def sb(name, shape, dt=F32):
            return stack.enter_context(nc.sbuf_tensor(name, shape, dt))

        def sem(name):
            return stack.enter_context(nc.semaphore(name))

        ident, vscale = keep["ident"], keep["vscale"]
        wq, wo, win, wf = keep["wq"], keep["wo"], keep["win"], keep["wf"]
        bo = sb("bo", [P, D])
        bf = sb("bf", [P, D])
        bq = sb("bq", [P, DK])
        bin_ = sb("bin", [P, 1])
        hinge = sb("hinge", [P, 3, PAIRS])
        b2 = sb("b2", [P, 1])
        ones = sb("ones", [P, P], F32R)
        kbd = sb("kbd", [P, 2, DK, 4, C], F32R)
        fill = sb("fillrows", [P, C], F32R)
        v = sb("v_c", [C, 2, 2, D], F16)
        x1 = keep["x_tile"]
        xr = [sb(f"xr{p}", [P, R, D]) for p in range(2)]
        x2 = [sb(f"x2_{p}", [P, R, D]) for p in range(2)]
        xn = sb("xn_c", [P, 2, D])
        xT = [sb(f"xT_c{h}", [P, DK, 4 * P], F32R) for h in range(2)]
        q = [sb(f"q{h}", [P, DK, 4 * P], F32R) for h in range(2)]
        prob = sb("prob_c", [P, H, C])
        pT = [sb(f"pT{h}", [C, H, P], F16) for h in range(2)]
        attn = sb("attn_c", [P, D])
        aT = [sb(f"aT_c{h}", [P, DK, P], F32R) for h in range(2)]
        xn2 = sb("xn2", [P, D])
        x2T = [sb(f"x2T{h}", [P, DK, 4 * P], F32R) for h in range(2)]
        s_sb = sb("s_sb", [P, 4 * P])
        relu = sb("relu", [P, 4, 4 * P])
        g_sb = sb("g_sb", [P, 4 * P])
        gT = [sb(f"gT{h}", [P, 4 * P], F32R) for h in range(2)]
        ntop = sb("ntop", [P, H])
        total = sb("total_c", [P, 2, H])
        rtotal = sb("rtotal", [P, H])
        half = sb("half_c", [P, R])
        stats, mv, vare, rstd = (sb(f"{n}_c", sh) for n, sh in
                                 (("stats", [P, R, 6]), ("mv", [P, R, 2]), ("vare", [P, R]), ("rstd", [P, R])))
        stats2, mv2, vare2, rstd2 = (sb(f"{n}_2", sh) for n, sh in
                                     (("stats", [P, 6]), ("mv", [P, 2]), ("vare", [P, 1]), ("rstd", [P, 1])))

        sc = [stack.enter_context(nc.psum_tensor(f"sc{m}", [P, 512], F32)) for m in range(4)]
        ring = [stack.enter_context(nc.psum_tensor(f"ring{i}", [P, 512], F32)) for i in range(4)]

        psum = {k: sem(f"psum_{k}") for k in TURNS_OVER}
        taken = {k: sem(f"taken_{k}") for k in TURNS_OVER}
        hi = {k: sem(f"hi_{k}") for k in ("xT", "x2T", "aT", "pT", "q")}
        in_small = sem("in_small")
        consts, k_zero = sem("c_consts"), sem("k_zero")
        x1_in = keep["x1_in"]
        k_in, v_in = sem("k_in"), [sem("v_in0"), sem("v_in1")]
        bn_done, mv_done, var_done, rstd_done, xm_done, xn_done, res_done = (
            sem(f"c_{n}") for n in ("bn", "mv", "var", "rstd", "xm", "xn", "res"))
        bn2_done, mv2_done, var2_done, rstd2_done, x2m_done, xn2_done, bf_added = (
            sem(f"c_{n}") for n in ("bn2", "mv2", "var2", "rstd2", "x2m", "xn2", "bf_added"))
        scored, topped, exped, summed = sem("scored"), sem("topped"), sem("exped"), sem("summed")
        relu_done, hinged, g_hi, g_lo = sem("relu_done"), sem("hinged"), sem("g_hi"), sem("g_lo")
        stored = [[sem(f"stored{p}_{t}") for t in range(R)] for p in range(2)]

        small = [(bo[:, :], b_in["bo"].rearrange("(o n) -> o n", o=1).to_broadcast([P, D])),
                 (bf[:, :], b_in["bf"].rearrange("(o n) -> o n", o=1).to_broadcast([P, D])),
                 (bq[:, :], b_in["bq"]), (bin_[0:M, :], b_in["bin"]), (bin_[M:2 * M, :], b_in["bin"]),
                 (b2[0:M, :], b_in["b2"])]
        small += [(hinge[M * z:M * z + M, n, :], b_in[name][z]) for n, name in enumerate(("w1", "b1", "w2"))
                  for z in range(2)]

        block = stack.enter_context(nc.Block())

        @block.sync
        def _(sp):
            def load_ctx(j, p):
                row = j // 4
                rows = [row * P + DH * h for h in range(4)]
                rows = rows if isinstance(j, int) else [sp.snap(first) for first in rows]
                sp.wait_ge(k_zero, 1)
                wait_each(sp, (scored, 16 * j), (psum["pv"], 4 * (j - 1)))
                for h in range(4):
                    sp.dma_start(kbd[DH * h:DH * h + DH, :, :, h, :].bitcast(F32),
                                 k_flat[bass.ds(rows[h], DH), :, :, :]).then_inc(k_in, 16)
                sp.dma_start(fill[:, :].bitcast(F32), mask_flat[bass.ds(rows[0], P), :]).then_inc(k_in, 16)
                sp.dma_start(v[:, p, :, :], v_flat[bass.ds(rows[0], P), :, :]).then_inc(v_in[p], 16)

            k_flat = scratch["k"].rearrange("r p a m c -> (r p) a m c")
            mask_flat = scratch["mask"].rearrange("r p c -> (r p) c")
            v_flat = scratch["v"].rearrange("r c a n -> (r c) a n")
            x1_flat = x1_dram.rearrange("r s d -> (r s) d")
            out_flat = out.rearrange("r s d -> (r s) d")

            def tokens(first, count):
                first = first if isinstance(first, int) else sp.snap(first)
                return bass.ds(first, count)

            def store(j, p, t):
                at = tokens((j - 2) * (R * P) + t * P, P)
                wait(sp, taken["out"], TURNS_OVER["out"](j, t))
                sp.dma_start(out_flat[at, :], x2[p][:, t, :]).then_inc(stored[p][t], 16)

            def step(j, p):
                if has(j, 1) and not is_step(j, -1):
                    at = tokens((j + 1) * (R * P), R * P)
                    wait_each(sp, (xn_done, R * (j + 1)), (res_done, R * (j + 1)))
                    sp.dma_start(x1[:, :, :], x1_flat[at, :].rearrange("(t p) d -> p t d", p=P)).then_inc(x1_in, 16)
                if active(j - 1, "out", 3):
                    store(j - 1, 1 - p, 3)
                for t in range(R - 1):
                    if active(j, "out", t):
                        store(j, p, t)
                if has(j, 1):
                    load_ctx(j + 1, 1 - p)

            run_steps(sp, step, TILES + 1)
            store(TILES + 1, 1, 3)
            for p in range(2):
                for t in range(R):
                    sp.wait_ge(stored[p][t], 16 * (TILES // 2))

        @block.gpsimd
        def _(pool):
            def step(j, p):
                def norm(i):
                    over = 4 * (j + 1) + i + 1
                    wait(pool, psum["xT"], over - 2)
                    nc.gpsimd.tensor_tensor(xn[:, i % 2, :], x1[:, i, :], mv[:, i, 0:1].to_broadcast([P, D]),
                                            ALU.subtract).then_inc(xm_done, 1)
                    wait(pool, xm_done, over)
                    nc.gpsimd.tensor_tensor(xn[:, i % 2, :], xn[:, i % 2, :], rstd[:, i:i + 1].to_broadcast([P, D]),
                                            ALU.mult).then_inc(xn_done, 1)

                def residual(i):
                    if is_step(j, -1) and i == 0:
                        pool.wait_ge(in_small, 16 * len(small))
                    wait(pool, taken["wo"], 4 * (j - 1) + i + 1)
                    nc.gpsimd.tensor_tensor(xr[1 - p][:, i, :], x1[:, i, :], bo[:, :], ALU.add).then_inc(res_done, 1)

                for t in range(R):
                    if active(j, "x2T", t):
                        over = TURNS_OVER["x2T"](j, t)
                        pp, tt = tile_at(t, 3, p)
                        wait(pool, var2_done, over)
                        nc.gpsimd.tensor_tensor(rstd2[:, :], vare2[:, :], half[:, 0:1], ALU.pow).then_inc(rstd2_done, 1)
                        wait(pool, psum["x2T"], over - 1)
                        nc.gpsimd.tensor_tensor(xn2[:, :], x2[pp][:, tt, :], mv2[:, 0:1].to_broadcast([P, D]),
                                                ALU.subtract).then_inc(x2m_done, 1)
                        wait(pool, x2m_done, over)
                        wait(pool, rstd2_done, over)
                        nc.gpsimd.tensor_tensor(xn2[:, :], xn2[:, :], rstd2[:, 0:1].to_broadcast([P, D]),
                                                ALU.mult).then_inc(xn2_done, 1)
                        nc.gpsimd.tensor_tensor(x2[pp][:, tt, :], x2[pp][:, tt, :], bf[:, :],
                                                ALU.add).then_inc(bf_added, 1)
                    if has(j, 1):
                        if t < 2:
                            part = slice(2 * t, 2 * t + 2)
                            wait(pool, var_done, 2 * (j + 1) + t + 1)
                            nc.gpsimd.tensor_tensor(rstd[:, part], vare[:, part], half[:, part],
                                                    ALU.pow).then_inc(rstd_done, 1)
                            wait(pool, rstd_done, 2 * (j + 1) + t + 1)
                            wait(pool, x1_in, 16 * (j + 2))
                            norm(2 * t)
                            norm(2 * t + 1)
                        if t == 1:
                            residual(0)
                        if t == 2:
                            residual(1)
                            residual(2)
                            residual(3)

            nc.gpsimd.memset(half[:, :], -0.5)
            nc.gpsimd.memset(ones[:, :].bitcast(F32), 1.0)
            nc.gpsimd.memset(kbd[:, :, :, :, :].bitcast(F32), 0.0).then_inc(k_zero, 1)
            pool.wait_ge(k_zero, 1)
            run_steps(pool, step, TILES + 1)

        @block.tensor
        def _(pe):
            def bank(j, p, turn):
                before = bank_before(j, turn)
                if before:
                    wait(pe, taken[before[0]], before[1])
                return ring[bank_of(p, turn)]

            def product(dst, terms):
                terms = [(s[a], m[b]) for s, m in terms for a, b in PASSES]
                for n, (s, m) in enumerate(terms):
                    last = nc.tensor.matmul(dst, s, m, start=(n == 0), stop=(n == len(terms) - 1))
                return last

            def transpose_tile(dst, src):
                for k in range(DK):
                    last = nc.tensor.transpose(dst[:, k * P:(k + 1) * P], src[:, k * P:(k + 1) * P], ident[:, :])
                return last

            def step(j, p):
                for t in range(R):
                    cols = slice(t * P, (t + 1) * P)
                    if has(j):
                        if t == 0:
                            wait(pe, taken["q"], 4 * (j + 1))
                            wait(pe, k_in, 80 * (j + 1))
                        for m in range(4):
                            wait(pe, exped, 16 * j + 4 * t + m - 3)
                            for n, (a, b) in enumerate(PASSES):
                                nc.tensor.matmul(sc[m][:, :], q[a][:, m, cols],
                                                 kbd[:, b, m, :, :].rearrange("p h c -> p (h c)"),
                                                 start=(n == 0), stop=False)
                            nc.tensor.matmul(sc[m][:, :], ones[:, :],
                                             fill[:, :].rearrange("p (o c) -> p o c", o=1).to_broadcast([P, 4, C]),
                                             start=False, stop=True).then_inc(scored, 1)
                    if active(j, "out", t):
                        if t == 0:
                            wait(pe, g_lo, j - 1)
                        dst = bank(j, p, ("out", t))
                        product(dst[:, :], [([gT[0][:, cols], gT[1][:, cols]],
                                             [wf[0][:, :, :], wf[1][:, :, :]])]).then_inc(psum["out"], 1)
                    if active(j, "pv", t):
                        over = TURNS_OVER["pv"](j, t)
                        pp = p if t > 0 else 1 - p
                        wait(pe, taken["pT"], 4 * over)
                        if t == 1:
                            if isinstance(j, int):
                                pe.wait_ge(v_in[pp], 16 * (j // 2 + 1))
                            else:
                                pe.wait_ge(v_in[pp], 8 * (j - p) + 16)
                        dst = bank(j, p, ("pv", t))
                        for h in range(H):
                            head = slice(h * DH, (h + 1) * DH)
                            for n, (a, b) in enumerate(PASSES):
                                last = nc.tensor.matmul(dst[:, head], pT[a][:, h, :], v[:, pp, b, head],
                                                        start=(n == 0), stop=(n == 2))
                        last.then_inc(psum["pv"], 1)
                    if t in (1, 2) and has(j, 1):
                        for i in (2 * t - 2, 2 * t - 1):
                            wait(pe, xn_done, 4 * (j + 1) + i + 1)
                            transpose_tile(bank(j, p, ("xT", i)), xn[:, i % 2, :]).then_inc(psum["xT"], 1)
                    if active(j, "wo", t):
                        wait(pe, taken["aT"], TURNS_OVER["wo"](j, t))
                        dst = bank(j, p, ("wo", t))
                        product(dst[:, :], [([aT[0][:, k, :], aT[1][:, k, :]], [wo[0][:, k, :], wo[1][:, k, :]])
                                            for k in range(DK)]).then_inc(psum["wo"], 1)
                    if t == 3 and active(j, "s", 0):
                        wait(pe, taken["x2T"], 4 * j)
                        for i in range(2):
                            dst = bank(j, p, ("s", i))
                            part = slice(2 * P * i, 2 * P * (i + 1))
                            product(dst[:, 0:2 * P], [([win[0][:, k, :], win[1][:, k, :]],
                                                       [x2T[0][:, k, part], x2T[1][:, k, part]])
                                                      for k in range(DK)]).then_inc(psum["s"], 1)
                    if active(j, "x2T", t):
                        wait(pe, xn2_done, TURNS_OVER["x2T"](j, t))
                        transpose_tile(bank(j, p, ("x2T", t)), xn2).then_inc(psum["x2T"], 1)
                    if active(j, "aT", t):
                        wait(pe, taken["pv"], TURNS_OVER["pv"](j, t))
                        transpose_tile(bank(j, p, ("aT", t)), attn).then_inc(psum["aT"], 1)
                    if t == 3 and has(j, 1):
                        wait(pe, taken["xT"], 4 * (j + 2))
                        for m in range(DK):
                            dst = bank(j, p, ("q", m))
                            ms = slice(m * P, (m + 1) * P)
                            product(dst[:, :], [([wq[0][:, k, ms], wq[1][:, k, ms]],
                                                 [xT[0][:, k, :], xT[1][:, k, :]])
                                                for k in range(DK)]).then_inc(psum["q"], 1)
                    if has(j):
                        for g in range(4):
                            wait(pe, exped, 16 * j + 4 * t + g + 1)
                            dst = bank(j, p, ("pT", 4 * t + g))
                            for h in range(4):
                                last = nc.tensor.transpose(dst[:, h * P:(h + 1) * P], prob[:, 4 * g + h, :], ident[:, :])
                            last.then_inc(psum["pT"], 1)

            pe.wait_ge(k_zero, 1)
            run_steps(pe, step, TILES + 1)

        @block.scalar
        def _(act):
            def take_hi(j, p, kind, i, dst, func=ACT.Copy, **kw):
                wait(act, psum[kind], TURNS_OVER[kind](j, i))
                nc.scalar.activation(dst, ring[bank_of(p, (kind, i))][:, :], func, **kw).then_inc(hi[kind], 1)

            def step(j, p):
                def hinges(first, count):
                    if not active(j, "s", 0):
                        return
                    wait(act, taken["s"], 2 * j)
                    for i in range(first, first + count):
                        wait(act, hinged, PAIRS * (j - 1) + i - 3)
                        nc.scalar.activation(relu[:, i % 4, :], s_sb[:, :], ACT.Relu, bias=hinge[:, 1, i:i + 1],
                                             scale=hinge[:, 0, i:i + 1]).then_inc(relu_done, 1)

                for t in range(R):
                    for g in range(4):
                        if g == 3 and t in (1, 2) and has(j, 1):
                            for i in (2 * t - 2, 2 * t - 1):
                                if i == 0:
                                    wait(act, psum["q"], 4 * (j + 1))
                                take_hi(j, p, "xT", i, xT[0][:, :, i * P:(i + 1) * P])
                        if has(j):
                            wait(act, topped, 16 * j + 4 * t + g + 1)
                            wait(act, psum["pT"], 16 * j + 4 * t - 3 + g)
                            if g == 0:
                                wait(act, taken["pv"], 4 * j + t - 1)
                            for h in range(4 * g, 4 * g + 4):
                                last = nc.scalar.activation(prob[:, h, :], sc[g][:, (h % 4) * C:(h % 4 + 1) * C],
                                                            ACT.Exp, bias=ntop[:, h:h + 1],
                                                            accum_out=total[:, t % 2, h:h + 1])
                            last.then_inc(exped, 1)
                    if active(j, "x2T", t):
                        if t == 3:
                            wait(act, psum["s"], 2 * j)
                        tok = slice((t + 1) % 4 * P, ((t + 1) % 4 + 1) * P)
                        take_hi(j, p, "x2T", t, x2T[0][:, :, tok])
                    if active(j, "aT", t):
                        wait(act, psum["wo"], TURNS_OVER["wo"](j, t))
                        take_hi(j, p, "aT", t, aT[0][:, :, :])
                    if t == 3:
                        if is_step(j, -1):
                            act.wait_ge(in_small, 16 * len(small))
                        if has(j, 1):
                            wait(act, scored, 16 * (j + 1))
                        for m in range(DK):
                            hinges(*HINGE_RUNS[m])
                            if has(j, 1):
                                take_hi(j, p, "q", m, q[0][:, m, :], ACT.Identity, bias=bq[:, m:m + 1])
                    if has(j):
                        wait(act, psum["pv"], 4 * j + t)
                        for g in range(4):
                            take_hi(j, p, "pT", 4 * t + g, pT[0][:, 4 * g:4 * g + 4, :])
                    if t == 3 and active(j, "s", 0):
                        wait(act, hinged, PAIRS * j)
                        wait(act, psum["out"], 4 * (j - 1))
                        nc.scalar.activation(gT[0][:, :], g_sb[:, :], ACT.Copy).then_inc(g_hi, 1)

            for dst, src in small:
                act.dma_start(dst, src).then_inc(in_small, 16)
            run_steps(act, step, TILES + 1)

        @block.vector
        def _(dve):
            def take_lo(j, p, kind, i, dst, hi_part):
                wait(dve, hi[kind], TURNS_OVER[kind](j, i))
                src = ring[bank_of(p, (kind, i))][:, :]
                nc.vector.tensor_tensor(dst, src, hi_part, ALU.subtract).then_inc(taken[kind], 1)

            def step(j, p):
                def hinges(first, count):
                    if not active(j, "s", 0):
                        return
                    base = PAIRS * (j - 1)
                    for i in range(first, first + count):
                        wait(dve, relu_done, base + i + 1)
                        wait(dve, hinged, base + i)
                        if i == 0:
                            wait(dve, g_lo, j - 1)
                            nc.vector.tensor_scalar(g_sb[:, :], relu[:, 0, :], hinge[:, 2, 0:1], b2[:, 0:1],
                                                    ALU.mult, ALU.add).then_inc(hinged, 1)
                        else:
                            nc.vector.scalar_tensor_tensor(out=g_sb[:, :], in0=relu[:, i % 4, :],
                                                           scalar=hinge[:, 2, i:i + 1], in1=g_sb[:, :],
                                                           op0=ALU.mult, op1=ALU.add).then_inc(hinged, 1)

                for t in range(R):
                    two, one = active(j, "x2T", t), has(j, 1) and t < 2
                    part = slice(2 * t, 2 * t + 2)
                    over2 = TURNS_OVER["x2T"](j, t)
                    pp, tt = tile_at(t, 3, p)

                    def tops(g):
                        if not has(j):
                            return
                        wait(dve, scored, 16 * j + 4 * t + g + 1)
                        if g == 0:
                            wait(dve, exped, 16 * j + 4 * t)
                        nc.vector.tensor_reduce(ntop[:, 4 * g:4 * g + 4], sc[g][:, :].rearrange("p (h c) -> p h c", c=C),
                                                AX.X, ALU.max, negate=True).then_inc(topped, 1)

                    tops(0)
                    if two:
                        wait(dve, taken["wo"], over2)
                        nc.vector.bn_stats(stats2[:, :], x2[pp][:, tt, :]).then_inc(bn2_done, 1)
                        wait(dve, bn2_done, over2)
                        wait(dve, xn2_done, over2 - 1)
                    tops(1)
                    if two:
                        nc.vector.bn_aggr(mv2[:, :], stats2[:, :]).then_inc(mv2_done, 1)
                        wait(dve, mv2_done, over2)
                        nc.vector.tensor_scalar(vare2[:, :], mv2[:, 1:2], EPS, None, ALU.add).then_inc(var2_done, 1)
                    tops(2)
                    tops(3)
                    if active(j, "out", t):
                        wait(dve, psum["out"], TURNS_OVER["out"](j, t))
                        if t == 0:
                            wait(dve, bf_added, 4 * (j - 1))
                        nc.vector.tensor_tensor(x2[p][:, t, :], ring[bank_of(p, ("out", t))][:, :], x2[p][:, t, :],
                                                ALU.add).then_inc(taken["out"], 1)
                    if active(j, "pv", t):
                        over = TURNS_OVER["pv"](j, t)
                        wait(dve, exped, 4 * over)
                        wait(dve, taken["pv"], over - 1)
                        nc.vector.reciprocal(rtotal[:, :], total[:, (t - 1) % 2, :]).then_inc(summed, 1)
                        wait(dve, summed, over)
                        wait(dve, psum["pv"], over)
                        wait(dve, psum["aT"], over - 1)
                        nc.vector.tensor_tensor(attn[:, :].rearrange("p (h d) -> p h d", d=DH),
                                                ring[bank_of(p, ("pv", t))][:, :].rearrange("p (h d) -> p h d", d=DH),
                                                bcast(rtotal[:, :], DH), ALU.mult).then_inc(taken["pv"], 1)
                    if one:
                        wait(dve, x1_in, 16 * (j + 2))
                        for i in (2 * t, 2 * t + 1):
                            last = nc.vector.bn_stats(stats[:, i, :], x1[:, i, :])
                        last.then_inc(bn_done, 1)
                        wait(dve, bn_done, 2 * (j + 1) + t + 1)
                        wait(dve, xn_done, R * (j + 1))
                    if t in (1, 2) and has(j, 1):
                        for i in (2 * t - 2, 2 * t - 1):
                            tok = slice(i * P, (i + 1) * P)
                            take_lo(j, p, "xT", i, xT[1][:, :, tok], xT[0][:, :, tok].bitcast(F32))
                    if active(j, "wo", t):
                        over = TURNS_OVER["wo"](j, t)
                        pw, tw = tile_at(t, 2, p)
                        wait(dve, psum["wo"], over)
                        wait(dve, res_done, over)
                        if isinstance(j, int):
                            wait(dve, stored[pw][tw], 16 * ((j - (t < 2)) // 2))
                        else:
                            wait(dve, stored[pw][tw], 8 * (j - (t < 2) - pw))
                        nc.vector.tensor_tensor(x2[pw][:, tw, :], ring[bank_of(p, ("wo", t))][:, :], xr[pw][:, tw, :],
                                                ALU.add).then_inc(taken["wo"], 1)
                    if one:
                        for i in (2 * t, 2 * t + 1):
                            last = nc.vector.bn_aggr(mv[:, i, :], stats[:, i, :])
                        last.then_inc(mv_done, 1)
                        wait(dve, mv_done, 2 * (j + 1) + t + 1)
                        nc.vector.tensor_scalar(vare[:, part], mv[:, part, 1], EPS, None,
                                                ALU.add).then_inc(var_done, 1)
                    if t == 3 and active(j, "s", 0):
                        wait(dve, relu_done, PAIRS * (j - 1))
                        for i in range(2):
                            wait(dve, psum["s"], TURNS_OVER["s"](j, i))
                            nc.vector.tensor_scalar(s_sb[:, 2 * P * i:2 * P * (i + 1)],
                                                    ring[bank_of(p, ("s", i))][:, 0:2 * P], bin_[:, 0:1], None,
                                                    ALU.add).then_inc(taken["s"], 1)
                    if two:
                        tok = slice((t + 1) % 4 * P, ((t + 1) % 4 + 1) * P)
                        take_lo(j, p, "x2T", t, x2T[1][:, :, tok], x2T[0][:, :, tok].bitcast(F32))
                    if active(j, "aT", t):
                        take_lo(j, p, "aT", t, aT[1][:, :, :], aT[0][:, :, :].bitcast(F32))
                    if t == 3:
                        if is_step(j, -1):
                            dve.wait_ge(in_small, 16 * len(small))
                            dve.wait_ge(consts, 1)
                        for m in range(DK):
                            hinges(*HINGE_RUNS[m])
                            if has(j, 1):
                                wait(dve, hi["q"], TURNS_OVER["q"](j, m))
                                nc.vector.scalar_tensor_tensor(out=q[1][:, m, :], in0=ring[bank_of(p, ("q", m))][:, :],
                                                               scalar=bq[:, m:m + 1], in1=q[0][:, m, :].bitcast(F32),
                                                               op0=ALU.add, op1=ALU.subtract).then_inc(taken["q"], 1)
                    if has(j):
                        for g in range(4):
                            heads = slice(4 * g, 4 * g + 4)
                            take_lo(j, p, "pT", 4 * t + g, pT[1][:, heads, :], pT[0][:, heads, :])
                    if t == 3 and active(j, "s", 0):
                        wait(dve, g_hi, j)
                        nc.vector.tensor_tensor(gT[1][:, :], g_sb[:, :], gT[0][:, :].bitcast(F32),
                                                ALU.subtract).then_inc(g_lo, 1)

            nc.vector.memset(b2[M:2 * M, :], 0.0).then_inc(consts, 1)
            run_steps(dve, step, TILES + 1)


def build_program(nc, x, ctx, mask, w, b, out, debug_x1=None):
    x1_dram = debug_x1 if debug_x1 is not None else nc.dram_tensor("x1_scratch", [R, S, D], F32).ap()
    scratch = {"k": nc.dram_tensor("k_scratch", [R, P, 2, DK, C], F32).ap(),
               "v": nc.dram_tensor("v_scratch", [R, C, 2, D], F16).ap(),
               "mask": nc.dram_tensor("mask_scratch", [R, P, C], F32).ap()}
    with ExitStack() as stack:
        def sb(name, shape, dt=F32):
            return stack.enter_context(nc.sbuf_tensor(name, shape, dt))

        keep = {"ident": sb("ident", [P, P]), "vscale": sb("vscale", [P, DK])}
        keep["x_tile"] = sb("x_tile0", [P, R, D])
        keep["x_in"] = stack.enter_context(nc.semaphore("x_in0"))
        keep["x1_in"] = stack.enter_context(nc.semaphore("x1_in"))
        keep["wqkv"] = [sb(f"wqkv{h}", [P, DK, 3 * D], F32R) for h in range(2)]
        for name, first, width in (("wq", 0, D), ("wo", D, D), ("win", 2 * D, 2 * M), ("wf", 2 * D + 2 * M, P)):
            keep[name] = [part[:, :, first:first + width] for part in keep["wqkv"]]
        with ExitStack() as stack1:
            def sb1(name, shape, dt=F32):
                return stack1.enter_context(nc.sbuf_tensor(name, shape, dt))

            keep["wout"] = [sb1(f"wout{h}", [P, DK, D], F32R) for h in range(2)]
            keep["bqkv"] = sb1("bqkv", [P, 3 * D])
            keep["bout"] = sb1("bout", [P, D])
            prepare_block(nc, x, ctx, mask, w, b, scratch, keep)
            self_block(nc, x, x1_dram, w, keep)
        if debug_x1 is None:
            cross_block(nc, x1_dram, scratch, w, b, out, keep)


def kernel(**inputs):
    import concourse.bacc as bacc
    from concourse.bass_utils import run_bass_kernel_spmd

    nc = bacc.Bacc("TRN2", target_bir_lowering=False, num_devices=1)
    arrays = {}

    def dram(name, array):
        arrays[name] = np.ascontiguousarray(array)
        return nc.dram_tensor(name, arrays[name].shape, mybir.dt.from_np(arrays[name].dtype),
                              kind="ExternalInput").ap()

    given = {name: np.asarray(a) for name, a in inputs.items()}
    w = {name: dram(f"in_{name}", given[key].T) for name, key in (
        ("wqkv", "L0_attn_qkv_w"), ("wout", "L0_attn_out_w"), ("wq", "L0_xattn_Wq"), ("wk", "L0_xattn_Wk"),
        ("wv", "L0_xattn_Wv"), ("wo", "L0_xattn_Wo"))}
    w["win"] = dram("in_win", given["L0_ffn_Win"])
    w["wf"] = dram("in_wf", given["L0_ffn_Wout"])
    b = {name: dram(f"in_{name}", given[key]) for name, key in (
        ("bqkv", "L0_attn_qkv_b"), ("bout", "L0_attn_out_b"), ("bo", "L0_xattn_bo"), ("bf", "L0_ffn_bout"))}
    for name, key in (("bk", "L0_xattn_bk"), ("bv", "L0_xattn_bv"), ("bq", "L0_xattn_bq")):
        b[name] = dram(f"in_{name}", given[key].reshape(DK, P).T)
    for name, key in (("bin", "L0_ffn_bin_"), ("b2", "L0_ffn_b2")):
        b[name] = dram(f"in_{name}", given[key].reshape(M, 1))
    for name, key in (("w1", "L0_ffn_W1"), ("b1", "L0_ffn_b1"), ("w2", "L0_ffn_W2")):
        b[name] = dram(f"in_{name}", given[key].reshape(M, PAIRS, 2).transpose(2, 0, 1))
    x = dram("in_x", given["x"])
    ctx = dram("in_ctx", given["ctx_1024"])
    mask = dram("in_mask", given["mask_BxS2_bf1"].view(np.uint8))
    out = nc.dram_tensor("out", (R, S, D), F32, kind="ExternalOutput").ap()
    build_program(nc, x, ctx, mask, w, b, out)
    return run_bass_kernel_spmd(nc, [arrays], core_ids=[0]).results[0]["out"]
```
